# Optimizing a Trainium2 kernel written in Bass

```python
import numpy as np
import jax
import jax.numpy as jnp

def _softmax(x, axis=-1):
    return jax.nn.softmax(x, axis=axis)

def _gelu(x):
    return jax.nn.gelu(x, approximate=True)

def _silu(x):
    return jax.nn.silu(x)

def _sigmoid(x):
    return jax.nn.sigmoid(x)

def _layernorm(x, axis=-1, eps=1e-05):
    m = jnp.mean(x, axis=axis, keepdims=True)
    v = jnp.var(x, axis=axis, keepdims=True)
    return (x - m) / jnp.sqrt(v + eps)

def _scatter_add(tgt, idx, src, axis=0):
    return tgt.at[idx].add(src)

def _segment_sum(src, seg, n):
    return jax.ops.segment_sum(src, seg, n)
kernel_name = 'mk_flamingo_gated_d2_seqx_r4_9aa6df'

def setup_inputs(seed: int=0):
    np.random.seed(seed)
    _w = jnp.asarray

    def _rec_inputs():
        import jax
        import jax.numpy as jnp
        _rk = jax.random.key(seed)
        x = 7.22e-05 + 1 * jax.random.normal(jax.random.fold_in(_rk, 1), (8, 256, 512), jnp.float32)
        _lenS = 256 - jax.random.randint(jax.random.fold_in(_rk, 7), (8,), 0, max(1, 256 // 4) + 1, jnp.int32)
        _lenS2 = 256 - jax.random.randint(jax.random.fold_in(_rk, 8), (8,), 0, max(1, 256 // 4) + 1, jnp.int32)
        _ctx_512P = jax.random.normal(jax.random.fold_in(_rk, 11), (8, 16, 128), jnp.float32)
        _ctx_512c = jax.random.dirichlet(jax.random.fold_in(_rk, 511), 0.3 * jnp.ones((16,), jnp.float32), (8, 256))
        _ctx_512t = jnp.einsum('bsk,bkd->bsd', _ctx_512c, _ctx_512P)
        _ctx_512t = _ctx_512t * jax.lax.rsqrt(jnp.mean(jnp.square(_ctx_512t)) + 1e-12) * 0.953939
        ctx_512 = -0.000514642 + 1.00011 * (_ctx_512t + 0.3 * jax.random.normal(jax.random.fold_in(_rk, 611), (8, 256, 128), jnp.float32))
        _g = jax.random.normal(jax.random.fold_in(_rk, 9001), (2, 2), jnp.float32)
        _g = jnp.sign(_g) * jnp.maximum(jnp.abs(_g), 1.0) + (_g == 0) * 1.0
        g_xattn = _g[0]
        g_ffn = _g[1]
        return (x, ctx_512, g_xattn, g_ffn)
    x, ctx_512, g_xattn, g_ffn = _rec_inputs()

    def _L0_xattn_setup():
        import jax, jax.numpy as jnp
        import numpy as np
        B, S, E = (2, 512, 512)
        QH, KVH = (32, 8)
        D = E // QH
        G = QH // KVH
        DROPOUT = 1.0
        key = jax.random.key(seed)
        k1, k2, k3 = jax.random.split(key, 3)
        q = jax.random.normal(k1, (B, S, E), dtype=jnp.float32)
        k = jax.random.normal(k2, (B, S, E // G), dtype=jnp.float32)
        v = jax.random.normal(k3, (B, S, E // G), dtype=jnp.float32)
        return {'q': q, 'k': k, 'v': v}
    _L0_xattn_all = _L0_xattn_setup()
    _L0_xattn_in = {k: v for k, v in _L0_xattn_all.items() if k in ()}
    del _L0_xattn_all

    def _L0_ffn_setup():
        import jax, jax.numpy as jnp
        import numpy as np
        B, S, H, E, D, K = (2, 512, 512, 8, 512, 2)
        key = jax.random.key(seed)
        ks = jax.random.split(key, 4)
        return {'x': jax.random.normal(ks[0], (B, S, H), jnp.float32), 'router_w': jax.random.normal(ks[1], (H, E), jnp.float32) / np.sqrt(H).astype(np.float32), 'router_b': jnp.zeros((E,), jnp.float32), 'expert_w': jax.random.normal(ks[2], (E, H, D), jnp.float32) / np.sqrt(H).astype(np.float32), 'expert_b': jnp.zeros((E, D), jnp.float32), 'out_w': jax.random.normal(ks[3], (D, D), jnp.float32) / np.sqrt(D).astype(np.float32), 'out_b': jnp.zeros((D,), jnp.float32)}
    _L0_ffn_all = _L0_ffn_setup()
    _L0_ffn_in = {k: v for k, v in _L0_ffn_all.items() if k in ('router_w', 'router_b', 'expert_w', 'expert_b', 'out_w', 'out_b')}
    del _L0_ffn_all

    def _L1_xattn_setup():
        import jax, jax.numpy as jnp
        import numpy as np
        B, S, H, NH, L = (2, 512, 512, 16, 128)
        HD = H // NH
        key = jax.random.key(seed)
        k1, k2, k3, k4, k5 = jax.random.split(key, 5)
        scale = 0.02
        return {'q': jax.random.normal(k1, (B, S, H), dtype=jnp.float32), 'latent_kv': jax.random.normal(k2, (B, S, L), dtype=jnp.float32), 'Wq': jax.random.normal(k3, (H, H), dtype=jnp.float32) * scale, 'Wkv_expand': jax.random.normal(k4, (2 * H, L), dtype=jnp.float32) * scale, 'Wout': jax.random.normal(k5, (H, H), dtype=jnp.float32) * scale}
    _L1_xattn_all = _L1_xattn_setup()
    _L1_xattn_in = {k: v for k, v in _L1_xattn_all.items() if k in ('Wq', 'Wkv_expand', 'Wout')}
    del _L1_xattn_all

    def _L1_ffn_setup():
        import jax, jax.numpy as jnp
        import numpy as np
        HIDDEN = 512
        INTER = 2048
        BATCH, LOCAL_SEQ = (2, 1024)
        key = jax.random.key(seed)
        k1, k2, k3 = jax.random.split(key, 3)
        h_shard = jax.random.normal(k1, (BATCH, LOCAL_SEQ, HIDDEN), dtype=jnp.float32)
        w_gate_up = jax.random.normal(k2, (2 * INTER, HIDDEN), dtype=jnp.float32) * 0.02
        w_down = jax.random.normal(k3, (HIDDEN, INTER), dtype=jnp.float32) * 0.02
        return {'h_shard': h_shard, 'w_gate_up': w_gate_up, 'w_down': w_down}
    _L1_ffn_all = _L1_ffn_setup()
    _L1_ffn_in = {k: v for k, v in _L1_ffn_all.items() if k in ('w_gate_up', 'w_down')}
    del _L1_ffn_all
    return {'x': x, 'ctx_512': ctx_512, 'g_xattn': g_xattn, 'g_ffn': g_ffn, 'L0_ffn_router_w': _L0_ffn_in['router_w'], 'L0_ffn_router_b': _L0_ffn_in['router_b'], 'L0_ffn_expert_w': _L0_ffn_in['expert_w'], 'L0_ffn_expert_b': _L0_ffn_in['expert_b'], 'L0_ffn_out_w': _L0_ffn_in['out_w'], 'L0_ffn_out_b': _L0_ffn_in['out_b'], 'L1_xattn_Wq': _L1_xattn_in['Wq'], 'L1_xattn_Wkv_expand': _L1_xattn_in['Wkv_expand'], 'L1_xattn_Wout': _L1_xattn_in['Wout'], 'L1_ffn_w_gate_up': _L1_ffn_in['w_gate_up'], 'L1_ffn_w_down': _L1_ffn_in['w_down']}

def reference(x, ctx_512, g_xattn, g_ffn, L0_ffn_router_w, L0_ffn_router_b, L0_ffn_expert_w, L0_ffn_expert_b, L0_ffn_out_w, L0_ffn_out_b, L1_xattn_Wq, L1_xattn_Wkv_expand, L1_xattn_Wout, L1_ffn_w_gate_up, L1_ffn_w_down):
    import jax
    import jax.numpy as jnp

    def _L0_xattn_ref(q, k, v):
        import jax, jax.numpy as jnp
        import numpy as np
        B, S, E = (2, 512, 512)
        QH, KVH = (32, 8)
        D = E // QH
        G = QH // KVH
        DROPOUT = 1.0
        b, s, _ = q.shape
        qh = q.reshape(b, s, KVH, G, D).transpose(0, 2, 3, 1, 4)
        kh = k.reshape(b, s, KVH, D).transpose(0, 2, 1, 3)
        vh = v.reshape(b, s, KVH, D).transpose(0, 2, 1, 3)
        scale = 1.0 / jnp.sqrt(jnp.float32(D))
        scores = jnp.einsum('bkgsd,bktd->bkgst', qh, kh) * scale
        attn = jax.nn.softmax(scores, axis=-1) / DROPOUT
        out = jnp.einsum('bkgst,bktd->bkgsd', attn, vh)
        return out.transpose(0, 3, 1, 2, 4).reshape(b, s, E)

    def _L0_ffn_ref(x, router_w, router_b, expert_w, expert_b, out_w, out_b):
        import jax, jax.numpy as jnp
        import numpy as np
        B, S, H, E, D, K = (2, 512, 512, 8, 512, 2)
        num_experts = expert_w.shape[0]
        router_logits = jnp.einsum('bsh,he->bse', x, router_w) + router_b
        router_probs = jax.nn.softmax(router_logits, axis=-1)
        top_k_probs, top_k_indices = jax.lax.top_k(router_probs, K)
        top_k_probs = top_k_probs / jnp.sum(top_k_probs, axis=-1, keepdims=True)
        onehot = jax.nn.one_hot(top_k_indices, num_experts, dtype=x.dtype)
        gates = jnp.einsum('bsk,bske->bse', top_k_probs, onehot)
        expert_out = jax.nn.gelu(jnp.einsum('bsh,ehd->ebsd', x, expert_w) + expert_b[:, None, None, :])
        combined = jnp.einsum('bse,ebsd->bsd', gates, expert_out)
        return jnp.einsum('bsd,df->bsf', combined, out_w) + out_b

    def _L1_xattn_ref(q, latent_kv, Wq, Wkv_expand, Wout):
        import jax, jax.numpy as jnp
        import numpy as np
        B, S, H, NH, L = (2, 512, 512, 16, 128)
        HD = H // NH
        b, sq, _ = q.shape
        sk = latent_kv.shape[1]
        qp = q @ Wq.T
        kv = latent_kv @ Wkv_expand.T
        k, v = jnp.split(kv, 2, axis=-1)
        qh = qp.reshape(b, sq, NH, HD).transpose(0, 2, 1, 3)
        kh = k.reshape(b, sk, NH, HD).transpose(0, 2, 1, 3)
        vh = v.reshape(b, sk, NH, HD).transpose(0, 2, 1, 3)
        inv_sqrt_d = 1.0 / jnp.sqrt(jnp.float32(HD))
        scores = jnp.einsum('bhqd,bhkd->bhqk', qh, kh) * inv_sqrt_d
        causal = jnp.tril(jnp.ones((sq, sk), dtype=bool))
        scores = jnp.where(causal, scores, jnp.finfo(scores.dtype).min)
        attn = jax.nn.softmax(scores, axis=-1)
        out = jnp.einsum('bhqk,bhkd->bhqd', attn, vh)
        out = out.transpose(0, 2, 1, 3).reshape(b, sq, H)
        return out @ Wout.T

    def _L1_ffn_ref(h_shard, w_gate_up, w_down):
        import jax, jax.numpy as jnp
        import numpy as np
        HIDDEN = 512
        INTER = 2048
        BATCH, LOCAL_SEQ = (2, 1024)
        batch, local_seq, hidden = h_shard.shape
        gate_up = jnp.einsum('bsh,oh->bso', h_shard, w_gate_up)
        gate, up = jnp.split(gate_up, 2, axis=-1)
        h = jax.nn.silu(gate) * up
        out = jnp.einsum('bsi,hi->bsh', h, w_down)
        return out
    x = x + jnp.tanh(g_xattn[0]) * _L0_xattn_ref(_layernorm(x, axis=-1), ctx_512, ctx_512)
    x = x + jnp.tanh(g_ffn[0]) * _L0_ffn_ref(_layernorm(x, axis=-1), L0_ffn_router_w, L0_ffn_router_b, L0_ffn_expert_w, L0_ffn_expert_b, L0_ffn_out_w, L0_ffn_out_b)
    x = x + jnp.tanh(g_xattn[1]) * _L1_xattn_ref(_layernorm(x, axis=-1), ctx_512, L1_xattn_Wq, L1_xattn_Wkv_expand, L1_xattn_Wout)
    x = x + jnp.tanh(g_ffn[1]) * _L1_ffn_ref(_layernorm(x, axis=-1), L1_ffn_w_gate_up, L1_ffn_w_down)
    return x

_drawn_inputs = setup_inputs


def setup_inputs(seed=0):
    import zlib

    import numpy as np

    out = dict(_drawn_inputs(seed))
    spreads = {'g_ffn': (-1.0, 0.6),
     'L0_ffn_router_b': (0.0, 0.1),
     'L0_ffn_expert_b': (0.0, 0.268),
     'L0_ffn_out_b': (0.0, 0.1)}
    factors = {'L1_xattn_Wq': 33.611}
    for name, (base, spread) in spreads.items():
        noise = np.random.default_rng([zlib.crc32(name.encode()), seed]).standard_normal(out[name].shape)
        drawn = base * np.exp(spread * noise) if base else spread * noise
        out[name] = jnp.asarray(drawn.astype(out[name].dtype))
    for name, factor in factors.items():
        out[name] = (out[name] * factor).astype(out[name].dtype)
    return out
```

```python
from contextlib import ExitStack

import concourse.bass as bass
from concourse import mybir

P = 128
F32 = mybir.dt.float32
F16 = mybir.dt.float16
ALU = mybir.AluOpType
ACT = mybir.ActivationFunctionType
AX = mybir.AxisListType

B, S, E, L = 8, 256, 512, 128
TILES = B * S // P
ST = S // P
KC = E // P
EPS = 1e-5

X_SCALE = 512.0
W_SCALE = 256.0
M_SCALE = 4096.0
LIFT0 = 887.0

H0, KV0, D0 = 32, 8, 16
G0 = H0 // KV0
R0 = 64
V0 = 2 * D0 + 1
PAIRS = 2
X_LOAD = 7


class Norm:

    STEPS = 6

    def __init__(self, nc, mem, tag, t):
        def sb(name, shape, dt):
            return mem.enter_context(nc.sbuf_tensor(f"{tag}_{name}", shape, dt))

        def sem(name):
            return mem.enter_context(nc.semaphore(f"{tag}_{name}"))

        self.x, self.consts = t["x"], t["norm_consts"]
        self.bn = sb("bn", [P, ST, 6], F32)
        self.tmp = sb("norm_tmp", [P, 4, ST], F32)
        self.mean = sb("mean", [P, ST], F32)
        self.rstd = sb("rstd", [P, ST], F32)
        self.xn = sb("xn", [P, ST, E], F32)
        self.bn_ok, self.chain, self.xn_ok = sem("bn_ok"), sem("norm_chain"), sem("xn_ok")

    def const(self, k):
        return self.consts[:, k:k + 1].to_broadcast([P, ST])

    def statistics(self, dve, tile, n):
        for st in range(ST):
            ins = dve.bn_stats(self.bn[:, st, :], self.x[:, tile + st, :])
        ins.then_inc(self.bn_ok, 1)

    def deviation(self, pool, n):
        bn, tmp, chain, at = self.bn, self.tmp, self.chain, self.STEPS * n
        pool.wait_ge(self.bn_ok, n + 1)
        pool.tensor_tensor(self.mean[:, :], bn[:, :, 1], bn[:, :, 4], ALU.add)
        pool.tensor_tensor(tmp[:, 0], bn[:, :, 1], bn[:, :, 4], ALU.subtract)
        pool.tensor_tensor(tmp[:, 1], bn[:, :, 2], bn[:, :, 5], ALU.add).then_inc(chain, 1)
        pool.wait_ge(chain, at + 1)
        pool.tensor_tensor(self.mean[:, :], self.mean[:, :], self.const(0), ALU.mult)
        pool.tensor_tensor(tmp[:, 2], tmp[:, 0], tmp[:, 0], ALU.mult)
        pool.tensor_tensor(tmp[:, 1], tmp[:, 1], self.const(1), ALU.mult).then_inc(chain, 1)
        pool.wait_ge(chain, at + 2)
        pool.tensor_tensor(tmp[:, 3], tmp[:, 1], tmp[:, 2], ALU.add).then_inc(chain, 1)
        pool.wait_ge(chain, at + 3)
        pool.tensor_tensor(tmp[:, 0], tmp[:, 3], self.const(2), ALU.add).then_inc(chain, 1)
        pool.wait_ge(chain, at + 4)
        pool.tensor_tensor(tmp[:, 1], tmp[:, 0], self.const(3), ALU.pow).then_inc(chain, 1)
        pool.wait_ge(chain, at + 5)
        pool.tensor_tensor(self.rstd[:, :], tmp[:, 1], self.const(4), ALU.mult).then_inc(chain, 1)

    def normalise(self, dve, tile, n):
        dve.wait_ge(self.chain, self.STEPS * (n + 1))
        for st in range(ST):
            ins = dve.tensor_scalar(self.xn[:, st, :], self.x[:, tile + st, :], self.mean[:, st:st + 1],
                                    self.rstd[:, st:st + 1], ALU.subtract, ALU.mult)
        ins.then_inc(self.xn_ok, 1)


class Split:

    def __init__(self, nc, mem, tag, slots):
        def sem(name):
            return mem.enter_context(nc.semaphore(f"{tag}_{name}"))

        self.rows = mem.enter_context(nc.sbuf_tensor(f"{tag}_rows", [P, 2, ST, E], F16))
        self.cols = mem.enter_context(nc.sbuf_tensor(f"{tag}_cols", [P, slots, 2, KC, S], F16))
        self.hi_ok, self.lo_ok = sem("hi_ok"), sem("lo_ok")
        self.turned, self.cols_ok = sem("turned"), sem("cols_ok")

    def high(self, act, src):
        act.activation(self.rows[:, 0], src, ACT.Copy).then_inc(self.hi_ok, 1)

    def low(self, dve, src, n):
        dve.wait_ge(self.hi_ok, n + 1)
        dve.tensor_tensor(self.rows[:, 1], src, self.rows[:, 0], ALU.subtract).then_inc(self.lo_ok, 1)

    def turn(self, pe, half, psum, ident):
        for k in range(KC):
            for st in range(ST):
                ins = pe.transpose(psum[:, k, st * P:(st + 1) * P], self.rows[:, half, st, k * P:(k + 1) * P],
                                   ident[:, :])
        ins.then_inc(self.turned, 1)

    def out(self, act, half, psum, par, n):
        act.wait_ge(self.turned, 2 * n + half + 1)
        act.activation(self.cols[:, par, half], psum, ACT.Copy).then_inc(self.cols_ok, 1)


PRODUCTS = ((0, 0), (1, 0), (0, 1))


def project(pe, psum, cols, par, st, weights, k_chunks=KC, more=False):
    last = len(PRODUCTS) * k_chunks - 1
    i = 0
    for k in range(k_chunks):
        for a, b in PRODUCTS:
            ins = pe.matmul(psum, cols[:, par, a, k, st * P:(st + 1) * P], weights[:, b, k, :],
                            start=(i == 0), stop=(i == last and not more))
            i += 1
    return ins


NORM_CONSTS = (0.5, 4.0 / E, 4.0 * EPS, -0.5, 2.0 * X_SCALE)


def phase_attention0(nc, mem, t):
    x, w_e, stage, ident, gates = t["x"], t["w_e"], t["stage"], t["ident"], t["tanh_g"]
    ctx_d, x_d, expert_d = t["ctx_d"], t["x_d"], t["expert_d"]
    GPB = KV0
    NG = PAIRS * GPB
    TRIPS = B // PAIRS

    def sb(name, shape, dt):
        return mem.enter_context(nc.sbuf_tensor("a0_" + name, shape, dt))

    def sem(name):
        return mem.enter_context(nc.semaphore("a0_" + name))

    wscale = sb("wscale", [P, 1], F32)
    ctx = sb("ctx", [P, PAIRS, ST, L], F32)
    norm = Norm(nc, mem, "a0", t)
    xn = norm.xn
    qst = sb("qst", [P, PAIRS, ST, H0, R0], F16)
    kst = sb("kst", [P, ST, KV0, 2 * R0], F16)
    kT = sb("kT", [P, PAIRS, KV0, S], F16)
    vst = sb("vst", [P, PAIRS, ST, KV0, V0], F16)
    qT1 = sb("qT1", [P, 2, 2, S], F16)
    qT2 = sb("qT2", [P, 2, 2, S], F16)
    p32 = sb("p32", [P, ST, 2, 2, S], F32)
    p_hi = sb("p_hi", [P, 4, 2, 2, S], F16)
    p_lo = sb("p_lo", [P, 4, 2, 2, S], F16)
    negm = sb("negm", [P, 2, ST, 2, 2], F32)
    oall = sb("oall", [P, PAIRS, ST, H0, V0], F32)
    rec = sb("rec", [P, ST, H0], F32)
    inc = sb("inc", [P, ST, H0, D0], F32)
    v256 = sb("v256", [P, ST * KV0, D0], F32)

    pS2 = mem.enter_context(nc.psum_tensor("a0_pS2", [P, 2, 2, 2, S], F32))
    pS1 = mem.enter_context(nc.psum_tensor("a0_pS1", [P, 2, 2, S], F32))
    pT = mem.enter_context(nc.psum_tensor("a0_pT", [P, 4, S], F16))
    pO = mem.enter_context(nc.psum_tensor("a0_pO", [P, 512], F32))
    o_ps = pO[:, 0:ST * G0 * V0].rearrange("p (s h d) -> p s h d", s=ST, h=G0)

    x0_in, x_in = sem("x0_in"), sem("x_in")
    ctx_in = [sem(f"ctx{par}_in") for par in range(PAIRS)]
    stage_in = [sem(f"stage{par}_in") for par in range(PAIRS)]
    const_set, qzero = sem("const_set"), sem("qzero")
    v_ok = sem("v_ok")
    qhi_ok, qlo_ok, khi_ok, klo_ok = sem("qhi_ok"), sem("qlo_ok"), sem("khi_ok"), sem("klo_ok")
    t1_done, t2_done, tk_done = sem("t1_done"), sem("t2_done"), sem("tk_done")
    qT1_ok, qT2_ok, kT_ok = sem("qT1_ok"), sem("qT2_ok"), sem("kT_ok")
    s1_done, max_ok, mhi_ok, m_ok = sem("s1_done"), sem("max_ok"), sem("mhi_ok"), sem("m_ok")
    s2_done, exp_done = sem("s2_done"), sem("exp_done")
    plo_ok = [sem(f"plo{c}_ok") for c in range(ST)]
    v256_ok, vhi_ok, osum_ok = sem("v256_ok"), sem("vhi_ok"), sem("osum_ok")
    pv_done, o_ok = sem("pv_done"), sem("o_ok")
    rec0_ok, rec_ok, inc_ok, x_ok = sem("rec0_ok"), sem("rec_ok"), sem("inc_ok"), sem("x_ok")
    whi_ok, wscaled, wlo_ok = sem("whi_ok"), sem("wscaled"), sem("wlo_ok")
    PRIME_EXP, PRIME_PV, PRIME_O, PRIME_INC, PRIME_W, PRIME_LO = 2, 2, 1, 1, 2, 1

    with nc.Block() as block:

        @block.sync
        def _(sp):
            def load_ctx(b, par):
                sp.dma_start(ctx[:, par], ctx_d[:, b]).then_inc(ctx_in[par], 16)

            load_ctx(0, 0)
            sp.dma_start(x[:, 0:ST, :], x_d[:, 0:ST, :]).then_inc(x0_in, 16)
            load_ctx(1, 1)
            for n in range(ST, TILES, X_LOAD):
                sp.dma_start(x[:, n:n + X_LOAD, :], x_d[:, n:n + X_LOAD, :]).then_inc(x_in, 16)
            with sp.Fori(0, TRIPS) as it:
                for par in range(PAIRS):
                    sp.wait_ge(wlo_ok, it * PAIRS + par + 1)
                    sp.dma_start(stage[:, par], expert_d[:, it * PAIRS + par]).then_inc(stage_in[par], 16)
                for par in range(PAIRS):
                    sp.wait_ge(klo_ok, it * PAIRS + par + 1)
                    sp.wait_ge(v_ok, it * PAIRS + par + 1)
                    load_ctx((it * PAIRS + PAIRS + par) % B, par)
            for par in range(PAIRS):
                sp.wait_ge(ctx_in[par], 16 * (TRIPS + 1))

        @block.gpsimd
        def _(pool):
            def values(par, n, loads):
                pool.wait_ge(ctx_in[par], 16 * loads)
                pool.wait_ge(pv_done, (n - 1) * GPB + PRIME_PV)
                pool.wait_ge(const_set, 5)
                v_high_low(par, n)

            def v_high_low(par, n):
                src = ctx[:, par].rearrange("p c (g d) -> p (c g) d", d=D0)
                dst = vst[:, par].rearrange("p c g d -> p (c g) d")
                scale = wscale[:, :].unsqueeze(2).to_broadcast([P, ST * KV0, D0])
                pool.tensor_tensor(v256[:, :, :], src, scale, ALU.mult).then_inc(v256_ok, 1)
                pool.tensor_tensor(dst[:, :, 0:D0], src, scale, ALU.mult).then_inc(vhi_ok, 1)
                pool.wait_ge(v256_ok, n + 1)
                pool.wait_ge(vhi_ok, n + 1)
                pool.tensor_tensor(dst[:, :, D0 + 1:], v256[:, :, :], dst[:, :, 0:D0],
                                   ALU.subtract).then_inc(v_ok, 1)

            def p_low(slot, n):
                pool.wait_ge(exp_done, n * 2 + 2 + PRIME_EXP)
                pool.tensor_tensor(p_lo[:, 2 * slot + 1], p32[:, 1], p_hi[:, 2 * slot + 1],
                                   ALU.subtract).then_inc(plo_ok[1], 1)

            def finish(par, tile, n):
                pool.wait_ge(o_ok, (n + 1) * GPB + PRIME_O)
                pool.tensor_tensor(inc[:, :, :, :], oall[:, par, :, :, 0:D0], oall[:, par, :, :, D0 + 1:],
                                   ALU.add).then_inc(osum_ok, 1)
                pool.wait_ge(osum_ok, n + 1)
                pool.wait_ge(rec_ok, n + 1)
                pool.tensor_tensor(inc[:, :, :, :], inc[:, :, :, :],
                                   rec[:, :, :].unsqueeze(3).to_broadcast([P, ST, H0, D0]),
                                   ALU.mult).then_inc(inc_ok, 1)
                pool.wait_ge(inc_ok, n + 1 + PRIME_INC)
                pool.wait_ge(const_set, 5)
                xb = x[:, bass.ds(tile, ST), :]
                pool.tensor_tensor(xb, xb, inc[:, :, :, :].rearrange("p s h d -> p s (h d)"),
                                   ALU.add).then_inc(x_ok, 1)

            def split_low(par, e, n):
                pool.wait_ge(whi_ok, n + 1)
                sg = stage[:, par].rearrange("p k n -> p (k n)")
                pool.tensor_tensor(sg, sg, wscale[:, :].to_broadcast([P, KC * E]), ALU.mult).then_inc(wscaled, 1)
                pool.wait_ge(wscaled, n + 1)
                lo = w_e[:, e, 1].rearrange("p k n -> p (k n)")
                hi = w_e[:, e, 0].rearrange("p k n -> p (k n)")
                pool.tensor_tensor(lo, sg, hi, ALU.subtract).then_inc(wlo_ok, 1)

            pool.sem_inc(wlo_ok, PRIME_W)
            pool.sem_inc(inc_ok, PRIME_INC)
            pool.sem_inc(plo_ok[1], PRIME_LO)
            for k, value in enumerate(NORM_CONSTS):
                ins = pool.memset(norm.consts[:, k:k + 1], value)
            ins.then_inc(const_set, 1)
            pool.memset(wscale[:, :], W_SCALE).then_inc(const_set, 1)
            pool.memset(vst[:, :, :, :, D0:D0 + 1], 1.0).then_inc(const_set, 1)
            pool.memset(qst[:, :, :, :, :], 0.0).then_inc(qzero, 1)
            pool.wait_ge(qzero, 1)
            pool.memset(qst[:, :, :, :, 3 * D0 + 2:3 * D0 + 3], LIFT0).then_inc(const_set, 2)
            pool.wait_ge(const_set, 5)
            norm.deviation(pool, 0)
            pool.wait_ge(ctx_in[0], 16)
            v_high_low(0, 0)
            with pool.Fori(0, TRIPS) as it:
                for i in range(NG):
                    par, j = divmod(i, GPB)
                    g, b = it * NG + i, it * PAIRS + par
                    p_low(i % 2, g)
                    if j == 0:
                        norm.deviation(pool, b + 1)
                    if j == 2:
                        values(1 - par, b + 1, it + 1 + par)
                    if j == 3:
                        split_low(par, b, b)
                    if i == GPB + 1:
                        finish(0, it * PAIRS * ST, it * PAIRS)
                finish(1, (it * PAIRS + 1) * ST, it * PAIRS + 1)

        @block.scalar
        def _(act):
            def q_high(par, n):
                act.wait_ge(norm.xn_ok, n + 1)
                for st in range(ST):
                    for a in (0, 2):
                        ins = act.activation(qst[:, par, st, :, a * D0:(a + 1) * D0],
                                             xn[:, st, :].rearrange("p (h d) -> p h d", d=D0), ACT.Copy)
                ins.then_inc(qhi_ok, 1)

            def k_high(par, n, loads):
                act.wait_ge(ctx_in[par], 16 * loads)
                src = ctx[:, par].rearrange("p c (g d) -> p c g d", d=D0)
                for base in (0, D0, R0, R0 + D0):
                    ins = act.activation(kst[:, :, :, base:base + D0], src, ACT.Copy, scale=W_SCALE)
                ins.then_inc(khi_ok, 1)

            def k_out(par, half, n):
                act.wait_ge(tk_done, n * 2 + half + 1)
                act.activation(kT[:, par, 4 * half:4 * half + 4, :], pT[:, :, :], ACT.Copy).then_inc(kT_ok, 1)

            def q2_out(slot, n):
                act.wait_ge(t2_done, n + 1)
                act.activation(qT2[:, slot], pT[:, 0:2, :], ACT.Copy).then_inc(qT2_ok, 1)

            def exps(slot, c, n):
                act.wait_ge(s2_done, n * 2 + c + 1)
                if c == 0:
                    act.wait_ge(pv_done, n - 1 + PRIME_PV)
                scale = D0 ** -0.5 / (X_SCALE * W_SCALE)
                act.activation(p_hi[:, 2 * slot + c], pS2[:, c], ACT.Exp, scale=scale)
                act.wait_ge(plo_ok[c], n + PRIME_LO)
                act.activation(p32[:, c], pS2[:, c], ACT.Exp, scale=scale).then_inc(exp_done, 1)

            def split_high(par, e, it):
                act.wait_ge(stage_in[par], it * 16 + 16)
                act.wait_ge(const_set, 5)
                act.activation(w_e[:, e, 0].rearrange("p k n -> p (k n)"),
                               stage[:, par].rearrange("p k n -> p (k n)"), ACT.Copy,
                               scale=W_SCALE).then_inc(whi_ok, 1)

            act.sem_inc(exp_done, PRIME_EXP)
            act.wait_ge(const_set, 5)
            act.wait_ge(t["gates_in"], 32)
            act.activation(gates[:, :], t["g_raw"][:, :], ACT.Tanh).then_inc(t["gates_ok"], 1)
            act.wait_ge(t["kconst"], 1)
            k_high(0, 0, 1)
            q_high(0, 0)
            k_out(0, 0, 0)
            k_out(0, 1, 0)
            q2_out(0, 0)
            with act.Fori(0, TRIPS) as it:
                for i in range(NG):
                    par, j = divmod(i, GPB)
                    g, b = it * NG + i, it * PAIRS + par
                    exps(i % 2, 0, g)
                    q2_out((i + 1) % 2, g + 1)
                    exps(i % 2, 1, g)
                    if j == 0:
                        k_high(1 - par, b + 1, it + 1 + par)
                    if j == 1:
                        split_high(par, b, it)
                    if j == 2:
                        q_high(1 - par, b + 1)
                    if j in (3, 4):
                        k_out(1 - par, j - 3, b + 1)

        @block.vector
        def _(dve):
            def q_low(par, n):
                dve.wait_ge(qhi_ok, n + 1)
                for st in range(ST):
                    ins = dve.tensor_tensor(qst[:, par, st, :, D0:2 * D0],
                                            xn[:, st, :].rearrange("p (h d) -> p h d", d=D0),
                                            qst[:, par, st, :, 0:D0], ALU.subtract)
                ins.then_inc(qlo_ok, 1)

            def k_low(par, n):
                dve.wait_ge(khi_ok, n + 1)
                src = ctx[:, par].rearrange("p c (g d) -> p (c g) d", d=D0)
                flat = kst[:, :, :, :].rearrange("p c g r -> p (c g) r")
                for base in (0, R0):
                    ins = dve.scalar_tensor_tensor(flat[:, :, base + 2 * D0:base + 3 * D0], src, W_SCALE,
                                                   flat[:, :, base:base + D0], ALU.mult, ALU.subtract)
                ins.then_inc(klo_ok, 1)

            def p_low(slot, n):
                dve.wait_ge(exp_done, n * 2 + 1 + PRIME_EXP)
                dve.tensor_tensor(p_lo[:, 2 * slot], p32[:, 0], p_hi[:, 2 * slot],
                                  ALU.subtract).then_inc(plo_ok[0], 1)

            def q1_out(slot, n):
                dve.wait_ge(t1_done, n + 1)
                dve.tensor_copy(qT1[:, slot], pT[:, 0:2, :]).then_inc(qT1_ok, 1)

            def row_max(st, n, slot):
                dve.wait_ge(s1_done, n * 2 + st + 1)
                dve.tensor_reduce(negm[:, slot, st], pS1[:, :, :, :], AX.X, ALU.max, negate=True).then_inc(max_ok, 1)

            def put_max(par, g, n, slot):
                dve.wait_ge(max_ok, n * 2 + 2)
                heads = qst[:, par, :, G0 * g:G0 * g + G0, :].rearrange("p s (j r) c -> p s r j c", r=2)
                for st in range(ST):
                    ins = dve.tensor_scalar(heads[:, st, :, :, 3 * D0], negm[:, slot, st], 1.0 / M_SCALE, None, ALU.mult)
                ins.then_inc(mhi_ok, 1)
                dve.wait_ge(mhi_ok, n + 1)
                for st in range(ST):
                    ins = dve.scalar_tensor_tensor(heads[:, st, :, :, 3 * D0 + 1], negm[:, slot, st], 1.0 / M_SCALE,
                                                   heads[:, st, :, :, 3 * D0], ALU.mult, ALU.subtract)
                ins.then_inc(m_ok, 1)

            def o_out(par, g, n):
                dve.wait_ge(pv_done, n + 1 + PRIME_PV)
                dve.tensor_copy(oall[:, par, :, G0 * g:G0 * g + G0, :], o_ps).then_inc(o_ok, 1)

            def row_sums(par, n):
                dve.wait_ge(o_ok, n * GPB + GPB + PRIME_O)
                dve.wait_ge(inc_ok, n + PRIME_INC)
                dve.reciprocal(rec[:, :, :], oall[:, par, :, :, D0]).then_inc(rec0_ok, 1)
                dve.wait_ge(rec0_ok, n + 1)
                dve.tensor_scalar(rec[:, :, :], rec[:, :, :], gates[:, 0:1], 1.0 / W_SCALE, ALU.mult, ALU.mult).then_inc(rec_ok, 1)

            dve.sem_inc(o_ok, PRIME_O)
            dve.sem_inc(plo_ok[0], PRIME_LO)
            dve.memset(kst[:, :, :, :], 0.0).then_inc(t["kzero"], 1)
            dve.wait_ge(t["kzero"], 1)
            for base in (0, R0):
                ins = dve.memset(kst[:, :, :, base + 3 * D0:base + 3 * D0 + 3], M_SCALE)
            ins.then_inc(t["kconst"], 1)
            dve.wait_ge(x0_in, 16)
            norm.statistics(dve, 0, 0)
            norm.normalise(dve, 0, 0)
            dve.wait_ge(t["gates_ok"], 1)
            k_low(0, 0)
            q_low(0, 0)
            q1_out(0, 0)
            q1_out(1, 1)
            row_max(0, 0, 0)
            row_max(1, 0, 0)
            put_max(0, 0, 0, 0)
            q1_out(0, 2)
            row_max(0, 1, 1)
            row_max(1, 1, 1)
            put_max(0, 1, 1, 1)
            dve.wait_ge(x_in, 16 * (TILES - ST) // X_LOAD)
            with dve.Fori(0, TRIPS) as it:
                for i in range(NG):
                    par, j = divmod(i, GPB)
                    g, b = it * NG + i, it * PAIRS + par
                    row_max(0, g + 2, i % 2)
                    p_low(i % 2, g)
                    q1_out((i + 3) % 2, g + 3)
                    if i >= 1:
                        o_out((i - 1) // GPB, (i - 1) % GPB, g - 1)
                    if i == GPB:
                        row_sums(0, b - 1)
                    row_max(1, g + 2, i % 2)
                    put_max((i + 2) // GPB % 2, (i + 2) % GPB, g + 2, i % 2)
                    if j == 0:
                        norm.statistics(dve, ((b + 1) * ST) % TILES, b + 1)
                    if j == 1:
                        norm.normalise(dve, ((b + 1) * ST) % TILES, b + 1)
                        k_low(1 - par, b + 1)
                    if j == 3:
                        q_low(1 - par, b + 1)
                o_out(1, GPB - 1, it * NG + NG - 1)
                row_sums(1, it * PAIRS + 1)

        @block.tensor
        def _(pe):
            def keys(half, n):
                for g in range(4):
                    for c in range(ST):
                        ins = pe.transpose(pT[:, g, c * P:(c + 1) * P], kst[:, c, 4 * half + g, :], ident[:, :])
                ins.then_inc(tk_done, 1)

            def q_turn(par, g, done):
                for j in range(2):
                    for st in range(ST):
                        src = qst[:, par, st, G0 * g + 2 * j:G0 * g + 2 * j + 2, :].rearrange("p h r -> p (h r)")
                        ins = pe.transpose(pT[:, j, st * P:(st + 1) * P], src, ident[:, :])
                ins.then_inc(done, 1)

            def scores_by_row(slot, par, g, st, first=False):
                for j in range(2):
                    for r in range(2):
                        rows = slice(R0 * r, R0 * r + 3 * D0)
                        ins = pe.matmul(pS1[:, r, j, :], qT1[rows, slot, j, st * P:(st + 1) * P],
                                        kT[rows, par, g, :], start=True, stop=True)
                ins.then_inc(s1_done, 1)

            def scores_by_key(slot, par, g, c):
                for r in range(2):
                    rows = slice(R0 * r, R0 * r + 3 * D0 + 3)
                    ins = pe.matmul(pS2[:, c, r].rearrange("p j s -> p (j s)"),
                                    kT[rows, par, g, c * P:(c + 1) * P],
                                    qT2[rows, slot].rearrange("p j s -> p (j s)"), start=True, stop=True)
                ins.then_inc(s2_done, 1)

            def weigh(slot, par, g, n):
                pe.wait_ge(plo_ok[0], n + 1 + PRIME_LO)
                pe.wait_ge(plo_ok[1], n + 1 + PRIME_LO)
                pe.wait_ge(o_ok, n + PRIME_O)
                for st in range(ST):
                    for h in range(G0):
                        for c in range(ST):
                            for half, probs in enumerate((p_hi, p_lo)):
                                ins = pe.matmul(o_ps[:, st, h, :],
                                                probs[:, 2 * slot + c, h % 2, h // 2, st * P:(st + 1) * P],
                                                vst[:, par, c, g, :], start=(c == 0 and half == 0),
                                                stop=(c == ST - 1 and half == 1))
                ins.then_inc(pv_done, 1)

            pe.sem_inc(pv_done, PRIME_PV)
            pe.wait_ge(t["ident_in"], 16)
            pe.wait_ge(klo_ok, 1)
            keys(0, 0)
            pe.wait_ge(kT_ok, 1)
            keys(1, 0)
            pe.wait_ge(qlo_ok, 1)
            pe.wait_ge(kT_ok, 2)
            q_turn(0, 0, t1_done)
            pe.wait_ge(qT1_ok, 1)
            q_turn(0, 1, t1_done)
            pe.wait_ge(qT1_ok, 2)
            scores_by_row(0, 0, 0, 0)
            pe.wait_ge(max_ok, 1)
            scores_by_row(0, 0, 0, 1)
            q_turn(0, 2, t1_done)
            pe.wait_ge(max_ok, 2)
            scores_by_row(1, 0, 1, 0)
            pe.wait_ge(max_ok, 3)
            scores_by_row(1, 0, 1, 1)
            pe.wait_ge(qT1_ok, 3)
            pe.wait_ge(m_ok, 1)
            q_turn(0, 0, t2_done)
            with pe.Fori(0, TRIPS) as it:
                for i in range(NG):
                    par, j = divmod(i, GPB)
                    g, b = it * NG + i, it * PAIRS + par
                    pe.wait_ge(qT2_ok, g + 1)
                    pe.wait_ge(exp_done, 2 * g - 1 + PRIME_EXP)
                    scores_by_key(i % 2, par, j, 0)
                    p1, g1 = (i + 1) // GPB % 2, (i + 1) % GPB
                    pe.wait_ge(m_ok, g + 2)
                    pe.wait_ge(qT1_ok, g + 3)
                    if j in (4, 5):
                        pe.wait_ge(kT_ok, (b + 1) * 2 + j - 3)
                    q_turn(p1, g1, t2_done)
                    p2, g2 = (i + 2) // GPB % 2, (i + 2) % GPB
                    if g2 == 0:
                        pe.wait_ge(kT_ok, (b + 1) * 2 + 2)
                    pe.wait_ge(max_ok, 2 * g + 4)
                    scores_by_row((i + 2) % 2, p2, g2, 0)
                    pe.wait_ge(exp_done, 2 * g + PRIME_EXP)
                    scores_by_key(i % 2, par, j, 1)
                    p3, g3 = (i + 3) // GPB % 2, (i + 3) % GPB
                    if g3 == 0:
                        pe.wait_ge(qlo_ok, b + 2)
                    pe.wait_ge(qT2_ok, g + 2)
                    q_turn(p3, g3, t1_done)
                    if i >= 1:
                        pm, gm = (i - 1) // GPB, (i - 1) % GPB
                        if gm == 0:
                            pe.wait_ge(v_ok, it * PAIRS + pm + 1)
                        weigh((i - 1) % 2, pm, gm, g - 1)
                    if j in (3, 4):
                        if j == 3:
                            pe.wait_ge(klo_ok, b + 2)
                        pe.wait_ge(qT1_ok, g + 4)
                        keys(j - 3, b + 1)
                    pe.wait_ge(max_ok, 2 * g + 5)
                    scores_by_row((i + 2) % 2, p2, g2, 1)
                weigh((NG - 1) % 2, 1, GPB - 1, it * NG + NG - 1)


BIAS_OUT, BIAS_ROUTER, BIAS_ROWS, BIAS_LOW = 8, 9, 10, 32
NE = 8
C_SCALE = 256.0


def phase_experts(nc, mem, t):
    x, w_e, stage, ident, w_small = t["x"], t["w_e"], t["stage"], t["ident"], t["w_small"]
    TRIPS = B // PAIRS
    UNITS = NE * ST
    RING = 4

    def sb(name, shape, dt):
        return mem.enter_context(nc.sbuf_tensor("m_" + name, shape, dt))

    def sem(name):
        return mem.enter_context(nc.semaphore("m_" + name))

    norm = Norm(nc, mem, "m", t)
    hid = Split(nc, mem, "m_hid", PAIRS)
    com = Split(nc, mem, "m_com", 1)
    y = sb("y", [P, RING, E], F32)
    acc = sb("acc", [P, PAIRS, ST, E], F32)
    sel = sb("sel", [P, BIAS_ROWS, P], F16)
    bias_raw = sb("bias_raw", [P, E], F32)
    bias_hi = sb("bias_hi", [P, E], F16)
    bias = sb("bias", [P, E], F16)
    rw_raw = sb("rw_raw", [P, KC, NE], F32)
    rw = sb("rw", [P, 2, KC, NE], F16)
    ramp = sb("ramp", [P, NE], F32)
    wscale = sb("wscale", [P, 1], F32)
    gscale = sb("gscale", [P, 1], F32)
    logit = sb("logit", [P, ST, NE], F32)
    rest = sb("rest", [P, ST, NE], F32)
    first = sb("first", [P, ST, NE], F32)
    second = sb("second", [P, ST, NE], F32)
    best = sb("best", [P, 6, ST], F32)
    tanh_d = sb("tanh_d", [P, ST], F32)
    gate = sb("gate", [P, PAIRS, ST, NE], F32)

    pE = mem.enter_context(nc.psum_tensor("m_pE", [P, RING, E], F32))
    pT = mem.enter_context(nc.psum_tensor("m_pT", [P, 2, KC, S], F16))
    pR = mem.enter_context(nc.psum_tensor("m_pR", [P, 512], F32))
    pO = mem.enter_context(nc.psum_tensor("m_pO", [P, E], F32))
    logits_ps = pR[:, 0:ST * NE].rearrange("p (s e) -> p s e", s=ST)

    consts_in, zeroed, consts_ok, bias_ok = sem("consts_in"), sem("zeroed"), sem("consts_ok"), sem("bias_ok")
    rw_ok, ramp_ok, wscale_ok = sem("rw_ok"), sem("ramp_ok"), sem("wscale_ok")
    small_in, small_hi, small_32, small_lo = sem("small_in"), sem("small_hi"), sem("small_32"), sem("small_lo")
    routed, tanh_ok, gate_chain = sem("routed"), sem("tanh_ok"), sem("gate_chain")
    expert_done, gelu_done, acc_done = sem("expert_done"), sem("gelu_done"), sem("acc_done")
    out_done, x_ok = sem("out_done"), sem("x_ok")
    GATE_STEPS, GATE_DIFF = 18, 9
    PRIME_X, PRIME_COLS, PRIME_SMALL = 1, 1, 1

    with nc.Block() as block:

        @block.sync
        def _(sp):
            sp.dma_start(sel[:, :, :], t["sel_d"]).then_inc(consts_in, 16)
            sp.dma_start(rw_raw[:, :, :], t["router_d"]).then_inc(consts_in, 16)
            sp.dma_start(ramp[:, :], t["ramp_d"].partition_broadcast(P)).then_inc(consts_in, 16)
            sp.wait_ge(zeroed, 1)
            for row in (0, BIAS_LOW):
                sp.dma_start(bias_raw[row:row + NE, :], t["expert_b_d"]).then_inc(consts_in, 16)
                sp.dma_start(bias_raw[row + BIAS_OUT:row + BIAS_OUT + 1, :], t["out_b_d"]).then_inc(consts_in, 16)
                sp.dma_start(bias_raw[row + BIAS_ROUTER:row + BIAS_ROUTER + 1, 0:NE],
                             t["router_b_d"]).then_inc(consts_in, 16)
            with sp.Fori(0, TRIPS) as it:
                sp.wait_ge(small_lo, it + PRIME_SMALL)
                sp.dma_start(stage[:, 0], t["small_d"][:, it]).then_inc(small_in, 16)

        @block.gpsimd
        def _(pool):
            pool.sem_inc(small_lo, PRIME_SMALL)
            pool.memset(bias_raw[:, :], 0.0).then_inc(zeroed, 1)
            pool.memset(wscale[:, :], W_SCALE).then_inc(wscale_ok, 1)
            pool.wait_ge(wscale_ok, 1)
            norm.deviation(pool, 0)
            with pool.Fori(0, TRIPS) as it:
                norm.deviation(pool, it * PAIRS + 1)
                raw = stage[:, 0].rearrange("p k n -> p (k n)")
                hi = w_small[:, it, 0].rearrange("p k n -> p (k n)")
                lo = w_small[:, it, 1].rearrange("p k n -> p (k n)")
                wide = wscale[:, :].to_broadcast([P, KC * E])
                pool.wait_ge(small_in, it * 16 + 16)
                pool.wait_ge(wscale_ok, 1)
                pool.tensor_tensor(hi, raw, wide, ALU.mult).then_inc(small_hi, 1)
                pool.wait_ge(small_hi, it + 1)
                pool.tensor_tensor(raw, raw, wide, ALU.mult).then_inc(small_32, 1)
                pool.wait_ge(small_32, it + 1)
                pool.wait_ge(wscale_ok, 1)
                pool.tensor_tensor(lo, raw, hi, ALU.subtract).then_inc(small_lo, 1)
                norm.deviation(pool, it * PAIRS + 2)

        @block.scalar
        def _(act):
            def gelu(e, st, n):
                u = n * UNITS + e * ST + st
                slot = (e * ST + st) % RING
                act.wait_ge(expert_done, u + 1)
                act.wait_ge(acc_done, u + 1)
                act.activation(y[:, slot], pE[:, slot], ACT.Gelu_apprx_tanh,
                               scale=1.0 / (X_SCALE * W_SCALE)).then_inc(gelu_done, 1)

            def half_difference(n):
                act.wait_ge(gate_chain, n * GATE_STEPS + GATE_DIFF)
                act.activation(tanh_d[:, :], best[:, 4], ACT.Tanh, scale=0.5).then_inc(tanh_ok, 1)

            def hid_high(n):
                act.wait_ge(norm.xn_ok, n + 1)
                hid.high(act, norm.xn[:, :, :])

            def com_high(par, n):
                act.wait_ge(acc_done, (n + 1) * UNITS + RING)
                com.high(act, acc[:, par])

            act.sem_inc(gelu_done, RING)
            act.sem_inc(com.cols_ok, PRIME_COLS)
            act.wait_ge(bias_ok, 1)
            act.activation(bias_hi[:, :], bias_raw[:, :], ACT.Copy, scale=W_SCALE).then_inc(consts_ok, 1)
            act.activation(rw[:, 0], rw_raw[:, :, :], ACT.Copy, scale=W_SCALE).then_inc(consts_ok, 1)
            hid_high(0)
            for half in range(2):
                hid.out(act, half, pT[:, half], 0, 0)
            half_difference(0)
            with act.Fori(0, TRIPS) as it:
                for par in range(PAIRS):
                    b = it * PAIRS + par
                    for e in range(NE):
                        for st in range(ST):
                            gelu(e, st, b)
                        if par == 1 and e == 0:
                            com_high(0, b - 1)
                        if par == 1 and e == 1:
                            for half in range(2):
                                com.out(act, half, pT[:, half], 0, b - 1)
                        if e == 2:
                            hid_high(b + 1)
                        if par == 0 and e == 3:
                            for half in range(2):
                                hid.out(act, half, pT[:, half], 1, b + 1)
                        if par == 0 and e == 6:
                            half_difference(b + 1)
                b = it * PAIRS + 1
                for half in range(2):
                    hid.out(act, half, pT[:, half], 0, b + 1)
                com_high(1, b)
                half_difference(b + 1)
                for half in range(2):
                    com.out(act, half, pT[:, half], 0, b)

        @block.vector
        def _(dve):
            def spread(ap):
                return ap.unsqueeze(2).to_broadcast([P, ST, NE])

            def link(n, k):
                dve.wait_ge(gate_chain, n * GATE_STEPS + k)

            ramp3 = ramp[:, :].unsqueeze(1).to_broadcast([P, ST, NE])

            def first_best(src, out, m, w, n, k):
                link(n, k)
                dve.tensor_reduce(best[:, m], src, AX.X, ALU.max).then_inc(gate_chain, 1)
                link(n, k + 1)
                dve.tensor_tensor(out, src, spread(best[:, m]), ALU.is_equal).then_inc(gate_chain, 1)
                link(n, k + 2)
                dve.tensor_tensor(out, out, ramp3, ALU.mult).then_inc(gate_chain, 1)
                link(n, k + 3)
                dve.tensor_reduce(best[:, w], out, AX.X, ALU.max).then_inc(gate_chain, 1)
                link(n, k + 4)
                dve.tensor_tensor(out, out, spread(best[:, w]), ALU.is_equal).then_inc(gate_chain, 1)

            def gates_a(n):
                dve.wait_ge(routed, n + 1)
                dve.tensor_scalar(logit[:, :, :], logits_ps, 1.0 / (X_SCALE * W_SCALE), None,
                                  ALU.mult).then_inc(gate_chain, 1)
                first_best(logit[:, :, :], first[:, :, :], 0, 1, n, 1)
                link(n, 6)
                dve.scalar_tensor_tensor(rest[:, :, :], first[:, :, :], -1e30, logit[:, :, :],
                                         ALU.mult, ALU.add).then_inc(gate_chain, 1)
                link(n, 7)
                dve.tensor_reduce(best[:, 2], rest[:, :, :], AX.X, ALU.max).then_inc(gate_chain, 1)
                link(n, 8)
                dve.tensor_tensor(best[:, 4], best[:, 0], best[:, 2], ALU.subtract).then_inc(gate_chain, 1)

            def gates_b(par, n):
                link(n, 9)
                dve.tensor_tensor(second[:, :, :], rest[:, :, :], spread(best[:, 2]),
                                  ALU.is_equal).then_inc(gate_chain, 1)
                link(n, 10)
                dve.tensor_tensor(second[:, :, :], second[:, :, :], ramp3, ALU.mult).then_inc(gate_chain, 1)
                link(n, 11)
                dve.tensor_reduce(best[:, 3], second[:, :, :], AX.X, ALU.max).then_inc(gate_chain, 1)
                link(n, 12)
                dve.tensor_tensor(second[:, :, :], second[:, :, :], spread(best[:, 3]),
                                  ALU.is_equal).then_inc(gate_chain, 1)
                dve.wait_ge(tanh_ok, n + 1)
                dve.tensor_scalar(best[:, 0], tanh_d[:, :], C_SCALE / 2, C_SCALE / 2,
                                  ALU.mult, ALU.add).then_inc(gate_chain, 1)
                dve.tensor_scalar(best[:, 5], tanh_d[:, :], -C_SCALE / 2, C_SCALE / 2,
                                  ALU.mult, ALU.add).then_inc(gate_chain, 1)
                link(n, 15)
                dve.tensor_tensor(first[:, :, :], first[:, :, :], spread(best[:, 0]),
                                  ALU.mult).then_inc(gate_chain, 1)
                dve.tensor_tensor(second[:, :, :], second[:, :, :], spread(best[:, 5]),
                                  ALU.mult).then_inc(gate_chain, 1)
                link(n, 17)
                dve.tensor_tensor(gate[:, par], first[:, :, :], second[:, :, :], ALU.add).then_inc(gate_chain, 1)

            def accumulate(par, e, st, n):
                u = n * UNITS + e * ST + st
                slot = (e * ST + st) % RING
                if e >= 1:
                    dve.wait_ge(acc_done, u - 1 + RING)
                dve.wait_ge(gelu_done, u + 1 + RING)
                scalar = gate[:, par, st, e:e + 1]
                if e == 0:
                    dve.tensor_scalar(acc[:, par, st], y[:, slot], scalar, None, ALU.mult).then_inc(acc_done, 1)
                else:
                    dve.scalar_tensor_tensor(acc[:, par, st], y[:, slot], scalar, acc[:, par, st],
                                             ALU.mult, ALU.add).then_inc(acc_done, 1)

            def update(tile, st, n):
                dve.wait_ge(out_done, n * ST + st + 1)
                dve.wait_ge(rw_ok, 1)
                xt = x[:, tile + st, :]
                dve.scalar_tensor_tensor(xt, pO[:, :], gscale[:, :], xt, ALU.mult, ALU.add).then_inc(x_ok, 1)

            dve.sem_inc(acc_done, RING)
            dve.sem_inc(x_ok, PRIME_X)
            norm.statistics(dve, 0, 0)
            dve.memset(bias[:, :], 0.0).then_inc(ramp_ok, 1)
            dve.tensor_scalar(gscale[:, :], t["tanh_g"][:, 2:3], 1.0 / (C_SCALE * W_SCALE), None, ALU.mult)
            dve.wait_ge(consts_in, 9 * 16)
            dve.tensor_copy(ramp[:, :], ramp[:, :]).then_inc(bias_ok, 1)
            norm.normalise(dve, 0, 0)
            dve.wait_ge(ramp_ok, 1)
            dve.wait_ge(consts_ok, 2)
            dve.tensor_copy(bias[0:BIAS_ROWS, :], bias_hi[0:BIAS_ROWS, :])
            low = slice(BIAS_LOW, BIAS_LOW + BIAS_ROWS)
            dve.scalar_tensor_tensor(bias[low, :], bias_raw[low, :], W_SCALE, bias_hi[low, :],
                                     ALU.mult, ALU.subtract)
            dve.scalar_tensor_tensor(rw[:, 1], rw_raw[:, :, :], W_SCALE, rw[:, 0],
                                     ALU.mult, ALU.subtract).then_inc(rw_ok, 1)
            dve.drain().then_inc(zeroed, 1)
            hid.low(dve, norm.xn[:, :, :], 0)
            gates_a(0)
            gates_b(0, 0)
            with dve.Fori(0, TRIPS) as it:
                for par in range(PAIRS):
                    b = it * PAIRS + par
                    ahead = ((b + 1) * ST) % TILES
                    dve.wait_ge(gate_chain, (b + 1) * GATE_STEPS)
                    for e in range(NE):
                        for st in range(ST):
                            accumulate(par, e, st, b)
                        if e == 0:
                            if par == 1:
                                com.low(dve, acc[:, 0], b - 1)
                            norm.statistics(dve, ahead, b + 1)
                        if e == 1:
                            norm.normalise(dve, ahead, b + 1)
                        if e == 2:
                            hid.low(dve, norm.xn[:, :, :], b + 1)
                        if par == 1 and e in (3, 5):
                            update((b - 1) * ST, (e - 3) // 2, b - 1)
                        if par == 0 and e == 5:
                            gates_a(b + 1)
                        if par == 0 and e == 6:
                            gates_b(1, b + 1)
                b = it * PAIRS + 1
                com.low(dve, acc[:, 1], b)
                gates_a(b + 1)
                gates_b(0, b + 1)
                for st in range(ST):
                    update(b * ST, st, b)

        @block.tensor
        def _(pe):
            def route(par, n):
                pe.wait_ge(gate_chain, (n - 1) * GATE_STEPS + 1)
                route_now(par)

            def route_now(par):
                for st in range(ST):
                    project(pe, logits_ps[:, st], hid.cols, par, st, rw, more=True)
                    ins = pe.matmul(logits_ps[:, st], sel[:, BIAS_ROUTER, :], bias[:, 0:NE], start=False, stop=True)
                ins.then_inc(routed, 1)

            def expert(par, e, st, n):
                u = n * UNITS + e * ST + st
                slot = (e * ST + st) % RING
                pe.wait_ge(gelu_done, u + 1)
                project(pe, pE[:, slot], hid.cols, par, st, w_e[:, e], more=True)
                pe.matmul(pE[:, slot], sel[:, e, :], bias[:, :], start=False, stop=True).then_inc(expert_done, 1)

            def combine(st, n):
                pe.wait_ge(com.cols_ok, 2 * n + 2 + PRIME_COLS)
                pe.wait_ge(x_ok, n * ST + st + PRIME_X)
                project(pe, pO[:, :], com.cols, 0, st, w_small[:, 0], more=True)
                pe.matmul(pO[:, :], sel[:, BIAS_OUT, :], bias[:, :], start=False, stop=True).then_inc(out_done, 1)

            pe.wait_ge(hid.lo_ok, 1)
            for half in range(2):
                hid.turn(pe, half, pT[:, half], ident)
            pe.wait_ge(rw_ok, 1)
            pe.wait_ge(hid.cols_ok, 2)
            route_now(0)
            with pe.Fori(0, TRIPS) as it:
                for par in range(PAIRS):
                    b = it * PAIRS + par
                    pe.wait_ge(hid.cols_ok, 2 * b + 2)
                    for e in range(NE):
                        for st in range(ST):
                            expert(par, e, st, b)
                        if par == 0 and e == 3:
                            pe.wait_ge(hid.lo_ok, b + 2)
                            pe.wait_ge(com.cols_ok, 2 * b + PRIME_COLS)
                            for half in range(2):
                                hid.turn(pe, half, pT[:, half], ident)
                        if par == 0 and e == 4:
                            pe.wait_ge(hid.cols_ok, 2 * b + 4)
                            route(1, b + 1)
                        if par == 1 and e == 1:
                            pe.wait_ge(com.lo_ok, b)
                            for half in range(2):
                                com.turn(pe, half, pT[:, half], ident)
                        if par == 1 and e in (2, 4):
                            pe.wait_ge(small_lo, 1 + PRIME_SMALL)
                            combine((e - 2) // 2, b - 1)
                b = it * PAIRS + 1
                pe.wait_ge(hid.lo_ok, b + 2)
                for half in range(2):
                    hid.turn(pe, half, pT[:, half], ident)
                pe.wait_ge(hid.cols_ok, 2 * b + 4)
                route(0, b + 1)
                pe.wait_ge(com.lo_ok, b + 1)
                for half in range(2):
                    com.turn(pe, half, pT[:, half], ident)
                for st in range(ST):
                    combine(st, b)


H1, D1 = 16, 32
G1 = 4
R1 = 128
V1 = 2 * D1 + 1
Q1_SCALE, K1_SCALE, V1_SCALE = 64.0, 1024.0, 1024.0
LIFT1 = 627.0
MASK = 32768.0


def phase_attention1(nc, mem, t):
    x, ident, w_small = t["x"], t["ident"], t["w_small"]
    GPB = H1 // G1
    NG = PAIRS * GPB
    TRIPS = B // PAIRS
    W = S + P

    def sb(name, shape, dt):
        return mem.enter_context(nc.sbuf_tensor("a1_" + name, shape, dt))

    def sem(name):
        return mem.enter_context(nc.semaphore("a1_" + name))

    arena = t["w_e"][:, :, :, :, :].rearrange("p e a k n -> p (e a k n)")
    used = [0]

    def carve(n):
        used[0] += n
        return arena[:, used[0] - n:used[0]]

    qst = carve(PAIRS * ST * H1 * R1).rearrange("p (a s h r) -> p a s h r", a=PAIRS, s=ST, h=H1)
    kst = carve(ST * H1 * R1).rearrange("p (s h r) -> p s h r", s=ST, h=H1)
    kT = carve(PAIRS * H1 * S).rearrange("p (a h t) -> p a h t", a=PAIRS, h=H1)
    p_hi = carve(2 * G1 * W).rearrange("p (a h w) -> p a h w", a=2, h=G1)
    p_lo = carve(2 * G1 * W).rearrange("p (a h w) -> p a h w", a=2, h=G1)
    vst = carve(PAIRS * ST * H1 * V1).rearrange("p (a s h d) -> p a s h d", a=PAIRS, s=ST, h=H1)

    norm = Norm(nc, mem, "a1", t)
    hid = Split(nc, mem, "a1_hid", 1)
    com = Split(nc, mem, "a1_com", 1)
    ctx = sb("ctx", [P, PAIRS, ST, L], F32)
    cx = sb("cx", [P, 2, ST, L], F16)
    cxT = sb("cxT", [P, 2, S], F16)
    qT1 = sb("qT1", [P, 2, G1, S], F16)
    qT2 = sb("qT2", [P, 2, G1, S], F16)
    p32 = sb("p32", [P, G1, W], F32)
    negm = sb("negm", [P, 2, ST, G1], F32)
    oall = sb("oall", [P, ST, H1, V1], F32)
    o32 = sb("o32", [P, ST, H1, D1], F32)
    rec = sb("rec", [P, ST, H1], F32)
    gscale = sb("gscale", [P, 1], F32)
    big_ident = sb("big_ident", [P, P], F16)
    mask_row = sb("mask_row", [P, P], F16)
    mask_key = sb("mask_key", [P, P], F16)

    pS2 = mem.enter_context(nc.psum_tensor("a1_pS2", [P, 2, 512], F32))
    pS1 = mem.enter_context(nc.psum_tensor("a1_pS1", [P, G1, S], F32))
    pT = mem.enter_context(nc.psum_tensor("a1_pT", [P, 2, G1, S], F16))
    pO = mem.enter_context(nc.psum_tensor("a1_pO", [P, 512], F32))
    pP = mem.enter_context(nc.psum_tensor("a1_pP", [P, E], F32))
    o_ps = pO[:, 0:G1 * V1].rearrange("p (h d) -> p h d", h=G1)
    pP_heads = pP[:, :].rearrange("p (h d) -> p h d", h=H1)
    pT_cx = pT[:, 0].rearrange("p g t -> p (g t)")[:, 0:2 * S].rearrange("p (a t) -> p a t", a=2)

    ctx_in = [sem(f"ctx{par}_in") for par in range(PAIRS)]
    masks_in, zeroed, const_set, k_const = sem("masks_in"), sem("zeroed"), sem("const_set"), sem("k_const")
    cxhi_ok, cxlo_ok, cx_turned, cx_ok = sem("cxhi_ok"), sem("cxlo_ok"), sem("cx_turned"), sem("cx_ok")
    projected, pphi_ok, pp_ok = sem("projected"), sem("pphi_ok"), sem("pp_ok")
    k_turned, kT_ok = sem("k_turned"), sem("kT_ok")
    t1_done, t2_done, qT1_ok, qT2_ok = sem("t1_done"), sem("t2_done"), sem("qT1_ok"), sem("qT2_ok")
    dup_ok = sem("dup_ok")
    s1_done, max_ok, mhi_ok, m_ok = sem("s1_done"), sem("max_ok"), sem("mhi_ok"), sem("m_ok")
    s2_done, exp_done = sem("s2_done"), sem("exp_done")
    plo_ok = [sem("plo_dve"), sem("plo_pool")]
    pv_done, o_ok = sem("pv_done"), sem("o_ok")
    rec_ok, osum_ok, o32_ok = sem("rec_ok"), sem("osum_ok"), sem("o32_ok")
    PRIME_EXP, PRIME_LO, PRIME_PV, PRIME_O = 2, 2, 4, 1

    STEP_USES = (("k", 0), ("k", 1)), (("v", 0), ("q", 0)), (("v", 1), ("q", 1)), (("out", 0), ("out", 1))
    PREP = 6

    def use(g, k):
        return PREP + 2 * g + k

    def high_count(b, j, k):
        return PREP * (b + 1) + 2 * j + k

    with nc.Block() as block:

        @block.sync
        def _(sp):
            def load_ctx(b, par):
                sp.dma_start(ctx[:, par], t["ctx_d"][:, b]).then_inc(ctx_in[par], 16)

            load_ctx(0, 0)
            load_ctx(1, 1)
            sp.dma_start(big_ident[:, :], t["big_ident_d"]).then_inc(masks_in, 16)
            sp.dma_start(mask_row[:, :], t["mask_row_d"]).then_inc(masks_in, 16)
            sp.dma_start(mask_key[:, :], t["mask_key_d"]).then_inc(masks_in, 16)
            with sp.Fori(0, TRIPS) as it:
                for par in range(PAIRS):
                    sp.wait_ge(cxlo_ok, it * PAIRS + par + 1)
                    load_ctx((it * PAIRS + PAIRS + par) % B, par)
            for par in range(PAIRS):
                sp.wait_ge(ctx_in[par], 16 * (TRIPS + 1))

        @block.gpsimd
        def _(pool):
            def p_low(slot, h, n):
                pool.wait_ge(exp_done, G1 * n + h + 1 + PRIME_EXP)
                pool.tensor_tensor(p_lo[:, slot, h], p32[:, h], p_hi[:, slot, h],
                                   ALU.subtract).then_inc(plo_ok[1], 1)

            def finish(n):
                pool.wait_ge(rec_ok, n + 1)
                pool.tensor_tensor(o32[:, :, :, :], oall[:, :, :, 0:D1], oall[:, :, :, D1 + 1:],
                                   ALU.add).then_inc(osum_ok, 1)
                pool.wait_ge(osum_ok, n + 1)
                pool.tensor_tensor(o32[:, :, :, :], o32[:, :, :, :],
                                   rec[:, :, :].unsqueeze(3).to_broadcast([P, ST, H1, D1]),
                                   ALU.mult).then_inc(o32_ok, 1)

            pool.sem_inc(plo_ok[1], PRIME_LO)
            pool.memset(qst, 0.0)
            pool.memset(vst, 0.0)
            pool.memset(p_hi[:, 1], 1.0)
            pool.memset(p_lo[:, 1], 0.0)
            pool.memset(oall[:, :, :, :], 0.0).then_inc(zeroed, 1)
            pool.wait_ge(zeroed, 1)
            pool.memset(qst[:, :, :, :, 3 * D1 + 2:3 * D1 + 3], LIFT1)
            pool.memset(oall[:, :, :, D1:D1 + 1], 1.0)
            pool.memset(vst[:, :, :, :, D1:D1 + 1], 1.0).then_inc(const_set, 1)
            norm.deviation(pool, 0)
            norm.deviation(pool, 1)
            with pool.Fori(0, TRIPS) as it:
                for i in range(NG):
                    par, j = divmod(i, GPB)
                    g, b = it * NG + i, it * PAIRS + par
                    if j == 2:
                        norm.deviation(pool, b + 2)
                    for h in (2, 3):
                        p_low(i % 2, h, g)
                    if j == 0:
                        finish(b)
            finish(B)

        @block.scalar
        def _(act):
            def exps(slot, h, n):
                u = G1 * n + h
                act.wait_ge(s2_done, u + 1)
                if h == 0:
                    act.wait_ge(pv_done, 2 * n + PRIME_PV)
                scale = D1 ** -0.5 / (Q1_SCALE * K1_SCALE)
                act.activation(p_hi[:, slot, h], pS2[:, h % 2, 0:W], ACT.Exp, scale=scale)
                act.wait_ge(plo_ok[h // 2], 2 * n + h % 2 + 1)
                act.activation(p32[:, h], pS2[:, h % 2, 0:W], ACT.Exp, scale=scale).then_inc(exp_done, 1)

            def ctx_high(par, loads):
                act.wait_ge(ctx_in[par], 16 * loads)
                act.activation(cx[:, 0], ctx[:, par], ACT.Copy, scale=W_SCALE).then_inc(cxhi_ok, 1)

            def hid_high(n):
                act.wait_ge(norm.xn_ok, n + 1)
                hid.high(act, norm.xn[:, :, :])

            def hid_out(n):
                for half in range(2):
                    hid.out(act, half, pT[:, half], 0, n)

            def ctx_out(n):
                act.wait_ge(cx_turned, n + 1)
                act.activation(cxT[:, :, :], pT_cx, ACT.Copy).then_inc(cx_ok, 1)

            def high(kind, par, st, uses):
                act.wait_ge(projected, uses + 1)
                if kind == "q":
                    ins = act.activation(qst[:, par, st, :, 0:D1], pP_heads, ACT.Copy,
                                         scale=Q1_SCALE / (X_SCALE * W_SCALE))
                elif kind == "k":
                    ins = act.activation(kst[:, st, :, 0:D1], pP_heads, ACT.Copy,
                                         scale=K1_SCALE / (W_SCALE * W_SCALE))
                else:
                    ins = act.activation(vst[:, par, st, :, 0:D1], pP_heads, ACT.Copy,
                                         scale=V1_SCALE / (W_SCALE * W_SCALE))
                ins.then_inc(pphi_ok, 1)

            def keys_out(par, k, n):
                act.wait_ge(k_turned, 4 * n + k + 1)
                act.activation(kT[:, par, G1 * k:G1 * k + G1, :], pT[:, k % 2], ACT.Copy).then_inc(kT_ok, 1)

            def com_high(n):
                act.wait_ge(o32_ok, n + 1)
                com.high(act, o32[:, :, :, :].rearrange("p s h d -> p s (h d)"))

            act.sem_inc(exp_done, PRIME_EXP)
            ctx_high(0, 1)
            hid_high(0)
            hid_out(0)
            ctx_out(0)
            act.wait_ge(k_const, 1)
            act.wait_ge(const_set, 1)
            for n, (kind, st) in enumerate(PREPARE):
                high(kind, 0, st, n)
            for k in range(4):
                keys_out(0, k, 0)
            ctx_high(1, 1)
            hid_high(1)
            hid_out(1)
            ctx_out(1)
            with act.Fori(0, TRIPS) as it:
                for i in range(NG):
                    par, j = divmod(i, GPB)
                    g, b = it * NG + i, it * PAIRS + par
                    if j == 3:
                        hid_high(b + 2)
                    exps(i % 2, 0, g)
                    if j < 3:
                        kind, st = STEP_USES[j][0]
                        high(kind, 1 - par, st, use(g, 0))
                    exps(i % 2, 1, g)
                    if j == 2:
                        for k in (2, 3):
                            keys_out(1 - par, k, b + 1)
                        com_high(b)
                    if j == 3:
                        hid_out(b + 2)
                    exps(i % 2, 2, g)
                    if j < 3:
                        kind, st = STEP_USES[j][1]
                        high(kind, 1 - par, st, use(g, 1))
                    if j == 0:
                        ctx_high(par, it + 2)
                    if j == 1:
                        for k in (0, 1):
                            keys_out(1 - par, k, b + 1)
                    if j == 2:
                        for half in range(2):
                            com.out(act, half, pT[:, half], 0, b)
                    if j == 3:
                        ctx_out(b + 2)
                    exps(i % 2, 3, g)
            com_high(B)
            for half in range(2):
                com.out(act, half, pT[:, half], 0, B)

        @block.vector
        def _(dve):
            def ctx_low(par, n):
                dve.wait_ge(cxhi_ok, n + 1)
                dve.scalar_tensor_tensor(cx[:, 1], ctx[:, par], W_SCALE, cx[:, 0],
                                         ALU.mult, ALU.subtract).then_inc(cxlo_ok, 1)

            def low(kind, par, st, uses, highs):
                dve.wait_ge(pphi_ok, highs + 1)
                if kind == "q":
                    dst, hi = qst[:, par, st, :, D1:2 * D1], qst[:, par, st, :, 0:D1]
                    scale = Q1_SCALE / (X_SCALE * W_SCALE)
                elif kind == "k":
                    dst, hi = kst[:, st, :, 2 * D1:3 * D1], kst[:, st, :, 0:D1]
                    scale = K1_SCALE / (W_SCALE * W_SCALE)
                else:
                    dst, hi = vst[:, par, st, :, D1 + 1:], vst[:, par, st, :, 0:D1]
                    scale = V1_SCALE / (W_SCALE * W_SCALE)
                dve.scalar_tensor_tensor(dst, pP_heads, scale, hi, ALU.mult, ALU.subtract).then_inc(pp_ok, 1)
                if kind == "q":
                    dve.tensor_copy(qst[:, par, st, :, 2 * D1:3 * D1], hi).then_inc(dup_ok, 1)
                elif kind == "k":
                    dve.tensor_copy(kst[:, st, :, D1:2 * D1], hi).then_inc(dup_ok, 1)

            def p_low(slot, h, n):
                dve.wait_ge(exp_done, G1 * n + h + 1 + PRIME_EXP)
                dve.tensor_tensor(p_lo[:, slot, h], p32[:, h], p_hi[:, slot, h],
                                  ALU.subtract).then_inc(plo_ok[0], 1)

            def q1_out(slot, n):
                dve.wait_ge(t1_done, n + 1)
                dve.tensor_copy(qT1[:, slot], pT[:, 0]).then_inc(qT1_ok, 1)

            def q2_out(slot, n):
                dve.wait_ge(t2_done, n + 1)
                dve.tensor_copy(qT2[:, slot], pT[:, 1]).then_inc(qT2_ok, 1)

            def row_max(st, slot, n):
                dve.wait_ge(s1_done, 2 * n + st + 1)
                dve.tensor_reduce(negm[:, slot, st], pS1[:, :, 0:(st + 1) * P], AX.X, ALU.max,
                                  negate=True).then_inc(max_ok, 1)

            def put_max(par, g, slot, n):
                dve.wait_ge(max_ok, 2 * n + 2)
                heads = qst[:, par, :, G1 * g:G1 * g + G1, :]
                dve.tensor_scalar(heads[:, :, :, 3 * D1], negm[:, slot], 1.0 / M_SCALE, None,
                                  ALU.mult).then_inc(mhi_ok, 1)
                dve.wait_ge(mhi_ok, n + 1)
                dve.scalar_tensor_tensor(heads[:, :, :, 3 * D1 + 1], negm[:, slot], 1.0 / M_SCALE,
                                         heads[:, :, :, 3 * D1], ALU.mult, ALU.subtract).then_inc(m_ok, 1)

            def o_out(st, g, n, batch):
                if g == 0 and st == 0:
                    dve.wait_ge(osum_ok, batch + 1)
                dve.wait_ge(pv_done, 2 * n + st + 1 + PRIME_PV)
                dve.tensor_copy(oall[:, st, G1 * g:G1 * g + G1, :], o_ps).then_inc(o_ok, 1)

            def row_sums(n):
                dve.wait_ge(o_ok, (n * GPB + 1) * ST + PRIME_O)
                dve.reciprocal(rec[:, :, :], oall[:, :, :, D1]).then_inc(rec_ok, 1)

            def com_low(n):
                com.low(dve, o32[:, :, :, :].rearrange("p s h d -> p s (h d)"), n)

            def update(tile, st, uses):
                dve.wait_ge(projected, uses + 1)
                dve.wait_ge(k_const, 1)
                xt = x[:, tile + st, :]
                dve.scalar_tensor_tensor(xt, pP[:, :], gscale[:, :], xt, ALU.mult, ALU.add).then_inc(pp_ok, 1)

            dve.sem_inc(plo_ok[0], PRIME_LO)
            dve.sem_inc(o_ok, PRIME_O)
            norm.statistics(dve, 0, 0)
            dve.tensor_scalar(gscale[:, :], t["tanh_g"][:, 1:2], 1.0 / (V1_SCALE * W_SCALE), None, ALU.mult)
            dve.memset(kst, 0.0).then_inc(t["kzero"], 1)
            dve.wait_ge(t["kzero"], 2)
            dve.memset(kst[:, :, :, 3 * D1:3 * D1 + 3], M_SCALE).then_inc(k_const, 1)
            ctx_low(0, 0)
            norm.normalise(dve, 0, 0)
            norm.statistics(dve, ST, 1)
            hid.low(dve, norm.xn[:, :, :], 0)
            for n, (kind, st) in enumerate(PREPARE):
                low(kind, 0, st, n, n)
            ctx_low(1, 1)
            norm.normalise(dve, ST, 1)
            hid.low(dve, norm.xn[:, :, :], 1)
            q1_out(0, 0)
            row_max(0, 0, 0)
            row_max(1, 0, 0)
            put_max(0, 0, 0, 0)
            q2_out(0, 0)
            dve.wait_ge(const_set, 1)
            with dve.Fori(0, TRIPS) as it:
                for i in range(NG):
                    par, j = divmod(i, GPB)
                    g, b = it * NG + i, it * PAIRS + par
                    p1, g1, s1 = (i + 1) // GPB % 2, (i + 1) % GPB, (i + 1) % 2
                    if j == 3:
                        hid.low(dve, norm.xn[:, :, :], b + 2)
                    q1_out(s1, g + 1)
                    for k in range(2):
                        kind, st = STEP_USES[j][k]
                        if k == 1:
                            p_low(i % 2, 0, g)
                            row_max(0, s1, g + 1)
                            o_out(0, (i - 1) % GPB, g, b)
                            p_low(i % 2, 1, g)
                            row_max(1, s1, g + 1)
                            put_max(p1, g1, s1, g + 1)
                        if kind == "out":
                            update(((b - 1) * ST + TILES) % TILES, st, use(g, k))
                        else:
                            low(kind, 1 - par, st, use(g, k), high_count(b, j, k))
                    o_out(1, (i - 1) % GPB, g, b)
                    if j == 0:
                        row_sums(b)
                        ctx_low(par, b + 2)
                    if j == 1:
                        norm.statistics(dve, ((b + 2) * ST) % TILES, b + 2)
                    if j == 2:
                        com_low(b)
                        norm.normalise(dve, ((b + 2) * ST) % TILES, b + 2)
                    q2_out(s1, g + 1)
            for st in range(ST):
                o_out(st, GPB - 1, B * GPB, B)
            row_sums(B)
            com_low(B)
            for st in range(ST):
                update((B - 1) * ST, st, use(B * GPB, st))

        @block.tensor
        def _(pe):
            def turn_context():
                for half in range(2):
                    for c in range(ST):
                        ins = pe.transpose(pT_cx[:, half, c * P:(c + 1) * P], cx[:, half, c, :], ident[:, :])
                ins.then_inc(cx_turned, 1)

            def prepare(kind, st):
                if kind == "q":
                    ins = project(pe, pP[:, :], hid.cols, 0, st, w_small[:, 1])
                else:
                    part = 0 if kind == "k" else 1
                    for k, (a, w) in enumerate(PRODUCTS):
                        ins = pe.matmul(pP[:, :], cxT[:, a, st * P:(st + 1) * P], w_small[:, 3, w, part, :],
                                        start=(k == 0), stop=(k == 2))
                ins.then_inc(projected, 1)

            def turn_keys(k):
                for h in range(G1):
                    for c in range(ST):
                        ins = pe.transpose(pT[:, k % 2, h, c * P:(c + 1) * P], kst[:, c, G1 * k + h, :], ident[:, :])
                ins.then_inc(k_turned, 1)

            def q_turn(bank, par, g, done):
                for h in range(G1):
                    for st in range(ST):
                        ins = pe.transpose(pT[:, bank, h, st * P:(st + 1) * P], qst[:, par, st, G1 * g + h, :],
                                           ident[:, :])
                ins.then_inc(done, 1)

            def scores_by_row(slot, par, g, st):
                for h in range(G1):
                    pe.matmul(pS1[:, h, 0:(st + 1) * P], qT1[0:3 * D1, slot, h, st * P:(st + 1) * P],
                              kT[0:3 * D1, par, G1 * g + h, 0:(st + 1) * P], start=True, stop=False)
                    ins = pe.matmul(pS1[:, h, st * P:(st + 1) * P], big_ident[:, :], mask_row[:, :],
                                    start=False, stop=True)
                ins.then_inc(s1_done, 1)

            def scores_by_key(slot, par, g, h, n):
                pe.wait_ge(exp_done, G1 * n + h - 1 + PRIME_EXP)
                key = kT[:, par, G1 * g + h, :]
                pe.matmul(pS2[:, h % 2, 0:S], key[:, 0:P], qT2[:, slot, h, :], start=True, stop=False)
                pe.matmul(pS2[:, h % 2, 0:P], big_ident[:, :], mask_key[:, :], start=False, stop=True)
                pe.matmul(pS2[:, h % 2, S:W], key[:, P:S], qT2[:, slot, h, P:S], start=True, stop=False)
                pe.matmul(pS2[:, h % 2, S:W], big_ident[:, :], mask_key[:, :], start=False,
                          stop=True).then_inc(s2_done, 1)

            def weigh(slot, par, g, st, n):
                if st == 0:
                    for k in range(2):
                        pe.wait_ge(plo_ok[k], 2 * n + PRIME_LO)
                pe.wait_ge(o_ok, 2 * n + st + PRIME_O)
                for h in range(G1):
                    for c, at in ((0, 0),) if st == 0 else ((0, P), (1, S)):
                        for half, probs in enumerate((p_hi, p_lo)):
                            ins = pe.matmul(o_ps[:, h, :], probs[:, slot, h, at:at + P],
                                            vst[:, par, c, G1 * g + h, :],
                                            start=(c == 0 and half == 0), stop=(c == st and half == 1))
                ins.then_inc(pv_done, 1)

            def turn_hid(n):
                pe.wait_ge(hid.lo_ok, n + 1)
                for half in range(2):
                    hid.turn(pe, half, pT[:, half], ident)

            def turn_com(n):
                pe.wait_ge(com.lo_ok, n + 1)
                for half in range(2):
                    com.turn(pe, half, pT[:, half], ident)

            def output(st, n, uses):
                pe.wait_ge(com.cols_ok, 2 * n + 2)
                pe.wait_ge(pp_ok, uses)
                project(pe, pP[:, :], com.cols, 0, st, w_small[:, 2]).then_inc(projected, 1)

            pe.sem_inc(pv_done, PRIME_PV)
            turn_hid(0)
            pe.wait_ge(cxlo_ok, 1)
            pe.wait_ge(hid.cols_ok, 1)
            turn_context()
            pe.wait_ge(hid.cols_ok, 2)
            pe.wait_ge(cx_ok, 1)
            for n, (kind, st) in enumerate(PREPARE):
                if n:
                    pe.wait_ge(pp_ok, n)
                prepare(kind, st)
            pe.wait_ge(dup_ok, 4)
            for k in range(4):
                if k >= 2:
                    pe.wait_ge(kT_ok, k - 1)
                turn_keys(k)
            pe.wait_ge(kT_ok, 4)
            turn_hid(1)
            pe.wait_ge(hid.cols_ok, 3)
            pe.wait_ge(cxlo_ok, 2)
            turn_context()
            pe.wait_ge(cx_ok, 2)
            q_turn(0, 0, 0, t1_done)
            pe.wait_ge(qT1_ok, 1)
            pe.wait_ge(masks_in, 48)
            scores_by_row(0, 0, 0, 0)
            pe.wait_ge(max_ok, 1)
            scores_by_row(0, 0, 0, 1)
            pe.wait_ge(m_ok, 1)
            pe.wait_ge(hid.cols_ok, 4)
            q_turn(1, 0, 0, t2_done)
            pe.wait_ge(const_set, 1)
            with pe.Fori(0, TRIPS) as it:
                for i in range(NG):
                    par, j = divmod(i, GPB)
                    g, b = it * NG + i, it * PAIRS + par
                    p1, g1, s1 = (i + 1) // GPB % 2, (i + 1) % GPB, (i + 1) % 2

                    def use_bank(k):
                        kind, st = STEP_USES[j][k]
                        if kind == "out":
                            output(st, b, use(g, k))
                        else:
                            pe.wait_ge(pp_ok, use(g, k))
                            prepare(kind, st)

                    def weigh_before(st):
                        weigh((i - 1) % 2, (i - 1) // GPB % 2, (i - 1) % GPB, st, g)

                    pe.wait_ge(qT2_ok, g + 1)
                    scores_by_key(i % 2, par, j, 0, g)
                    if j == 0:
                        pe.wait_ge(cx_ok, b + 2)
                    if j == 2:
                        pe.wait_ge(kT_ok, 4 * (b + 1) + 1)
                    if j == 3:
                        pe.wait_ge(com.cols_ok, 2 * b + 1)
                        pe.wait_ge(dup_ok, 4 * (b + 2))
                    q_turn(0, p1, g1, t1_done)
                    use_bank(0)
                    scores_by_key(i % 2, par, j, 1, g)
                    pe.wait_ge(qT1_ok, g + 2)
                    pe.wait_ge(max_ok, 2 * g + 2)
                    scores_by_row(s1, p1, g1, 0)
                    if j == 2:
                        for k in (2, 3):
                            turn_keys(k)
                    if j == 3:
                        turn_hid(b + 2)
                    weigh_before(0)
                    scores_by_key(i % 2, par, j, 2, g)
                    pe.wait_ge(max_ok, 2 * g + 3)
                    scores_by_row(s1, p1, g1, 1)
                    use_bank(1)
                    weigh_before(1)
                    if j == 1:
                        pe.wait_ge(dup_ok, 4 * (b + 1) + 2)
                        for k in (0, 1):
                            turn_keys(k)
                    if j == 2:
                        pe.wait_ge(kT_ok, 4 * (b + 1) + 4)
                        turn_com(b)
                    if j == 3:
                        pe.wait_ge(cxlo_ok, b + 3)
                        pe.wait_ge(hid.cols_ok, 2 * (b + 2) + 1)
                        turn_context()
                    scores_by_key(i % 2, par, j, 3, g)
                    pe.wait_ge(m_ok, g + 2)
                    if j == 1:
                        pe.wait_ge(kT_ok, 4 * (b + 1) + 2)
                    if j == 2:
                        pe.wait_ge(com.cols_ok, 2 * b + 2)
                    if j == 3:
                        pe.wait_ge(hid.cols_ok, 2 * (b + 2) + 2)
                    q_turn(1, p1, g1, t2_done)
            for st in range(ST):
                weigh(1, 1, GPB - 1, st, B * GPB)
            pe.wait_ge(qT2_ok, B * GPB + 1)
            pe.wait_ge(qT1_ok, B * GPB + 1)
            turn_com(B)
            for st in range(ST):
                output(st, B, use(B * GPB, st))


PREPARE = (("k", 0), ("v", 0), ("k", 1), ("v", 1), ("q", 0), ("q", 1))


FF = 2048
FM = FF // E
FC = FF // P
H_SCALE = 256.0


def phase_feed_forward(nc, mem, t, out_d):
    x, stage, ident, w_gu, w_d = t["x"], t["stage"], t["ident"], t["w_e"], t["w_d"]
    TRIPS = B // PAIRS
    UNITS = FC // 2
    MATS = 3 * FM

    def sb(name, shape, dt):
        return mem.enter_context(nc.sbuf_tensor("f_" + name, shape, dt))

    def sem(name):
        return mem.enter_context(nc.semaphore("f_" + name))

    norm = Norm(nc, mem, "f", t)
    hid = Split(nc, mem, "f_hid", PAIRS)
    sg = sb("sg", [P, 2, 2, S], F32)
    h32 = sb("h32", [P, 2, 2, S], F32)
    hp = t["w_small"][:, 0:2].rearrange("p m a k n -> p (m a k n)").rearrange("p (a c s) -> p a c s", a=2, c=FC)
    gscale = sb("gscale", [P, 1], F32)

    pG = mem.enter_context(nc.psum_tensor("f_pG", [P, 2, 2, S], F32))
    pU = mem.enter_context(nc.psum_tensor("f_pU", [P, 2, 2, S], F32))
    pD = mem.enter_context(nc.psum_tensor("f_pD", [P, ST, E], F32))
    pT = mem.enter_context(nc.psum_tensor("f_pT", [P, 2, KC, S], F16))

    stage_in = [sem(f"stage{k}_in") for k in range(2)]
    whi_ok, wlo_ok, gs_ok = sem("whi_ok"), sem("wlo_ok"), sem("gs_ok")
    gu_done, silu_done, h_ok, hhi_ok, hlo_ok = sem("gu_done"), sem("silu_done"), sem("h_ok"), sem("hhi_ok"), sem("hlo_ok")
    down_done, x_ok, sent = sem("down_done"), sem("x_ok"), sem("sent")
    PRIME = 2

    def pair_of(m):
        return w_gu[:, m] if m < 2 * FM else w_d[:, m - 2 * FM]

    with nc.Block() as block:

        @block.sync
        def _(sp):
            for m in range(MATS):
                if m >= 2:
                    sp.wait_ge(wlo_ok, m - 1)
                src = t["gu_d"][:, m] if m < 2 * FM else t["down_d"][:, m - 2 * FM]
                sp.dma_start(stage[:, m % 2], src).then_inc(stage_in[m % 2], 16)
            with sp.Fori(0, B) as b:
                sp.wait_ge(x_ok, b * ST + ST + PRIME)
                sp.dma_start(out_d[:, bass.ds(b * ST, ST), :], x[:, bass.ds(b * ST, ST), :]).then_inc(sent, 16)
            sp.wait_ge(sent, 16 * B)

        @block.gpsimd
        def _(pool):
            def h_low(slot, u, n):
                pool.wait_ge(hhi_ok, n * UNITS + u + 1)
                pool.tensor_tensor(hp[:, 1, 2 * u:2 * u + 2, :], h32[:, slot], hp[:, 0, 2 * u:2 * u + 2, :],
                                   ALU.subtract).then_inc(hlo_ok, 1)

            pool.sem_inc(hlo_ok, PRIME)
            norm.deviation(pool, 0)
            with pool.Fori(0, TRIPS) as it:
                for par in range(PAIRS):
                    b = it * PAIRS + par
                    for u in range(UNITS):
                        h_low(u % 2, u, b)
                        if u == 0:
                            norm.deviation(pool, b + 1)

        @block.scalar
        def _(act):
            def silu(slot, u, n):
                k = n * UNITS + u
                act.wait_ge(gu_done, k + 1)
                act.wait_ge(h_ok, k - 1 + PRIME)
                act.activation(sg[:, slot], pG[:, slot], ACT.Silu,
                               scale=1.0 / (X_SCALE * W_SCALE)).then_inc(silu_done, 1)

            def h_high(slot, u, n):
                act.wait_ge(h_ok, n * UNITS + u + 1 + PRIME)
                if u == 0:
                    act.wait_ge(down_done, n * ST + PRIME)
                act.activation(hp[:, 0, 2 * u:2 * u + 2, :], h32[:, slot], ACT.Copy).then_inc(hhi_ok, 1)

            def hid_high(n):
                act.wait_ge(norm.xn_ok, n + 1)
                hid.high(act, norm.xn[:, :, :])

            act.sem_inc(silu_done, PRIME)
            for m in range(MATS):
                act.wait_ge(stage_in[m % 2], 16 * (m // 2 + 1))
                act.activation(pair_of(m)[:, 0], stage[:, m % 2], ACT.Copy, scale=W_SCALE).then_inc(whi_ok, 1)
                if m == 0:
                    hid_high(0)
                if m == 1:
                    for half in range(2):
                        hid.out(act, half, pT[:, half], 0, 0)
            with act.Fori(0, TRIPS) as it:
                for par in range(PAIRS):
                    b = it * PAIRS + par
                    for u in range(UNITS):
                        silu(u % 2, u, b)
                        h_high(u % 2, u, b)
                        if u == 1:
                            hid_high(b + 1)
                        if u == 4:
                            for half in range(2):
                                hid.out(act, half, pT[:, half], 1 - par, b + 1)

        @block.vector
        def _(dve):
            def gated(slot, u, n):
                k = n * UNITS + u
                dve.wait_ge(silu_done, k + 1 + PRIME)
                dve.wait_ge(hlo_ok, k - 1 + PRIME)
                dve.scalar_tensor_tensor(h32[:, slot], pU[:, slot], H_SCALE / (X_SCALE * W_SCALE), sg[:, slot],
                                         ALU.mult, ALU.mult).then_inc(h_ok, 1)

            def update(tile, st, n):
                dve.wait_ge(down_done, n * ST + st + 1 + PRIME)
                dve.wait_ge(gs_ok, 1)
                xt = x[:, tile + st, :]
                dve.scalar_tensor_tensor(xt, pD[:, st], gscale[:, :], xt, ALU.mult, ALU.add).then_inc(x_ok, 1)

            dve.sem_inc(h_ok, PRIME)
            dve.sem_inc(x_ok, PRIME)
            norm.statistics(dve, 0, 0)
            dve.tensor_scalar(gscale[:, :], t["tanh_g"][:, 3:4], 1.0 / (H_SCALE * W_SCALE), None,
                              ALU.mult).then_inc(gs_ok, 1)
            norm.normalise(dve, 0, 0)
            for m in range(MATS):
                dve.wait_ge(whi_ok, m + 1)
                dve.scalar_tensor_tensor(pair_of(m)[:, 1], stage[:, m % 2], W_SCALE, pair_of(m)[:, 0],
                                         ALU.mult, ALU.subtract).then_inc(wlo_ok, 1)
                if m == 0:
                    hid.low(dve, norm.xn[:, :, :], 0)
            with dve.Fori(0, TRIPS) as it:
                for par in range(PAIRS):
                    b = it * PAIRS + par
                    ahead = ((b + 1) * ST) % TILES
                    for u in range(UNITS):
                        gated(u % 2, u, b)
                        if u == 0:
                            norm.statistics(dve, ahead, b + 1)
                            norm.normalise(dve, ahead, b + 1)
                        if u == 2:
                            hid.low(dve, norm.xn[:, :, :], b + 1)
                    for st in range(ST):
                        update(b * ST, st, b)

        @block.tensor
        def _(pe):
            def gate_up(par, slot, u, n):
                k = n * UNITS + u
                pe.wait_ge(silu_done, k - 1 + PRIME)
                pe.wait_ge(h_ok, k - 1 + PRIME)
                for psum, part in ((pG, 0), (pU, FM)):
                    for c in range(2):
                        chunk = 2 * u + c
                        m, at = part + chunk // KC, chunk % KC * P
                        i = 0
                        for kc in range(KC):
                            for a, w in PRODUCTS:
                                ins = pe.matmul(psum[:, slot, c], w_gu[:, m, w, kc, at:at + P],
                                                hid.cols[:, par, a, kc, :], start=(i == 0),
                                                stop=(i == KC * len(PRODUCTS) - 1))
                                i += 1
                ins.then_inc(gu_done, 1)

            def down(st, n):
                pe.wait_ge(x_ok, n * ST + st - 1 + PRIME)
                i, last = 0, FC * len(PRODUCTS) - 1
                for chunk in range(FC):
                    for a, w in PRODUCTS:
                        ins = pe.matmul(pD[:, st], hp[:, a, chunk, st * P:(st + 1) * P],
                                        w_d[:, chunk // KC, w, chunk % KC, :], start=(i == 0), stop=(i == last))
                        i += 1
                ins.then_inc(down_done, 1)

            pe.sem_inc(down_done, PRIME)
            pe.wait_ge(hid.lo_ok, 1)
            for half in range(2):
                hid.turn(pe, half, pT[:, half], ident)
            with pe.Fori(0, TRIPS) as it:
                for par in range(PAIRS):
                    b = it * PAIRS + par
                    pe.wait_ge(hid.cols_ok, 2 * b + 2)
                    pe.wait_ge(wlo_ok, MATS)
                    for u in range(UNITS):
                        gate_up(par, u % 2, u, b)
                        if u == 3:
                            pe.wait_ge(hid.lo_ok, b + 2)
                            for half in range(2):
                                hid.turn(pe, half, pT[:, half], ident)
                    pe.wait_ge(hlo_ok, (b + 1) * UNITS + PRIME)
                    for st in range(ST):
                        down(st, b)


def program(nc, a, out, debug_phase=None):
    with ExitStack() as mem:
        def sb(name, shape, dt):
            return mem.enter_context(nc.sbuf_tensor(name, shape, dt))

        def sem(name):
            return mem.enter_context(nc.semaphore(name))

        t = {}
        t["x"] = x = sb("x", [P, TILES, E], F32)
        t["w_e"] = sb("w_e", [P, NE, 2, KC, E], F16)
        t["stage"] = sb("stage", [P, 2, KC, E], F32)
        t["ident"] = sb("ident", [P, P], F16)
        t["g_raw"] = sb("g_raw", [P, 4], F32)
        t["norm_consts"] = sb("norm_consts", [P, len(NORM_CONSTS)], F32)
        t["tanh_g"] = sb("tanh_g", [P, 4], F32)
        for name in ("ident_in", "gates_in", "gates_ok", "kzero", "kconst"):
            t[name] = sem(name)
        t["ctx_d"] = a["ctx_512"].rearrange("b (c p) l -> p b c l", p=P)
        t["x_d"] = a["x"].rearrange("b (s p) e -> p (b s) e", p=P)
        t["expert_d"] = a["L0_ffn_expert_w"].rearrange("e (k p) d -> p e k d", p=P)
        nc.scalar.dma_start(t["ident"][:, :], a["ident"]).then_inc(t["ident_in"], 16)
        nc.scalar.dma_start(t["g_raw"][:, 0:2], a["g_xattn"].partition_broadcast(P)).then_inc(t["gates_in"], 16)
        nc.scalar.dma_start(t["g_raw"][:, 2:4], a["g_ffn"].partition_broadcast(P)).then_inc(t["gates_in"], 16)
        t["sel_d"], t["router_d"] = a["sel"], a["L0_ffn_router_w"].rearrange("(k p) e -> p k e", p=P)
        t["ramp_d"] = a["ramp"]
        t["expert_b_d"] = a["L0_ffn_expert_b"]
        t["out_b_d"] = a["L0_ffn_out_b"].rearrange("(a n) -> a n", a=1)
        t["router_b_d"] = a["L0_ffn_router_b"].rearrange("(a n) -> a n", a=1)
        t["small_d"] = a["small"].rearrange("m (k p) n -> p m k n", p=P)
        for name in ("big_ident", "mask_row", "mask_key"):
            t[name + "_d"] = a[name]
        t["gu_d"] = a["gate_up"].rearrange("(k p) (m n) -> p m k n", p=P, n=E)
        t["down_d"] = a["down"].rearrange("(m k p) n -> p m k n", k=KC, p=P)
        out_sent = sem("out_sent")
        with ExitStack() as pm:
            phase_attention0(nc, pm, t)
        if debug_phase is None or debug_phase > 1:
            t["w_small"] = sb("w_small", [P, 4, 2, KC, E], F16)
            with ExitStack() as pm:
                phase_experts(nc, pm, t)
        if debug_phase is None or debug_phase > 2:
            with ExitStack() as pm:
                phase_attention1(nc, pm, t)
        if debug_phase is None or debug_phase > 3:
            t["w_d"] = sb("w_d", [P, FM, 2, KC, E], F16)
            with ExitStack() as pm:
                phase_feed_forward(nc, pm, t, out.rearrange("b (s p) e -> p (b s) e", p=P))
            return
        if debug_phase:
            with nc.Block() as block:
                @block.sync
                def _(sp):
                    sp.dma_start(out.rearrange("b (s p) e -> p (b s) e", p=P), x[:, :, :]).then_inc(out_sent, 16)
                    sp.wait_ge(out_sent, 16)
            return


def kernel(_debug=None, **inputs):
    import numpy as np
    import concourse.bacc as bacc
    from concourse.bass_utils import run_bass_kernel_spmd

    nc = bacc.Bacc("TRN2", target_bir_lowering=False, num_devices=1)
    arrays = {k: np.ascontiguousarray(v) for k, v in inputs.items()}
    arrays["ident"] = np.eye(P, dtype=np.float16)
    arrays["ramp"] = np.arange(NE, 0, -1, dtype=np.float32)
    sel = np.zeros((P, BIAS_ROWS, P), np.float16)
    for r in range(BIAS_ROWS):
        sel[[r, BIAS_LOW + r], r, :] = C_SCALE if r == BIAS_OUT else X_SCALE
    arrays["sel"] = sel
    small = np.zeros((4, E, E), np.float32)
    small[0] = arrays.pop("L0_ffn_out_w")
    small[1] = arrays.pop("L1_xattn_Wq").T
    small[2] = arrays.pop("L1_xattn_Wout").T
    small[3].reshape(KC, P, E)[0:2] = arrays.pop("L1_xattn_Wkv_expand").T.reshape(P, 2, E).transpose(1, 0, 2)
    arrays["small"] = small
    arrays["gate_up"] = np.ascontiguousarray(arrays.pop("L1_ffn_w_gate_up").T)
    arrays["down"] = np.ascontiguousarray(arrays.pop("L1_ffn_w_down").T)
    arrays["big_ident"] = (MASK * np.eye(P)).astype(np.float16)
    later = np.triu(np.ones((P, P)), 1)
    arrays["mask_row"] = (-MASK * later).astype(np.float16)
    arrays["mask_key"] = (-MASK * later.T).astype(np.float16)
    aps = {k: nc.dram_tensor("in_" + k, v.shape, mybir.dt.from_np(v.dtype), kind="ExternalInput").ap()
           for k, v in arrays.items()}
    out = nc.dram_tensor("out", (B, S, E), F32, kind="ExternalOutput").ap()
    program(nc, aps, out, _debug)
    r = run_bass_kernel_spmd(nc, [{"in_" + k: v for k, v in arrays.items()}], core_ids=[0])
    return r.results[0]["out"]
```

```python
from contextlib import ExitStack

import concourse.bass as bass
from concourse import mybir

P = 128
F32 = mybir.dt.float32
F16 = mybir.dt.float16
ALU = mybir.AluOpType
ACT = mybir.ActivationFunctionType
AX = mybir.AxisListType

B, S, E, L = 8, 256, 512, 128
TILES = B * S // P
ST = S // P
KC = E // P
EPS = 1e-5

X_SCALE = 512.0
W_SCALE = 256.0
M_SCALE = 4096.0
LIFT0 = 887.0

H0, KV0, D0 = 32, 8, 16
G0 = H0 // KV0
R0 = 64
EXTRA0 = R0 + 3 * D0
V0 = D0 + 1
PAIRS = 2
X_LOAD = 7


class Norm:

    STEPS = 6

    def __init__(self, nc, mem, tag, t):
        def sb(name, shape, dt):
            return mem.enter_context(nc.sbuf_tensor(f"{tag}_{name}", shape, dt))

        def sem(name):
            return mem.enter_context(nc.semaphore(f"{tag}_{name}"))

        self.x, self.consts = t["x"], t["norm_consts"]
        self.bn = sb("bn", [P, ST, 6], F32)
        self.tmp = sb("norm_tmp", [P, 4, ST], F32)
        self.mean = sb("mean", [P, ST], F32)
        self.rstd = sb("rstd", [P, ST], F32)
        self.xn = sb("xn", [P, ST, E], F32)
        self.bn_ok, self.chain, self.xn_ok = sem("bn_ok"), sem("norm_chain"), sem("xn_ok")

    def const(self, k):
        return self.consts[:, k:k + 1].to_broadcast([P, ST])

    def statistics(self, dve, tile, n):
        for st in range(ST):
            ins = dve.bn_stats(self.bn[:, st, :], self.x[:, tile + st, :])
        ins.then_inc(self.bn_ok, 1)

    def deviation(self, pool, n):
        bn, tmp, chain, at = self.bn, self.tmp, self.chain, self.STEPS * n
        pool.wait_ge(self.bn_ok, n + 1)
        pool.tensor_tensor(self.mean[:, :], bn[:, :, 1], bn[:, :, 4], ALU.add)
        pool.tensor_tensor(tmp[:, 0], bn[:, :, 1], bn[:, :, 4], ALU.subtract)
        pool.tensor_tensor(tmp[:, 1], bn[:, :, 2], bn[:, :, 5], ALU.add).then_inc(chain, 1)
        pool.wait_ge(chain, at + 1)
        pool.tensor_tensor(self.mean[:, :], self.mean[:, :], self.const(0), ALU.mult)
        pool.tensor_tensor(tmp[:, 2], tmp[:, 0], tmp[:, 0], ALU.mult)
        pool.tensor_tensor(tmp[:, 1], tmp[:, 1], self.const(1), ALU.mult).then_inc(chain, 1)
        pool.wait_ge(chain, at + 2)
        pool.tensor_tensor(tmp[:, 3], tmp[:, 1], tmp[:, 2], ALU.add).then_inc(chain, 1)
        pool.wait_ge(chain, at + 3)
        pool.tensor_tensor(tmp[:, 0], tmp[:, 3], self.const(2), ALU.add).then_inc(chain, 1)
        pool.wait_ge(chain, at + 4)
        pool.tensor_tensor(tmp[:, 1], tmp[:, 0], self.const(3), ALU.pow).then_inc(chain, 1)
        pool.wait_ge(chain, at + 5)
        pool.tensor_tensor(self.rstd[:, :], tmp[:, 1], self.const(4), ALU.mult).then_inc(chain, 1)

    def normalise(self, dve, tile, n):
        dve.wait_ge(self.chain, self.STEPS * (n + 1))
        for st in range(ST):
            ins = dve.tensor_scalar(self.xn[:, st, :], self.x[:, tile + st, :], self.mean[:, st:st + 1],
                                    self.rstd[:, st:st + 1], ALU.subtract, ALU.mult)
        ins.then_inc(self.xn_ok, 1)


class Split:

    def __init__(self, nc, mem, tag, slots):
        def sem(name):
            return mem.enter_context(nc.semaphore(f"{tag}_{name}"))

        self.rows = mem.enter_context(nc.sbuf_tensor(f"{tag}_rows", [P, 2, ST, E], F16))
        self.cols = mem.enter_context(nc.sbuf_tensor(f"{tag}_cols", [P, slots, 2, KC, S], F16))
        self.hi_ok, self.lo_ok = sem("hi_ok"), sem("lo_ok")
        self.turned, self.cols_ok = sem("turned"), sem("cols_ok")

    def high(self, act, src):
        act.activation(self.rows[:, 0], src, ACT.Copy).then_inc(self.hi_ok, 1)

    def low(self, dve, src, n):
        dve.wait_ge(self.hi_ok, n + 1)
        dve.tensor_tensor(self.rows[:, 1], src, self.rows[:, 0], ALU.subtract).then_inc(self.lo_ok, 1)

    def turn(self, pe, half, psum, ident):
        for k in range(KC):
            for st in range(ST):
                ins = pe.transpose(psum[:, k, st * P:(st + 1) * P], self.rows[:, half, st, k * P:(k + 1) * P],
                                   ident[:, :])
        ins.then_inc(self.turned, 1)

    def out(self, act, half, psum, par, n):
        act.wait_ge(self.turned, 2 * n + half + 1)
        act.activation(self.cols[:, par, half], psum, ACT.Copy).then_inc(self.cols_ok, 1)


PRODUCTS = ((0, 0), (1, 0), (0, 1))


def project(pe, psum, cols, par, st, weights, k_chunks=KC, more=False):
    last = len(PRODUCTS) * k_chunks - 1
    i = 0
    for k in range(k_chunks):
        for a, b in PRODUCTS:
            ins = pe.matmul(psum, cols[:, par, a, k, st * P:(st + 1) * P], weights[:, b, k, :],
                            start=(i == 0), stop=(i == last and not more))
            i += 1
    return ins


NORM_CONSTS = (0.5, 4.0 / E, 4.0 * EPS, -0.5, 2.0 * X_SCALE)


def phase_attention0(nc, mem, t):
    x, w_e, stage, ident, gates = t["x"], t["w_e"], t["stage"], t["ident"], t["tanh_g"]
    ctx_d, x_d, expert_d = t["ctx_d"], t["x_d"], t["expert_d"]
    GPB = KV0
    NG = PAIRS * GPB
    TRIPS = B // PAIRS
    SLOTS = 4
    LAG = 2

    def sb(name, shape, dt):
        return mem.enter_context(nc.sbuf_tensor("a0_" + name, shape, dt))

    def sem(name):
        return mem.enter_context(nc.semaphore("a0_" + name))

    wscale = sb("wscale", [P, 1], F32)
    ctx = sb("ctx", [P, PAIRS, ST, L], F32)
    norm = Norm(nc, mem, "a0", t)
    xn = norm.xn
    qst = sb("qst", [P, PAIRS, ST, H0, R0], F16)
    kst = sb("kst", [P, ST, KV0, 2, 2 * R0], F16)
    kT = sb("kT", [P, 2, KV0, S], F16)
    extras = qst[:, :, :, :, :].rearrange("p a s (m r) c -> p a s m (r c)", r=2)
    extras = extras[:, :, :, :, EXTRA0:EXTRA0 + 6].rearrange("p a s (g j) (r k) -> p a s g j r k", j=2, r=2)
    vst = sb("vst", [P, PAIRS, ST, KV0, 2, V0], F16)
    qT1 = sb("qT1", [P, 2, 2, S], F16)
    qT2 = sb("qT2", [P, 2, 2, S], F16)
    p32 = sb("p32", [P, ST, 2, 2, S], F32)
    p_hi = sb("p_hi", [P, SLOTS * ST, 2, 2, S], F16)
    p_lo = sb("p_lo", [P, SLOTS * ST, 2, 2, S], F16)
    negm = sb("negm", [P, 2, ST, 2, 2], F32)
    oall = sb("oall", [P, PAIRS, ST, H0, V0], F32)
    rec = sb("rec", [P, ST, H0], F32)
    v256 = sb("v256", [P, ST * KV0, D0], F32)

    pS2 = mem.enter_context(nc.psum_tensor("a0_pS2", [P, 2, 2, 2, S], F32))
    pS1 = mem.enter_context(nc.psum_tensor("a0_pS1", [P, 2, 2, S], F32))
    pT = mem.enter_context(nc.psum_tensor("a0_pT", [P, 4, S], F16))
    pO = mem.enter_context(nc.psum_tensor("a0_pO", [P, 512], F32))
    o_ps = pO[:, 0:ST * G0 * V0].rearrange("p (s h d) -> p s h d", s=ST, h=G0)

    x0_in, x_in = sem("x0_in"), sem("x_in")
    ctx_in = [sem(f"ctx{par}_in") for par in range(PAIRS)]
    stage_in = [sem(f"stage{par}_in") for par in range(PAIRS)]
    const_set, qzero = sem("const_set"), sem("qzero")
    v_ok = sem("v_ok")
    qhi_ok, qlo_ok, khi_ok, klo_ok = sem("qhi_ok"), sem("qlo_ok"), sem("khi_ok"), sem("klo_ok")
    t1_done, t2_done, tk_done = sem("t1_done"), sem("t2_done"), sem("tk_done")
    qT1_ok, qT2_ok, kT_ok = sem("qT1_ok"), sem("qT2_ok"), sem("kT_ok")
    s1_done, max_ok, mhi_ok, m_ok = sem("s1_done"), sem("max_ok"), sem("mhi_ok"), sem("m_ok")
    s2_done, exp_done = sem("s2_done"), sem("exp_done")
    plo_ok = [sem(f"plo{c}_ok") for c in range(ST)]
    v256_ok, vhi_ok, zeroed = sem("v256_ok"), sem("vhi_ok"), sem("zeroed")
    pv_done, o_ok = sem("pv_done"), sem("o_ok")
    rec0_ok, rec_ok, inc_ok, x_ok = sem("rec0_ok"), sem("rec_ok"), sem("inc_ok"), sem("x_ok")
    lag_set = sem("lag_set")
    whi_ok, wscaled, wlo_ok = sem("whi_ok"), sem("wscaled"), sem("wlo_ok")
    PRIME_EXP, PRIME_PV, PRIME_O, PRIME_INC, PRIME_W, PRIME_LO, PRIME_X = 2, LAG, 1, 1, 2, LAG, 1

    with nc.Block() as block:

        @block.sync
        def _(sp):
            def load_ctx(b, par):
                sp.dma_start(ctx[:, par], ctx_d[:, b]).then_inc(ctx_in[par], 16)

            load_ctx(0, 0)
            sp.dma_start(x[:, 0:ST, :], x_d[:, 0:ST, :]).then_inc(x0_in, 16)
            load_ctx(1, 1)
            for n in range(ST, TILES, X_LOAD):
                sp.dma_start(x[:, n:n + X_LOAD, :], x_d[:, n:n + X_LOAD, :]).then_inc(x_in, 16)
            with sp.Fori(0, TRIPS) as it:
                for par in range(PAIRS):
                    sp.wait_ge(wlo_ok, it * PAIRS + par + 1)
                    sp.dma_start(stage[:, par], expert_d[:, it * PAIRS + par]).then_inc(stage_in[par], 16)
                for par in range(PAIRS):
                    sp.wait_ge(klo_ok, it * PAIRS + par + 1)
                    sp.wait_ge(v_ok, it * PAIRS + par + 1)
                    load_ctx((it * PAIRS + PAIRS + par) % B, par)
            for par in range(PAIRS):
                sp.wait_ge(ctx_in[par], 16 * (TRIPS + 1))

        @block.gpsimd
        def _(pool):
            def values(par, n, loads):
                pool.wait_ge(ctx_in[par], 16 * loads)
                pool.wait_ge(pv_done, (n - 1) * GPB + LAG + PRIME_PV)
                pool.wait_ge(const_set, 5)
                v_high_low(par, n)

            def v_high_low(par, n):
                src = ctx[:, par].rearrange("p c (g d) -> p (c g) d", d=D0)
                dst = vst[:, par].rearrange("p c g a d -> p (c g) a d")
                scale = wscale[:, :].unsqueeze(2).to_broadcast([P, ST * KV0, D0])
                pool.tensor_tensor(v256[:, :, :], src, scale, ALU.mult).then_inc(v256_ok, 1)
                pool.tensor_tensor(dst[:, :, 0, 0:D0], src, scale, ALU.mult).then_inc(vhi_ok, 1)
                pool.wait_ge(v256_ok, n + 1)
                pool.wait_ge(vhi_ok, n + 1)
                pool.tensor_tensor(dst[:, :, 1, 0:D0], v256[:, :, :], dst[:, :, 0, 0:D0],
                                   ALU.subtract).then_inc(v_ok, 1)

            def p_low(slot, n):
                pool.wait_ge(exp_done, n * 2 + 2 + PRIME_EXP)
                pool.tensor_tensor(p_lo[:, 2 * slot + 1], p32[:, 1], p_hi[:, 2 * slot + 1],
                                   ALU.subtract).then_inc(plo_ok[1], 1)

            def divide(par, n):
                pool.wait_ge(rec_ok, n + 1)
                ob = oall[:, par, :, :, 0:D0]
                pool.tensor_tensor(ob, ob, rec[:, :, :].unsqueeze(3).to_broadcast([P, ST, H0, D0]),
                                   ALU.mult).then_inc(inc_ok, 1)

            def add_to_x(par, tile, n):
                pool.wait_ge(inc_ok, n + 1 + PRIME_INC)
                pool.wait_ge(x_in, 16 * (TILES - ST) // X_LOAD)
                xb = x[:, bass.ds(tile, ST), :].rearrange("p s (h d) -> p s h d", d=D0)
                pool.tensor_tensor(xb, xb, oall[:, par, :, :, 0:D0], ALU.add).then_inc(x_ok, 1)

            def split_low(par, e, n, k):
                pool.wait_ge(whi_ok, 2 * n + k // 2 + 1)
                pool.tensor_tensor(stage[:, par, k], stage[:, par, k], wscale[:, :].to_broadcast([P, E]),
                                   ALU.mult).then_inc(wscaled, 1)
                pool.wait_ge(wscaled, KC * n + k + 1)
                ins = pool.tensor_tensor(w_e[:, e, 1, k], stage[:, par, k], w_e[:, e, 0, k], ALU.subtract)
                if k == KC - 1:
                    ins.then_inc(wlo_ok, 1)

            pool.sem_inc(wlo_ok, PRIME_W)
            pool.sem_inc(inc_ok, PRIME_INC)
            pool.sem_inc(x_ok, PRIME_X)
            pool.sem_inc(plo_ok[1], PRIME_LO)
            for k, value in enumerate(NORM_CONSTS):
                ins = pool.memset(norm.consts[:, k:k + 1], value)
            ins.then_inc(const_set, 1)
            pool.memset(wscale[:, :], W_SCALE).then_inc(const_set, 1)
            pool.memset(vst[:, :, :, :, :, :], 0.0).then_inc(zeroed, 1)
            pool.wait_ge(zeroed, 1)
            pool.memset(vst[:, :, :, :, 0, D0:D0 + 1], 1.0).then_inc(const_set, 1)
            pool.memset(qst[:, :, :, :, :], 0.0).then_inc(qzero, 1)
            pool.wait_ge(qzero, 1)
            pool.memset(extras[:, :, :, :, :, :, 2], LIFT0).then_inc(const_set, 2)
            pool.wait_ge(const_set, 5)
            norm.deviation(pool, 0)
            pool.wait_ge(ctx_in[0], 16)
            v_high_low(0, 0)
            pool.memset(p_hi[:, (SLOTS - LAG) * ST:], 1.0)
            pool.memset(p_lo[:, (SLOTS - LAG) * ST:], 0.0)
            pool.memset(oall[:, :, :, :, 0:D0], 0.0)
            pool.memset(oall[:, :, :, :, D0:D0 + 1], 1.0).then_inc(lag_set, 1)
            with pool.Fori(0, TRIPS) as it:
                for i in range(NG):
                    par, j = divmod(i, GPB)
                    g, b = it * NG + i, it * PAIRS + par
                    if j == 0:
                        norm.deviation(pool, b + 1)
                    p_low(i % SLOTS, g)
                    if j in (1, 3, 6, 7):
                        split_low(par, b, b, (1, 3, 6, 7).index(j))
                    if j == 2:
                        divide(1 - par, b)
                    if j == 4:
                        values(1 - par, b + 1, it + 1 + par)
                    if j == 5:
                        add_to_x(1 - par, ((b - 1) * ST + TILES) % TILES, b)
            divide(1, B)
            add_to_x(1, (B - 1) * ST, B)

        @block.scalar
        def _(act):
            def q_high(par, n):
                act.wait_ge(norm.xn_ok, n + 1)
                for st in range(ST):
                    for a in (0, 2):
                        ins = act.activation(qst[:, par, st, :, a * D0:(a + 1) * D0],
                                             xn[:, st, :].rearrange("p (h d) -> p h d", d=D0), ACT.Copy)
                ins.then_inc(qhi_ok, 1)

            def k_high(par, n, loads):
                act.wait_ge(ctx_in[par], 16 * loads)
                src = ctx[:, par].rearrange("p c (g d) -> p c g d", d=D0)
                for r in range(2):
                    for base in (R0 * r, R0 * r + D0):
                        ins = act.activation(kst[:, :, :, r, base:base + D0], src, ACT.Copy, scale=W_SCALE)
                ins.then_inc(khi_ok, 1)

            def k_out(half, r, n):
                act.wait_ge(tk_done, n + 1)
                act.activation(kT[:, r, 4 * half:4 * half + 4, :], pT[:, :, :], ACT.Copy).then_inc(kT_ok, 1)

            def q2_out(slot, n):
                act.wait_ge(t2_done, n + 1)
                act.activation(qT2[:, slot], pT[:, 0:2, :], ACT.Copy).then_inc(qT2_ok, 1)

            def exps(slot, c, n):
                act.wait_ge(s2_done, n * 2 + c + 1)
                if c == 0:
                    act.wait_ge(pv_done, n - SLOTS + 1 + LAG + PRIME_PV)
                scale = D0 ** -0.5 / (X_SCALE * W_SCALE)
                act.activation(p_hi[:, 2 * slot + c], pS2[:, c], ACT.Exp, scale=scale)
                act.wait_ge(plo_ok[c], n + PRIME_LO)
                act.activation(p32[:, c], pS2[:, c], ACT.Exp, scale=scale).then_inc(exp_done, 1)

            def split_high(par, e, it, half):
                act.wait_ge(stage_in[par], it * 16 + 16)
                act.wait_ge(const_set, 5)
                rows = slice(2 * half, 2 * half + 2)
                act.activation(w_e[:, e, 0, rows], stage[:, par, rows], ACT.Copy,
                               scale=W_SCALE).then_inc(whi_ok, 1)

            act.sem_inc(exp_done, PRIME_EXP)
            act.wait_ge(const_set, 5)
            act.wait_ge(t["gates_in"], 32)
            act.activation(gates[:, :], t["g_raw"][:, :], ACT.Tanh).then_inc(t["gates_ok"], 1)
            act.wait_ge(t["kconst"], 1)
            k_high(0, 0, 1)
            q_high(0, 0)
            k_out(0, 0, 0)
            k_out(0, 1, 1)
            q2_out(0, 0)
            act.wait_ge(lag_set, 1)
            with act.Fori(0, TRIPS) as it:
                for i in range(NG):
                    par, j = divmod(i, GPB)
                    g, b = it * NG + i, it * PAIRS + par
                    exps(i % SLOTS, 0, g)
                    q2_out((i + 1) % 2, g + 1)
                    exps(i % SLOTS, 1, g)
                    if j in (0, 1):
                        k_out(1, j, 4 * b + 2 + j)
                    if j == 0:
                        split_high(par, b, it, 0)
                    if j == 1:
                        k_high(1 - par, b + 1, it + 1 + par)
                    if j == 2:
                        q_high(1 - par, b + 1)
                    if j in (4, 5):
                        k_out(0, j - 4, 4 * (b + 1) + j - 4)
                    if j == 5:
                        split_high(par, b, it, 1)

        @block.vector
        def _(dve):
            def q_low(par, n):
                dve.wait_ge(qhi_ok, n + 1)
                for st in range(ST):
                    ins = dve.tensor_tensor(qst[:, par, st, :, D0:2 * D0],
                                            xn[:, st, :].rearrange("p (h d) -> p h d", d=D0),
                                            qst[:, par, st, :, 0:D0], ALU.subtract)
                ins.then_inc(qlo_ok, 1)

            def k_low(par, n):
                dve.wait_ge(khi_ok, n + 1)
                src = ctx[:, par].rearrange("p c (g d) -> p (c g) d", d=D0)
                for r in range(2):
                    flat = kst[:, :, :, r, :].rearrange("p c g n -> p (c g) n")
                    base = R0 * r
                    ins = dve.scalar_tensor_tensor(flat[:, :, base + 2 * D0:base + 3 * D0], src, W_SCALE,
                                                   flat[:, :, base:base + D0], ALU.mult, ALU.subtract)
                ins.then_inc(klo_ok, 1)

            def p_low(slot, n):
                dve.wait_ge(exp_done, n * 2 + 1 + PRIME_EXP)
                dve.tensor_tensor(p_lo[:, 2 * slot], p32[:, 0], p_hi[:, 2 * slot],
                                  ALU.subtract).then_inc(plo_ok[0], 1)

            def q1_out(slot, n):
                dve.wait_ge(t1_done, n + 1)
                dve.tensor_copy(qT1[:, slot], pT[:, 0:2, :]).then_inc(qT1_ok, 1)

            def row_max(st, n, slot):
                for r in range(2):
                    dve.wait_ge(s1_done, n * 4 + 2 * st + r + 1)
                    dve.tensor_reduce(negm[:, slot, st, r], pS1[:, r], AX.X, ALU.max, negate=True).then_inc(max_ok, 1)

            def put_max(par, g, n, slot):
                dve.wait_ge(max_ok, n * 4 + 4)
                for st in range(ST):
                    to = extras[:, par, st, g, :, :, 0].rearrange("p j r -> p r j")
                    ins = dve.tensor_scalar(to, negm[:, slot, st], 1.0 / M_SCALE, None, ALU.mult)
                ins.then_inc(mhi_ok, 1)
                dve.wait_ge(mhi_ok, n + 1)
                for st in range(ST):
                    hi = extras[:, par, st, g, :, :, 0].rearrange("p j r -> p r j")
                    to = extras[:, par, st, g, :, :, 1].rearrange("p j r -> p r j")
                    ins = dve.scalar_tensor_tensor(to, negm[:, slot, st], 1.0 / M_SCALE, hi, ALU.mult, ALU.subtract)
                ins.then_inc(m_ok, 1)

            def o_out(par, g, n):
                dve.wait_ge(pv_done, n + 1 + PRIME_PV)
                dve.tensor_copy(oall[:, par, :, G0 * g:G0 * g + G0, :], o_ps).then_inc(o_ok, 1)

            def row_sums(par, n):
                dve.wait_ge(o_ok, n * GPB + LAG + PRIME_O)
                dve.wait_ge(inc_ok, n + PRIME_INC)
                dve.reciprocal(rec[:, :, :], oall[:, par, :, :, D0]).then_inc(rec0_ok, 1)
                dve.wait_ge(rec0_ok, n + 1)
                dve.tensor_scalar(rec[:, :, :], rec[:, :, :], gates[:, 0:1], 1.0 / W_SCALE, ALU.mult, ALU.mult).then_inc(rec_ok, 1)

            dve.sem_inc(o_ok, PRIME_O)
            dve.sem_inc(plo_ok[0], PRIME_LO)
            dve.memset(kst[:, :, :, :, :], 0.0).then_inc(t["kzero"], 1)
            dve.wait_ge(t["kzero"], 1)
            for r in range(2):
                ins = dve.memset(kst[:, :, :, r, EXTRA0 + 3 * r:EXTRA0 + 3 * r + 3], M_SCALE)
            ins.then_inc(t["kconst"], 1)
            dve.wait_ge(x0_in, 16)
            norm.statistics(dve, 0, 0)
            norm.normalise(dve, 0, 0)
            dve.wait_ge(t["gates_ok"], 1)
            k_low(0, 0)
            q_low(0, 0)
            q1_out(0, 0)
            q1_out(1, 1)
            row_max(0, 0, 0)
            row_max(1, 0, 0)
            put_max(0, 0, 0, 0)
            q1_out(0, 2)
            row_max(0, 1, 1)
            row_max(1, 1, 1)
            put_max(0, 1, 1, 1)
            dve.wait_ge(x_in, 16 * (TILES - ST) // X_LOAD)
            dve.wait_ge(lag_set, 1)
            with dve.Fori(0, TRIPS) as it:
                for i in range(NG):
                    par, j = divmod(i, GPB)
                    g, b = it * NG + i, it * PAIRS + par
                    if j == LAG:
                        dve.wait_ge(x_ok, b + PRIME_X)
                    o_out((i - LAG) // GPB % 2, (i - LAG) % GPB, g)
                    row_max(0, g + 2, i % 2)
                    row_max(1, g + 2, i % 2)
                    q1_out((i + 3) % 2, g + 3)
                    put_max((i + 2) // GPB % 2, (i + 2) % GPB, g + 2, i % 2)
                    p_low(i % SLOTS, g)
                    if j == 0:
                        norm.statistics(dve, ((b + 1) * ST) % TILES, b + 1)
                    if j == 1:
                        norm.normalise(dve, ((b + 1) * ST) % TILES, b + 1)
                        row_sums(1 - par, b)
                    if j == 2:
                        k_low(1 - par, b + 1)
                    if j == 3:
                        q_low(1 - par, b + 1)
            for n in range(LAG):
                o_out(1, GPB - LAG + n, B * GPB + n)
            row_sums(1, B)

        @block.tensor
        def _(pe):
            def keys(half, r):
                for g in range(4):
                    for c in range(ST):
                        ins = pe.transpose(pT[:, g, c * P:(c + 1) * P], kst[:, c, 4 * half + g, r, :], ident[:, :])
                ins.then_inc(tk_done, 1)

            def q_turn(par, g, done):
                for j in range(2):
                    for st in range(ST):
                        src = qst[:, par, st, G0 * g + 2 * j:G0 * g + 2 * j + 2, :].rearrange("p h r -> p (h r)")
                        ins = pe.transpose(pT[:, j, st * P:(st + 1) * P], src, ident[:, :])
                ins.then_inc(done, 1)

            def scores_by_row(slot, g, st, n):
                for r in range(2):
                    if not (isinstance(n, int) and n == 0 and st == 0):
                        pe.wait_ge(max_ok, 4 * n + 2 * st + r - 1)
                    for j in range(2):
                        ins = pe.matmul(pS1[:, r, j, :], qT1[0:EXTRA0, slot, j, st * P:(st + 1) * P],
                                        kT[0:EXTRA0, r, g, :], start=True, stop=True)
                    ins.then_inc(s1_done, 1)

            def scores_by_key(slot, g, c):
                for r in range(2):
                    ins = pe.matmul(pS2[:, c, r].rearrange("p j s -> p (j s)"), kT[:, r, g, c * P:(c + 1) * P],
                                    qT2[:, slot].rearrange("p j s -> p (j s)"), start=True, stop=True)
                ins.then_inc(s2_done, 1)

            def weigh(slot, par, g, n):
                pe.wait_ge(plo_ok[0], n + 1)
                pe.wait_ge(plo_ok[1], n + 1)
                pe.wait_ge(o_ok, n + PRIME_O)
                for st in range(ST):
                    for h in range(G0):
                        i = 0
                        for c in range(ST):
                            for a, v in PRODUCTS:
                                probs = (p_hi, p_lo)[a]
                                ins = pe.matmul(o_ps[:, st, h, :],
                                                probs[:, 2 * slot + c, h % 2, h // 2, st * P:(st + 1) * P],
                                                vst[:, par, c, g, v, :], start=(i == 0),
                                                stop=(i == ST * len(PRODUCTS) - 1))
                                i += 1
                ins.then_inc(pv_done, 1)

            pe.sem_inc(pv_done, PRIME_PV)
            pe.wait_ge(t["ident_in"], 16)
            pe.wait_ge(klo_ok, 1)
            keys(0, 0)
            pe.wait_ge(kT_ok, 1)
            keys(0, 1)
            pe.wait_ge(qlo_ok, 1)
            pe.wait_ge(kT_ok, 2)
            q_turn(0, 0, t1_done)
            pe.wait_ge(qT1_ok, 1)
            q_turn(0, 1, t1_done)
            pe.wait_ge(qT1_ok, 2)
            scores_by_row(0, 0, 0, 0)
            scores_by_row(0, 0, 1, 0)
            q_turn(0, 2, t1_done)
            scores_by_row(1, 1, 0, 1)
            scores_by_row(1, 1, 1, 1)
            pe.wait_ge(qT1_ok, 3)
            pe.wait_ge(m_ok, 1)
            q_turn(0, 0, t2_done)
            pe.wait_ge(lag_set, 1)
            with pe.Fori(0, TRIPS) as it:
                for i in range(NG):
                    par, j = divmod(i, GPB)
                    g, b = it * NG + i, it * PAIRS + par
                    pe.wait_ge(qT2_ok, g + 1)
                    pe.wait_ge(exp_done, 2 * g - 1 + PRIME_EXP)
                    scores_by_key(i % 2, j, 0)
                    if j == LAG:
                        pe.wait_ge(v_ok, b + 1)
                    weigh((i - LAG) % SLOTS, (i - LAG) // GPB % 2, (i - LAG) % GPB, g)
                    p1, g1 = (i + 1) // GPB % 2, (i + 1) % GPB
                    pe.wait_ge(m_ok, g + 2)
                    pe.wait_ge(qT1_ok, g + 3)
                    if j in (1, 2):
                        pe.wait_ge(kT_ok, 4 * b + 2 + j)
                    if j in (5, 6):
                        pe.wait_ge(kT_ok, 4 * (b + 1) + j - 4)
                    q_turn(p1, g1, t2_done)
                    g2 = (i + 2) % GPB
                    scores_by_row((i + 2) % 2, g2, 0, g + 2)
                    pe.wait_ge(exp_done, 2 * g + PRIME_EXP)
                    scores_by_key(i % 2, j, 1)
                    scores_by_row((i + 2) % 2, g2, 1, g + 2)
                    p3, g3 = (i + 3) // GPB % 2, (i + 3) % GPB
                    if g3 == 0:
                        pe.wait_ge(qlo_ok, b + 2)
                    pe.wait_ge(qT2_ok, g + 2)
                    q_turn(p3, g3, t1_done)
                    if j in (0, 1, 4, 5):
                        if j == 4:
                            pe.wait_ge(klo_ok, b + 2)
                        pe.wait_ge(qT1_ok, g + 4)
                        keys(1 - j // 4, j % 4)
            for n in range(LAG):
                weigh(SLOTS - LAG + n, 1, GPB - LAG + n, B * GPB + n)


BIAS_OUT, BIAS_ROUTER, BIAS_ROWS, BIAS_LOW = 8, 9, 10, 32
NE = 8
C_SCALE = 256.0


def phase_experts(nc, mem, t):
    x, w_e, stage, ident, w_small = t["x"], t["w_e"], t["stage"], t["ident"], t["w_small"]
    TRIPS = B // PAIRS
    UNITS = NE * ST
    RING = 4

    def sb(name, shape, dt):
        return mem.enter_context(nc.sbuf_tensor("m_" + name, shape, dt))

    def sem(name):
        return mem.enter_context(nc.semaphore("m_" + name))

    norm = Norm(nc, mem, "m", t)
    hid = Split(nc, mem, "m_hid", PAIRS)
    com = Split(nc, mem, "m_com", 1)
    y = sb("y", [P, RING, E], F32)
    acc = sb("acc", [P, PAIRS, ST, E], F32)
    sel = sb("sel", [P, BIAS_ROWS, P], F16)
    bias_raw = sb("bias_raw", [P, E], F32)
    bias_hi = sb("bias_hi", [P, E], F16)
    bias = sb("bias", [P, E], F16)
    rw_raw = sb("rw_raw", [P, KC, NE], F32)
    rw = sb("rw", [P, 2, KC, NE], F16)
    ramp = sb("ramp", [P, NE], F32)
    wscale = sb("wscale", [P, 1], F32)
    gscale = sb("gscale", [P, 1], F32)
    logit = sb("logit", [P, ST, NE], F32)
    rest = sb("rest", [P, ST, NE], F32)
    first = sb("first", [P, ST, NE], F32)
    second = sb("second", [P, ST, NE], F32)
    best = sb("best", [P, 6, ST], F32)
    tanh_d = sb("tanh_d", [P, ST], F32)
    gate = sb("gate", [P, PAIRS, ST, NE], F32)

    pE = mem.enter_context(nc.psum_tensor("m_pE", [P, RING, E], F32))
    pT = mem.enter_context(nc.psum_tensor("m_pT", [P, 2, KC, S], F16))
    pR = mem.enter_context(nc.psum_tensor("m_pR", [P, 512], F32))
    pO = mem.enter_context(nc.psum_tensor("m_pO", [P, E], F32))
    logits_ps = pR[:, 0:ST * NE].rearrange("p (s e) -> p s e", s=ST)

    consts_in, zeroed, consts_ok, bias_ok = sem("consts_in"), sem("zeroed"), sem("consts_ok"), sem("bias_ok")
    rw_ok, ramp_ok, wscale_ok = sem("rw_ok"), sem("ramp_ok"), sem("wscale_ok")
    small_in, small_hi, small_32, small_lo = sem("small_in"), sem("small_hi"), sem("small_32"), sem("small_lo")
    routed, tanh_ok, gate_chain = sem("routed"), sem("tanh_ok"), sem("gate_chain")
    expert_done, gelu_done, acc_done = sem("expert_done"), sem("gelu_done"), sem("acc_done")
    out_done, x_ok = sem("out_done"), sem("x_ok")
    GATE_STEPS, GATE_DIFF = 18, 9
    PRIME_X, PRIME_COLS, PRIME_SMALL = 1, 1, 1

    with nc.Block() as block:

        @block.sync
        def _(sp):
            sp.dma_start(sel[:, :, :], t["sel_d"]).then_inc(consts_in, 16)
            sp.dma_start(rw_raw[:, :, :], t["router_d"]).then_inc(consts_in, 16)
            sp.dma_start(ramp[:, :], t["ramp_d"].partition_broadcast(P)).then_inc(consts_in, 16)
            sp.wait_ge(zeroed, 1)
            for row in (0, BIAS_LOW):
                sp.dma_start(bias_raw[row:row + NE, :], t["expert_b_d"]).then_inc(consts_in, 16)
                sp.dma_start(bias_raw[row + BIAS_OUT:row + BIAS_OUT + 1, :], t["out_b_d"]).then_inc(consts_in, 16)
                sp.dma_start(bias_raw[row + BIAS_ROUTER:row + BIAS_ROUTER + 1, 0:NE],
                             t["router_b_d"]).then_inc(consts_in, 16)
            with sp.Fori(0, TRIPS) as it:
                sp.wait_ge(small_lo, it + PRIME_SMALL)
                sp.dma_start(stage[:, 0], t["small_d"][:, it]).then_inc(small_in, 16)

        @block.gpsimd
        def _(pool):
            pool.sem_inc(small_lo, PRIME_SMALL)
            pool.memset(bias_raw[:, :], 0.0).then_inc(zeroed, 1)
            pool.memset(wscale[:, :], W_SCALE).then_inc(wscale_ok, 1)
            pool.wait_ge(wscale_ok, 1)
            norm.deviation(pool, 0)
            with pool.Fori(0, TRIPS) as it:
                norm.deviation(pool, it * PAIRS + 1)
                raw = stage[:, 0].rearrange("p k n -> p (k n)")
                hi = w_small[:, it, 0].rearrange("p k n -> p (k n)")
                lo = w_small[:, it, 1].rearrange("p k n -> p (k n)")
                wide = wscale[:, :].to_broadcast([P, KC * E])
                pool.wait_ge(small_in, it * 16 + 16)
                pool.wait_ge(wscale_ok, 1)
                pool.tensor_tensor(hi, raw, wide, ALU.mult).then_inc(small_hi, 1)
                pool.wait_ge(small_hi, it + 1)
                pool.tensor_tensor(raw, raw, wide, ALU.mult).then_inc(small_32, 1)
                pool.wait_ge(small_32, it + 1)
                pool.wait_ge(wscale_ok, 1)
                pool.tensor_tensor(lo, raw, hi, ALU.subtract).then_inc(small_lo, 1)
                norm.deviation(pool, it * PAIRS + 2)

        @block.scalar
        def _(act):
            def gelu(e, st, n):
                u = n * UNITS + e * ST + st
                slot = (e * ST + st) % RING
                act.wait_ge(expert_done, u + 1)
                act.wait_ge(acc_done, u + 1)
                act.activation(y[:, slot], pE[:, slot], ACT.Gelu_apprx_tanh,
                               scale=1.0 / (X_SCALE * W_SCALE)).then_inc(gelu_done, 1)

            def half_difference(n):
                act.wait_ge(gate_chain, n * GATE_STEPS + GATE_DIFF)
                act.activation(tanh_d[:, :], best[:, 4], ACT.Tanh, scale=0.5).then_inc(tanh_ok, 1)

            def hid_high(n):
                act.wait_ge(norm.xn_ok, n + 1)
                hid.high(act, norm.xn[:, :, :])

            def com_high(par, n):
                act.wait_ge(acc_done, (n + 1) * UNITS + RING)
                com.high(act, acc[:, par])

            act.sem_inc(gelu_done, RING)
            act.sem_inc(com.cols_ok, PRIME_COLS)
            act.wait_ge(bias_ok, 1)
            act.activation(bias_hi[:, :], bias_raw[:, :], ACT.Copy, scale=W_SCALE).then_inc(consts_ok, 1)
            act.activation(rw[:, 0], rw_raw[:, :, :], ACT.Copy, scale=W_SCALE).then_inc(consts_ok, 1)
            hid_high(0)
            for half in range(2):
                hid.out(act, half, pT[:, half], 0, 0)
            half_difference(0)
            with act.Fori(0, TRIPS) as it:
                for par in range(PAIRS):
                    b = it * PAIRS + par
                    for e in range(NE):
                        for st in range(ST):
                            gelu(e, st, b)
                        if par == 1 and e == 0:
                            com_high(0, b - 1)
                        if par == 1 and e == 1:
                            for half in range(2):
                                com.out(act, half, pT[:, half], 0, b - 1)
                        if e == 2:
                            hid_high(b + 1)
                        if par == 0 and e == 3:
                            for half in range(2):
                                hid.out(act, half, pT[:, half], 1, b + 1)
                        if par == 0 and e == 6:
                            half_difference(b + 1)
                b = it * PAIRS + 1
                for half in range(2):
                    hid.out(act, half, pT[:, half], 0, b + 1)
                com_high(1, b)
                half_difference(b + 1)
                for half in range(2):
                    com.out(act, half, pT[:, half], 0, b)

        @block.vector
        def _(dve):
            def spread(ap):
                return ap.unsqueeze(2).to_broadcast([P, ST, NE])

            def link(n, k):
                dve.wait_ge(gate_chain, n * GATE_STEPS + k)

            ramp3 = ramp[:, :].unsqueeze(1).to_broadcast([P, ST, NE])

            def first_best(src, out, m, w, n, k):
                link(n, k)
                dve.tensor_reduce(best[:, m], src, AX.X, ALU.max).then_inc(gate_chain, 1)
                link(n, k + 1)
                dve.tensor_tensor(out, src, spread(best[:, m]), ALU.is_equal).then_inc(gate_chain, 1)
                link(n, k + 2)
                dve.tensor_tensor(out, out, ramp3, ALU.mult).then_inc(gate_chain, 1)
                link(n, k + 3)
                dve.tensor_reduce(best[:, w], out, AX.X, ALU.max).then_inc(gate_chain, 1)
                link(n, k + 4)
                dve.tensor_tensor(out, out, spread(best[:, w]), ALU.is_equal).then_inc(gate_chain, 1)

            def gates_a(n):
                dve.wait_ge(routed, n + 1)
                dve.tensor_scalar(logit[:, :, :], logits_ps, 1.0 / (X_SCALE * W_SCALE), None,
                                  ALU.mult).then_inc(gate_chain, 1)
                first_best(logit[:, :, :], first[:, :, :], 0, 1, n, 1)
                link(n, 6)
                dve.scalar_tensor_tensor(rest[:, :, :], first[:, :, :], -1e30, logit[:, :, :],
                                         ALU.mult, ALU.add).then_inc(gate_chain, 1)
                link(n, 7)
                dve.tensor_reduce(best[:, 2], rest[:, :, :], AX.X, ALU.max).then_inc(gate_chain, 1)
                link(n, 8)
                dve.tensor_tensor(best[:, 4], best[:, 0], best[:, 2], ALU.subtract).then_inc(gate_chain, 1)

            def gates_b(par, n):
                link(n, 9)
                dve.tensor_tensor(second[:, :, :], rest[:, :, :], spread(best[:, 2]),
                                  ALU.is_equal).then_inc(gate_chain, 1)
                link(n, 10)
                dve.tensor_tensor(second[:, :, :], second[:, :, :], ramp3, ALU.mult).then_inc(gate_chain, 1)
                link(n, 11)
                dve.tensor_reduce(best[:, 3], second[:, :, :], AX.X, ALU.max).then_inc(gate_chain, 1)
                link(n, 12)
                dve.tensor_tensor(second[:, :, :], second[:, :, :], spread(best[:, 3]),
                                  ALU.is_equal).then_inc(gate_chain, 1)
                dve.wait_ge(tanh_ok, n + 1)
                dve.tensor_scalar(best[:, 0], tanh_d[:, :], C_SCALE / 2, C_SCALE / 2,
                                  ALU.mult, ALU.add).then_inc(gate_chain, 1)
                dve.tensor_scalar(best[:, 5], tanh_d[:, :], -C_SCALE / 2, C_SCALE / 2,
                                  ALU.mult, ALU.add).then_inc(gate_chain, 1)
                link(n, 15)
                dve.tensor_tensor(first[:, :, :], first[:, :, :], spread(best[:, 0]),
                                  ALU.mult).then_inc(gate_chain, 1)
                dve.tensor_tensor(second[:, :, :], second[:, :, :], spread(best[:, 5]),
                                  ALU.mult).then_inc(gate_chain, 1)
                link(n, 17)
                dve.tensor_tensor(gate[:, par], first[:, :, :], second[:, :, :], ALU.add).then_inc(gate_chain, 1)

            def accumulate(par, e, st, n):
                u = n * UNITS + e * ST + st
                slot = (e * ST + st) % RING
                if e >= 1:
                    dve.wait_ge(acc_done, u - 1 + RING)
                dve.wait_ge(gelu_done, u + 1 + RING)
                scalar = gate[:, par, st, e:e + 1]
                if e == 0:
                    dve.tensor_scalar(acc[:, par, st], y[:, slot], scalar, None, ALU.mult).then_inc(acc_done, 1)
                else:
                    dve.scalar_tensor_tensor(acc[:, par, st], y[:, slot], scalar, acc[:, par, st],
                                             ALU.mult, ALU.add).then_inc(acc_done, 1)

            def update(tile, st, n):
                dve.wait_ge(out_done, n * ST + st + 1)
                dve.wait_ge(rw_ok, 1)
                xt = x[:, tile + st, :]
                dve.scalar_tensor_tensor(xt, pO[:, :], gscale[:, :], xt, ALU.mult, ALU.add).then_inc(x_ok, 1)

            dve.sem_inc(acc_done, RING)
            dve.sem_inc(x_ok, PRIME_X)
            norm.statistics(dve, 0, 0)
            dve.memset(bias[:, :], 0.0).then_inc(ramp_ok, 1)
            dve.tensor_scalar(gscale[:, :], t["tanh_g"][:, 2:3], 1.0 / (C_SCALE * W_SCALE), None, ALU.mult)
            dve.wait_ge(consts_in, 9 * 16)
            dve.tensor_copy(ramp[:, :], ramp[:, :]).then_inc(bias_ok, 1)
            norm.normalise(dve, 0, 0)
            dve.wait_ge(ramp_ok, 1)
            dve.wait_ge(consts_ok, 2)
            dve.tensor_copy(bias[0:BIAS_ROWS, :], bias_hi[0:BIAS_ROWS, :])
            low = slice(BIAS_LOW, BIAS_LOW + BIAS_ROWS)
            dve.scalar_tensor_tensor(bias[low, :], bias_raw[low, :], W_SCALE, bias_hi[low, :],
                                     ALU.mult, ALU.subtract)
            dve.scalar_tensor_tensor(rw[:, 1], rw_raw[:, :, :], W_SCALE, rw[:, 0],
                                     ALU.mult, ALU.subtract).then_inc(rw_ok, 1)
            dve.drain().then_inc(zeroed, 1)
            hid.low(dve, norm.xn[:, :, :], 0)
            gates_a(0)
            gates_b(0, 0)
            with dve.Fori(0, TRIPS) as it:
                for par in range(PAIRS):
                    b = it * PAIRS + par
                    ahead = ((b + 1) * ST) % TILES
                    dve.wait_ge(gate_chain, (b + 1) * GATE_STEPS)
                    for e in range(NE):
                        for st in range(ST):
                            accumulate(par, e, st, b)
                        if e == 0:
                            if par == 1:
                                com.low(dve, acc[:, 0], b - 1)
                            norm.statistics(dve, ahead, b + 1)
                        if e == 1:
                            norm.normalise(dve, ahead, b + 1)
                        if e == 2:
                            hid.low(dve, norm.xn[:, :, :], b + 1)
                        if par == 1 and e in (3, 5):
                            update((b - 1) * ST, (e - 3) // 2, b - 1)
                        if par == 0 and e == 5:
                            gates_a(b + 1)
                        if par == 0 and e == 6:
                            gates_b(1, b + 1)
                b = it * PAIRS + 1
                com.low(dve, acc[:, 1], b)
                gates_a(b + 1)
                gates_b(0, b + 1)
                for st in range(ST):
                    update(b * ST, st, b)

        @block.tensor
        def _(pe):
            def route(par, n):
                pe.wait_ge(gate_chain, (n - 1) * GATE_STEPS + 1)
                route_now(par)

            def route_now(par):
                for st in range(ST):
                    project(pe, logits_ps[:, st], hid.cols, par, st, rw, more=True)
                    ins = pe.matmul(logits_ps[:, st], sel[:, BIAS_ROUTER, :], bias[:, 0:NE], start=False, stop=True)
                ins.then_inc(routed, 1)

            def expert(par, e, st, n):
                u = n * UNITS + e * ST + st
                slot = (e * ST + st) % RING
                pe.wait_ge(gelu_done, u + 1)
                project(pe, pE[:, slot], hid.cols, par, st, w_e[:, e], more=True)
                pe.matmul(pE[:, slot], sel[:, e, :], bias[:, :], start=False, stop=True).then_inc(expert_done, 1)

            def combine(st, n):
                pe.wait_ge(com.cols_ok, 2 * n + 2 + PRIME_COLS)
                pe.wait_ge(x_ok, n * ST + st + PRIME_X)
                project(pe, pO[:, :], com.cols, 0, st, w_small[:, 0], more=True)
                pe.matmul(pO[:, :], sel[:, BIAS_OUT, :], bias[:, :], start=False, stop=True).then_inc(out_done, 1)

            pe.wait_ge(hid.lo_ok, 1)
            for half in range(2):
                hid.turn(pe, half, pT[:, half], ident)
            pe.wait_ge(rw_ok, 1)
            pe.wait_ge(hid.cols_ok, 2)
            route_now(0)
            with pe.Fori(0, TRIPS) as it:
                for par in range(PAIRS):
                    b = it * PAIRS + par
                    pe.wait_ge(hid.cols_ok, 2 * b + 2)
                    for e in range(NE):
                        for st in range(ST):
                            expert(par, e, st, b)
                        if par == 0 and e == 3:
                            pe.wait_ge(hid.lo_ok, b + 2)
                            pe.wait_ge(com.cols_ok, 2 * b + PRIME_COLS)
                            for half in range(2):
                                hid.turn(pe, half, pT[:, half], ident)
                        if par == 0 and e == 4:
                            pe.wait_ge(hid.cols_ok, 2 * b + 4)
                            route(1, b + 1)
                        if par == 1 and e == 1:
                            pe.wait_ge(com.lo_ok, b)
                            for half in range(2):
                                com.turn(pe, half, pT[:, half], ident)
                        if par == 1 and e in (2, 4):
                            pe.wait_ge(small_lo, 1 + PRIME_SMALL)
                            combine((e - 2) // 2, b - 1)
                b = it * PAIRS + 1
                pe.wait_ge(hid.lo_ok, b + 2)
                for half in range(2):
                    hid.turn(pe, half, pT[:, half], ident)
                pe.wait_ge(hid.cols_ok, 2 * b + 4)
                route(0, b + 1)
                pe.wait_ge(com.lo_ok, b + 1)
                for half in range(2):
                    com.turn(pe, half, pT[:, half], ident)
                for st in range(ST):
                    combine(st, b)


H1, D1 = 16, 32
G1 = 4
R1 = 128
V1 = 2 * D1 + 1
Q1_SCALE, K1_SCALE, V1_SCALE = 64.0, 1024.0, 1024.0
LIFT1 = 627.0
MASK = 32768.0


def phase_attention1(nc, mem, t):
    x, ident, w_small = t["x"], t["ident"], t["w_small"]
    GPB = H1 // G1
    NG = PAIRS * GPB
    TRIPS = B // PAIRS
    W = S + P

    def sb(name, shape, dt):
        return mem.enter_context(nc.sbuf_tensor("a1_" + name, shape, dt))

    def sem(name):
        return mem.enter_context(nc.semaphore("a1_" + name))

    arena = t["w_e"][:, :, :, :, :].rearrange("p e a k n -> p (e a k n)")
    used = [0]

    def carve(n):
        used[0] += n
        return arena[:, used[0] - n:used[0]]

    qst = carve(PAIRS * ST * H1 * R1).rearrange("p (a s h r) -> p a s h r", a=PAIRS, s=ST, h=H1)
    kst = carve(ST * H1 * R1).rearrange("p (s h r) -> p s h r", s=ST, h=H1)
    kT = carve(PAIRS * H1 * S).rearrange("p (a h t) -> p a h t", a=PAIRS, h=H1)
    p_hi = carve(2 * G1 * W).rearrange("p (a h w) -> p a h w", a=2, h=G1)
    p_lo = carve(2 * G1 * W).rearrange("p (a h w) -> p a h w", a=2, h=G1)
    vst = carve(PAIRS * ST * H1 * V1).rearrange("p (a s h d) -> p a s h d", a=PAIRS, s=ST, h=H1)

    norm = Norm(nc, mem, "a1", t)
    hid = Split(nc, mem, "a1_hid", 1)
    com = Split(nc, mem, "a1_com", 1)
    ctx = sb("ctx", [P, PAIRS, ST, L], F32)
    cx = sb("cx", [P, 2, ST, L], F16)
    cxT = sb("cxT", [P, 2, S], F16)
    qT1 = sb("qT1", [P, 2, G1, S], F16)
    qT2 = sb("qT2", [P, 2, G1, S], F16)
    p32 = sb("p32", [P, G1, W], F32)
    negm = sb("negm", [P, 2, ST, G1], F32)
    oall = sb("oall", [P, ST, H1, V1], F32)
    o32 = sb("o32", [P, ST, H1, D1], F32)
    rec = sb("rec", [P, ST, H1], F32)
    gscale = sb("gscale", [P, 1], F32)
    big_ident = sb("big_ident", [P, P], F16)
    mask_row = sb("mask_row", [P, P], F16)
    mask_key = sb("mask_key", [P, P], F16)

    pS2 = mem.enter_context(nc.psum_tensor("a1_pS2", [P, 2, 512], F32))
    pS1 = mem.enter_context(nc.psum_tensor("a1_pS1", [P, G1, S], F32))
    pT = mem.enter_context(nc.psum_tensor("a1_pT", [P, 2, G1, S], F16))
    pO = mem.enter_context(nc.psum_tensor("a1_pO", [P, 512], F32))
    pP = mem.enter_context(nc.psum_tensor("a1_pP", [P, E], F32))
    o_ps = pO[:, 0:G1 * V1].rearrange("p (h d) -> p h d", h=G1)
    pP_heads = pP[:, :].rearrange("p (h d) -> p h d", h=H1)
    pT_cx = pT[:, 0].rearrange("p g t -> p (g t)")[:, 0:2 * S].rearrange("p (a t) -> p a t", a=2)

    ctx_in = [sem(f"ctx{par}_in") for par in range(PAIRS)]
    masks_in, zeroed, const_set, k_const = sem("masks_in"), sem("zeroed"), sem("const_set"), sem("k_const")
    cxhi_ok, cxlo_ok, cx_turned, cx_ok = sem("cxhi_ok"), sem("cxlo_ok"), sem("cx_turned"), sem("cx_ok")
    projected, pphi_ok, pp_ok = sem("projected"), sem("pphi_ok"), sem("pp_ok")
    k_turned, kT_ok = sem("k_turned"), sem("kT_ok")
    t1_done, t2_done, qT1_ok, qT2_ok = sem("t1_done"), sem("t2_done"), sem("qT1_ok"), sem("qT2_ok")
    dup_ok = sem("dup_ok")
    s1_done, max_ok, mhi_ok, m_ok = sem("s1_done"), sem("max_ok"), sem("mhi_ok"), sem("m_ok")
    s2_done, exp_done = sem("s2_done"), sem("exp_done")
    plo_ok = [sem("plo_dve"), sem("plo_pool")]
    pv_done, o_ok = sem("pv_done"), sem("o_ok")
    rec_ok, osum_ok, o32_ok = sem("rec_ok"), sem("osum_ok"), sem("o32_ok")
    PRIME_EXP, PRIME_LO, PRIME_PV, PRIME_O = 2, 2, 4, 1

    STEP_USES = (("k", 0), ("k", 1)), (("v", 0), ("q", 0)), (("v", 1), ("q", 1)), (("out", 0), ("out", 1))
    PREP = 6

    def use(g, k):
        return PREP + 2 * g + k

    def high_count(b, j, k):
        return PREP * (b + 1) + 2 * j + k

    with nc.Block() as block:

        @block.sync
        def _(sp):
            def load_ctx(b, par):
                sp.dma_start(ctx[:, par], t["ctx_d"][:, b]).then_inc(ctx_in[par], 16)

            load_ctx(0, 0)
            load_ctx(1, 1)
            sp.dma_start(big_ident[:, :], t["big_ident_d"]).then_inc(masks_in, 16)
            sp.dma_start(mask_row[:, :], t["mask_row_d"]).then_inc(masks_in, 16)
            sp.dma_start(mask_key[:, :], t["mask_key_d"]).then_inc(masks_in, 16)
            with sp.Fori(0, TRIPS) as it:
                for par in range(PAIRS):
                    sp.wait_ge(cxlo_ok, it * PAIRS + par + 1)
                    load_ctx((it * PAIRS + PAIRS + par) % B, par)
            for par in range(PAIRS):
                sp.wait_ge(ctx_in[par], 16 * (TRIPS + 1))

        @block.gpsimd
        def _(pool):
            def p_low(slot, h, n):
                pool.wait_ge(exp_done, G1 * n + h + 1 + PRIME_EXP)
                pool.tensor_tensor(p_lo[:, slot, h], p32[:, h], p_hi[:, slot, h],
                                   ALU.subtract).then_inc(plo_ok[1], 1)

            pool.sem_inc(plo_ok[1], PRIME_LO)
            pool.memset(qst, 0.0)
            pool.memset(vst, 0.0)
            pool.memset(p_hi[:, 1], 1.0)
            pool.memset(p_lo[:, 1], 0.0)
            pool.memset(oall[:, :, :, :], 0.0).then_inc(zeroed, 1)
            pool.wait_ge(zeroed, 1)
            pool.memset(qst[:, :, :, :, 3 * D1 + 2:3 * D1 + 3], LIFT1)
            pool.memset(oall[:, :, :, D1:D1 + 1], 1.0)
            pool.memset(vst[:, :, :, :, D1:D1 + 1], 1.0).then_inc(const_set, 1)
            norm.deviation(pool, 0)
            norm.deviation(pool, 1)
            with pool.Fori(0, TRIPS) as it:
                for i in range(NG):
                    par, j = divmod(i, GPB)
                    g, b = it * NG + i, it * PAIRS + par
                    if j == 2:
                        norm.deviation(pool, b + 2)
                    for h in (2, 3):
                        p_low(i % 2, h, g)

        @block.scalar
        def _(act):
            def exps(slot, h, n):
                u = G1 * n + h
                act.wait_ge(s2_done, u + 1)
                if h == 0:
                    act.wait_ge(pv_done, 2 * n + PRIME_PV)
                scale = D1 ** -0.5 / (Q1_SCALE * K1_SCALE)
                act.activation(p_hi[:, slot, h], pS2[:, h % 2, 0:W], ACT.Exp, scale=scale)
                act.wait_ge(plo_ok[h // 2], 2 * n + h % 2 + 1)
                act.activation(p32[:, h], pS2[:, h % 2, 0:W], ACT.Exp, scale=scale).then_inc(exp_done, 1)

            def ctx_high(par, loads):
                act.wait_ge(ctx_in[par], 16 * loads)
                act.activation(cx[:, 0], ctx[:, par], ACT.Copy, scale=W_SCALE).then_inc(cxhi_ok, 1)

            def hid_high(n):
                act.wait_ge(norm.xn_ok, n + 1)
                hid.high(act, norm.xn[:, :, :])

            def hid_out(half, n):
                hid.out(act, half, pT[:, 1 - half], 0, n)

            def ctx_out(n):
                act.wait_ge(cx_turned, n + 1)
                act.activation(cxT[:, :, :], pT_cx, ACT.Copy).then_inc(cx_ok, 1)

            def com_out(half, n):
                com.out(act, half, pT[:, 1 - half], 0, n)

            def high(kind, par, st, uses):
                act.wait_ge(projected, uses + 1)
                if kind == "q":
                    ins = act.activation(qst[:, par, st, :, 0:D1], pP_heads, ACT.Copy,
                                         scale=Q1_SCALE / (X_SCALE * W_SCALE))
                elif kind == "k":
                    ins = act.activation(kst[:, st, :, 0:D1], pP_heads, ACT.Copy,
                                         scale=K1_SCALE / (W_SCALE * W_SCALE))
                else:
                    ins = act.activation(vst[:, par, st, :, 0:D1], pP_heads, ACT.Copy,
                                         scale=V1_SCALE / (W_SCALE * W_SCALE))
                ins.then_inc(pphi_ok, 1)

            def keys_out(par, k, n):
                act.wait_ge(k_turned, 4 * n + k + 1)
                act.activation(kT[:, par, G1 * k:G1 * k + G1, :], pT[:, 1 - k % 2],
                               ACT.Copy).then_inc(kT_ok, 1)

            def com_high(n):
                act.wait_ge(o32_ok, n + 1)
                com.high(act, o32[:, :, :, :].rearrange("p s h d -> p s (h d)"))

            act.sem_inc(exp_done, PRIME_EXP)
            ctx_high(0, 1)
            hid_high(0)
            for half in range(2):
                hid_out(half, 0)
            ctx_out(0)
            act.wait_ge(k_const, 1)
            act.wait_ge(const_set, 1)
            for n, (kind, st) in enumerate(PREPARE):
                high(kind, 0, st, n)
            for k in range(4):
                keys_out(0, k, 0)
            ctx_high(1, 1)
            hid_high(1)
            ctx_out(1)
            with act.Fori(0, TRIPS) as it:
                for i in range(NG):
                    par, j = divmod(i, GPB)
                    g, b = it * NG + i, it * PAIRS + par
                    exps(i % 2, 0, g)
                    if j == 0:
                        hid_out(0, b + 1)
                    if j == 1 or j == 3:
                        keys_out(1 - par, j - 1, b + 1)
                    if j == 2:
                        com_out(0, b)
                    if j < 3:
                        kind, st = STEP_USES[j][0]
                        high(kind, 1 - par, st, use(g, 0))
                    exps(i % 2, 1, g)
                    if j == 0:
                        hid_out(1, b + 1)
                    if j == 1 or j == 3:
                        keys_out(1 - par, j, b + 1)
                    if j == 2:
                        com_out(1, b)
                    exps(i % 2, 2, g)
                    if j == 1:
                        com_high(b)
                    if j == 3:
                        hid_high(b + 2)
                    if j < 3:
                        kind, st = STEP_USES[j][1]
                        high(kind, 1 - par, st, use(g, 1))
                    exps(i % 2, 3, g)
                    if j == 0:
                        ctx_high(par, it + 2)
                    if j == 3:
                        ctx_out(b + 2)
            com_high(B)
            for half in range(2):
                com_out(half, B)

        @block.vector
        def _(dve):
            def ctx_low(par, n):
                dve.wait_ge(cxhi_ok, n + 1)
                dve.scalar_tensor_tensor(cx[:, 1], ctx[:, par], W_SCALE, cx[:, 0],
                                         ALU.mult, ALU.subtract).then_inc(cxlo_ok, 1)

            def low(kind, par, st, uses, highs):
                dve.wait_ge(pphi_ok, highs + 1)
                if kind == "q":
                    dst, hi = qst[:, par, st, :, D1:2 * D1], qst[:, par, st, :, 0:D1]
                    scale = Q1_SCALE / (X_SCALE * W_SCALE)
                elif kind == "k":
                    dst, hi = kst[:, st, :, 2 * D1:3 * D1], kst[:, st, :, 0:D1]
                    scale = K1_SCALE / (W_SCALE * W_SCALE)
                else:
                    dst, hi = vst[:, par, st, :, D1 + 1:], vst[:, par, st, :, 0:D1]
                    scale = V1_SCALE / (W_SCALE * W_SCALE)
                dve.scalar_tensor_tensor(dst, pP_heads, scale, hi, ALU.mult, ALU.subtract).then_inc(pp_ok, 1)
                if kind == "q":
                    dve.tensor_copy(qst[:, par, st, :, 2 * D1:3 * D1], hi).then_inc(dup_ok, 1)
                elif kind == "k":
                    dve.tensor_copy(kst[:, st, :, D1:2 * D1], hi).then_inc(dup_ok, 1)

            def p_low(slot, h, n):
                dve.wait_ge(exp_done, G1 * n + h + 1 + PRIME_EXP)
                dve.tensor_tensor(p_lo[:, slot, h], p32[:, h], p_hi[:, slot, h],
                                  ALU.subtract).then_inc(plo_ok[0], 1)

            def q1_out(slot, n):
                dve.wait_ge(t1_done, n + 1)
                dve.tensor_copy(qT1[:, slot], pT[:, 0]).then_inc(qT1_ok, 1)

            def q2_out(slot, n):
                dve.wait_ge(t2_done, n + 1)
                dve.tensor_copy(qT2[:, slot], pT[:, 1]).then_inc(qT2_ok, 1)

            def row_max(st, slot, n):
                dve.wait_ge(s1_done, 2 * n + st + 1)
                dve.tensor_reduce(negm[:, slot, st], pS1[:, :, 0:(st + 1) * P], AX.X, ALU.max,
                                  negate=True).then_inc(max_ok, 1)

            def put_max(par, g, slot, n):
                dve.wait_ge(max_ok, 2 * n + 2)
                heads = qst[:, par, :, G1 * g:G1 * g + G1, :]
                dve.tensor_scalar(heads[:, :, :, 3 * D1], negm[:, slot], 1.0 / M_SCALE, None,
                                  ALU.mult).then_inc(mhi_ok, 1)
                dve.wait_ge(mhi_ok, n + 1)
                dve.scalar_tensor_tensor(heads[:, :, :, 3 * D1 + 1], negm[:, slot], 1.0 / M_SCALE,
                                         heads[:, :, :, 3 * D1], ALU.mult, ALU.subtract).then_inc(m_ok, 1)

            def o_out(st, g, n, batch):
                if g == 0 and st == 0:
                    dve.wait_ge(osum_ok, batch + 1)
                dve.wait_ge(pv_done, 2 * n + st + 1 + PRIME_PV)
                dve.tensor_copy(oall[:, st, G1 * g:G1 * g + G1, :], o_ps).then_inc(o_ok, 1)

            def row_sums(n):
                dve.wait_ge(o_ok, (n * GPB + 1) * ST + PRIME_O)
                dve.reciprocal(rec[:, :, :], oall[:, :, :, D1]).then_inc(rec_ok, 1)

            def add_halves(n):
                dve.wait_ge(o_ok, (n * GPB + 1) * ST + PRIME_O)
                dve.tensor_tensor(o32[:, :, :, :], oall[:, :, :, 0:D1], oall[:, :, :, D1 + 1:],
                                  ALU.add).then_inc(osum_ok, 1)

            def divide(n):
                dve.wait_ge(rec_ok, n + 1)
                dve.wait_ge(osum_ok, n + 1)
                dve.tensor_tensor(o32[:, :, :, :], o32[:, :, :, :],
                                  rec[:, :, :].unsqueeze(3).to_broadcast([P, ST, H1, D1]),
                                  ALU.mult).then_inc(o32_ok, 1)

            def com_low(n):
                dve.wait_ge(o32_ok, n + 1)
                com.low(dve, o32[:, :, :, :].rearrange("p s h d -> p s (h d)"), n)

            def update(tile, st, uses):
                dve.wait_ge(projected, uses + 1)
                dve.wait_ge(k_const, 1)
                xt = x[:, tile + st, :]
                dve.scalar_tensor_tensor(xt, pP[:, :], gscale[:, :], xt, ALU.mult, ALU.add).then_inc(pp_ok, 1)

            dve.sem_inc(plo_ok[0], PRIME_LO)
            dve.sem_inc(o_ok, PRIME_O)
            norm.statistics(dve, 0, 0)
            dve.tensor_scalar(gscale[:, :], t["tanh_g"][:, 1:2], 1.0 / (V1_SCALE * W_SCALE), None, ALU.mult)
            dve.memset(kst, 0.0).then_inc(t["kzero"], 1)
            dve.wait_ge(t["kzero"], 2)
            dve.memset(kst[:, :, :, 3 * D1:3 * D1 + 3], M_SCALE).then_inc(k_const, 1)
            ctx_low(0, 0)
            norm.normalise(dve, 0, 0)
            norm.statistics(dve, ST, 1)
            hid.low(dve, norm.xn[:, :, :], 0)
            for n, (kind, st) in enumerate(PREPARE):
                low(kind, 0, st, n, n)
            ctx_low(1, 1)
            norm.normalise(dve, ST, 1)
            hid.low(dve, norm.xn[:, :, :], 1)
            q1_out(0, 0)
            row_max(0, 0, 0)
            row_max(1, 0, 0)
            put_max(0, 0, 0, 0)
            q2_out(0, 0)
            dve.wait_ge(const_set, 1)
            with dve.Fori(0, TRIPS) as it:
                for i in range(NG):
                    par, j = divmod(i, GPB)
                    g, b = it * NG + i, it * PAIRS + par
                    p1, g1, s1 = (i + 1) // GPB % 2, (i + 1) % GPB, (i + 1) % 2
                    q1_out(s1, g + 1)
                    for k in range(2):
                        kind, st = STEP_USES[j][k]
                        if k == 1:
                            p_low(i % 2, 0, g)
                            row_max(0, s1, g + 1)
                            o_out(0, (i - 1) % GPB, g, b)
                            p_low(i % 2, 1, g)
                            if j == 1:
                                divide(b)
                            row_max(1, s1, g + 1)
                            put_max(p1, g1, s1, g + 1)
                        if kind == "out":
                            update(((b - 1) * ST + TILES) % TILES, st, use(g, k))
                        else:
                            low(kind, 1 - par, st, use(g, k), high_count(b, j, k))
                    q2_out(s1, g + 1)
                    o_out(1, (i - 1) % GPB, g, b)
                    if j == 0:
                        row_sums(b)
                        add_halves(b)
                        ctx_low(par, b + 2)
                    if j == 1:
                        com_low(b)
                        norm.statistics(dve, ((b + 2) * ST) % TILES, b + 2)
                    if j == 2:
                        norm.normalise(dve, ((b + 2) * ST) % TILES, b + 2)
                    if j == 3:
                        hid.low(dve, norm.xn[:, :, :], b + 2)
            for st in range(ST):
                o_out(st, GPB - 1, B * GPB, B)
            row_sums(B)
            add_halves(B)
            divide(B)
            com_low(B)
            for st in range(ST):
                update((B - 1) * ST, st, use(B * GPB, st))

        @block.tensor
        def _(pe):
            def turn_context():
                for half in range(2):
                    for c in range(ST):
                        ins = pe.transpose(pT_cx[:, half, c * P:(c + 1) * P], cx[:, half, c, :], ident[:, :])
                ins.then_inc(cx_turned, 1)

            def prepare(kind, st):
                if kind == "q":
                    ins = project(pe, pP[:, :], hid.cols, 0, st, w_small[:, 1])
                else:
                    part = 0 if kind == "k" else 1
                    for k, (a, w) in enumerate(PRODUCTS):
                        ins = pe.matmul(pP[:, :], cxT[:, a, st * P:(st + 1) * P], w_small[:, 3, w, part, :],
                                        start=(k == 0), stop=(k == 2))
                ins.then_inc(projected, 1)

            def turn_keys(k):
                for h in range(G1):
                    for c in range(ST):
                        ins = pe.transpose(pT[:, 1 - k % 2, h, c * P:(c + 1) * P], kst[:, c, G1 * k + h, :], ident[:, :])
                ins.then_inc(k_turned, 1)

            def q_turn(bank, par, g, done):
                for h in range(G1):
                    for st in range(ST):
                        ins = pe.transpose(pT[:, bank, h, st * P:(st + 1) * P], qst[:, par, st, G1 * g + h, :],
                                           ident[:, :])
                ins.then_inc(done, 1)

            def scores_by_row(slot, par, g, st):
                for h in range(G1):
                    pe.matmul(pS1[:, h, 0:(st + 1) * P], qT1[0:3 * D1, slot, h, st * P:(st + 1) * P],
                              kT[0:3 * D1, par, G1 * g + h, 0:(st + 1) * P], start=True, stop=False)
                    ins = pe.matmul(pS1[:, h, st * P:(st + 1) * P], big_ident[:, :], mask_row[:, :],
                                    start=False, stop=True)
                ins.then_inc(s1_done, 1)

            def scores_by_key(slot, par, g, h, n):
                pe.wait_ge(exp_done, G1 * n + h - 1 + PRIME_EXP)
                key = kT[:, par, G1 * g + h, :]
                pe.matmul(pS2[:, h % 2, 0:S], key[:, 0:P], qT2[:, slot, h, :], start=True, stop=False)
                pe.matmul(pS2[:, h % 2, 0:P], big_ident[:, :], mask_key[:, :], start=False, stop=True)
                pe.matmul(pS2[:, h % 2, S:W], key[:, P:S], qT2[:, slot, h, P:S], start=True, stop=False)
                pe.matmul(pS2[:, h % 2, S:W], big_ident[:, :], mask_key[:, :], start=False,
                          stop=True).then_inc(s2_done, 1)

            def weigh(slot, par, g, st, n):
                if st == 0:
                    for k in range(2):
                        pe.wait_ge(plo_ok[k], 2 * n + PRIME_LO)
                pe.wait_ge(o_ok, 2 * n + st + PRIME_O)
                for h in range(G1):
                    for c, at in ((0, 0),) if st == 0 else ((0, P), (1, S)):
                        for half, probs in enumerate((p_hi, p_lo)):
                            ins = pe.matmul(o_ps[:, h, :], probs[:, slot, h, at:at + P],
                                            vst[:, par, c, G1 * g + h, :],
                                            start=(c == 0 and half == 0), stop=(c == st and half == 1))
                ins.then_inc(pv_done, 1)

            def turn_hid(half, n):
                pe.wait_ge(hid.lo_ok, n + 1)
                hid.turn(pe, half, pT[:, 1 - half], ident)

            def turn_com(half, n):
                pe.wait_ge(com.lo_ok, n + 1)
                com.turn(pe, half, pT[:, 1 - half], ident)

            def output(st, n, uses):
                pe.wait_ge(com.cols_ok, 2 * n + 2)
                pe.wait_ge(pp_ok, uses)
                project(pe, pP[:, :], com.cols, 0, st, w_small[:, 2]).then_inc(projected, 1)

            pe.sem_inc(pv_done, PRIME_PV)
            for half in range(2):
                turn_hid(half, 0)
            pe.wait_ge(cxlo_ok, 1)
            pe.wait_ge(hid.cols_ok, 2)
            turn_context()
            pe.wait_ge(cx_ok, 1)
            for n, (kind, st) in enumerate(PREPARE):
                if n:
                    pe.wait_ge(pp_ok, n)
                prepare(kind, st)
            pe.wait_ge(dup_ok, 4)
            for k in range(4):
                if k >= 2:
                    pe.wait_ge(kT_ok, k - 1)
                turn_keys(k)
            pe.wait_ge(kT_ok, 4)
            pe.wait_ge(cxlo_ok, 2)
            turn_context()
            pe.wait_ge(cx_ok, 2)
            q_turn(0, 0, 0, t1_done)
            pe.wait_ge(qT1_ok, 1)
            pe.wait_ge(masks_in, 48)
            scores_by_row(0, 0, 0, 0)
            pe.wait_ge(max_ok, 1)
            scores_by_row(0, 0, 0, 1)
            pe.wait_ge(m_ok, 1)
            q_turn(1, 0, 0, t2_done)
            pe.wait_ge(const_set, 1)
            with pe.Fori(0, TRIPS) as it:
                for i in range(NG):
                    par, j = divmod(i, GPB)
                    g, b = it * NG + i, it * PAIRS + par
                    p1, g1, s1 = (i + 1) // GPB % 2, (i + 1) % GPB, (i + 1) % 2

                    def use_bank(k):
                        kind, st = STEP_USES[j][k]
                        if kind == "out":
                            output(st, b, use(g, k))
                        else:
                            pe.wait_ge(pp_ok, use(g, k))
                            prepare(kind, st)

                    def weigh_before(st):
                        weigh((i - 1) % 2, (i - 1) // GPB % 2, (i - 1) % GPB, st, g)

                    def fill(half):
                        if j == 0:
                            turn_hid(half, b + 1)
                        if j == 1:
                            if half == 0:
                                pe.wait_ge(dup_ok, 4 * (b + 1) + 2)
                            turn_keys(half)
                        if j == 2:
                            turn_com(half, b)
                        if j == 3:
                            turn_keys(2 + half)

                    def fill_is_out(j, b, half):
                        if j == 0:
                            pe.wait_ge(hid.cols_ok, 2 * (b + 1) + half + 1)
                        if j == 1:
                            pe.wait_ge(kT_ok, 4 * (b + 1) + half + 1)
                        if j == 2:
                            pe.wait_ge(com.cols_ok, 2 * b + half + 1)
                        if j == 3:
                            pe.wait_ge(kT_ok, 4 * (b + 1) + half + 3)
                            if half == 1:
                                pe.wait_ge(cx_ok, b + 3)

                    pe.wait_ge(qT2_ok, g + 1)
                    scores_by_key(i % 2, par, j, 0, g)
                    fill(0)
                    if j == 3:
                        pe.wait_ge(dup_ok, 4 * (b + 2))
                    fill_is_out((j - 1) % GPB, b if j else b - 1, 1)
                    q_turn(0, p1, g1, t1_done)
                    use_bank(0)
                    scores_by_key(i % 2, par, j, 1, g)
                    pe.wait_ge(qT1_ok, g + 2)
                    pe.wait_ge(max_ok, 2 * g + 2)
                    scores_by_row(s1, p1, g1, 0)
                    fill(1)
                    weigh_before(0)
                    scores_by_key(i % 2, par, j, 2, g)
                    pe.wait_ge(max_ok, 2 * g + 3)
                    scores_by_row(s1, p1, g1, 1)
                    use_bank(1)
                    fill_is_out(j, b, 0)
                    if j == 3:
                        pe.wait_ge(kT_ok, 4 * (b + 1) + 4)
                        pe.wait_ge(cxlo_ok, b + 3)
                        turn_context()
                    scores_by_key(i % 2, par, j, 3, g)
                    pe.wait_ge(m_ok, g + 2)
                    q_turn(1, p1, g1, t2_done)
                    weigh_before(1)
            for st in range(ST):
                weigh(1, 1, GPB - 1, st, B * GPB)
            pe.wait_ge(qT2_ok, B * GPB + 1)
            pe.wait_ge(qT1_ok, B * GPB + 1)
            for half in range(2):
                turn_com(half, B)
            for st in range(ST):
                output(st, B, use(B * GPB, st))


PREPARE = (("k", 0), ("v", 0), ("k", 1), ("v", 1), ("q", 0), ("q", 1))


FF = 2048
FM = FF // E
FC = FF // P
H_SCALE = 256.0


def phase_feed_forward(nc, mem, t, out_d):
    x, stage, ident, w_gu, w_d = t["x"], t["stage"], t["ident"], t["w_e"], t["w_d"]
    TRIPS = B // PAIRS
    UNITS = FC // 2
    MATS = 3 * FM

    def sb(name, shape, dt):
        return mem.enter_context(nc.sbuf_tensor("f_" + name, shape, dt))

    def sem(name):
        return mem.enter_context(nc.semaphore("f_" + name))

    norm = Norm(nc, mem, "f", t)
    hid = Split(nc, mem, "f_hid", PAIRS)
    sg = sb("sg", [P, 2, 2, S], F32)
    h32 = sb("h32", [P, 2, 2, S], F32)
    hp = t["w_small"][:, 0:2].rearrange("p m a k n -> p (m a k n)").rearrange("p (a c s) -> p a c s", a=2, c=FC)
    gscale = sb("gscale", [P, 1], F32)

    pG = mem.enter_context(nc.psum_tensor("f_pG", [P, 2, 2, S], F32))
    pU = mem.enter_context(nc.psum_tensor("f_pU", [P, 2, 2, S], F32))
    pD = mem.enter_context(nc.psum_tensor("f_pD", [P, ST, E], F32))
    pT = mem.enter_context(nc.psum_tensor("f_pT", [P, 2, KC, S], F16))

    stage_in = [sem(f"stage{k}_in") for k in range(2)]
    whi_ok, wlo_ok, gs_ok = sem("whi_ok"), sem("wlo_ok"), sem("gs_ok")
    gu_done, silu_done, h_ok, hhi_ok, hlo_ok = sem("gu_done"), sem("silu_done"), sem("h_ok"), sem("hhi_ok"), sem("hlo_ok")
    down_done, x_ok, sent = sem("down_done"), sem("x_ok"), sem("sent")
    PRIME = 2

    def pair_of(m):
        return w_gu[:, m] if m < 2 * FM else w_d[:, m - 2 * FM]

    with nc.Block() as block:

        @block.sync
        def _(sp):
            for m in range(MATS):
                if m >= 2:
                    sp.wait_ge(wlo_ok, m - 1)
                src = t["gu_d"][:, m] if m < 2 * FM else t["down_d"][:, m - 2 * FM]
                sp.dma_start(stage[:, m % 2], src).then_inc(stage_in[m % 2], 16)
            with sp.Fori(0, B) as b:
                sp.wait_ge(x_ok, b * ST + ST + PRIME)
                sp.dma_start(out_d[:, bass.ds(b * ST, ST), :], x[:, bass.ds(b * ST, ST), :]).then_inc(sent, 16)
            sp.wait_ge(sent, 16 * B)

        @block.gpsimd
        def _(pool):
            def h_low(slot, u, n):
                pool.wait_ge(hhi_ok, n * UNITS + u + 1)
                pool.tensor_tensor(hp[:, 1, 2 * u:2 * u + 2, :], h32[:, slot], hp[:, 0, 2 * u:2 * u + 2, :],
                                   ALU.subtract).then_inc(hlo_ok, 1)

            pool.sem_inc(hlo_ok, PRIME)
            norm.deviation(pool, 0)
            with pool.Fori(0, TRIPS) as it:
                for par in range(PAIRS):
                    b = it * PAIRS + par
                    for u in range(UNITS):
                        h_low(u % 2, u, b)
                        if u == 0:
                            norm.deviation(pool, b + 1)

        @block.scalar
        def _(act):
            def silu(slot, u, n):
                k = n * UNITS + u
                act.wait_ge(gu_done, k + 1)
                act.wait_ge(h_ok, k - 1 + PRIME)
                act.activation(sg[:, slot], pG[:, slot], ACT.Silu,
                               scale=1.0 / (X_SCALE * W_SCALE)).then_inc(silu_done, 1)

            def h_high(slot, u, n):
                act.wait_ge(h_ok, n * UNITS + u + 1 + PRIME)
                if u == 0:
                    act.wait_ge(down_done, n * ST + PRIME)
                act.activation(hp[:, 0, 2 * u:2 * u + 2, :], h32[:, slot], ACT.Copy).then_inc(hhi_ok, 1)

            def hid_high(n):
                act.wait_ge(norm.xn_ok, n + 1)
                hid.high(act, norm.xn[:, :, :])

            act.sem_inc(silu_done, PRIME)
            for m in range(MATS):
                act.wait_ge(stage_in[m % 2], 16 * (m // 2 + 1))
                act.activation(pair_of(m)[:, 0], stage[:, m % 2], ACT.Copy, scale=W_SCALE).then_inc(whi_ok, 1)
                if m == 0:
                    hid_high(0)
                if m == 1:
                    for half in range(2):
                        hid.out(act, half, pT[:, half], 0, 0)
            with act.Fori(0, TRIPS) as it:
                for par in range(PAIRS):
                    b = it * PAIRS + par
                    for u in range(UNITS):
                        silu(u % 2, u, b)
                        h_high(u % 2, u, b)
                        if u == 1:
                            hid_high(b + 1)
                        if u == 4:
                            for half in range(2):
                                hid.out(act, half, pT[:, half], 1 - par, b + 1)

        @block.vector
        def _(dve):
            def gated(slot, u, n):
                k = n * UNITS + u
                dve.wait_ge(silu_done, k + 1 + PRIME)
                dve.wait_ge(hlo_ok, k - 1 + PRIME)
                dve.scalar_tensor_tensor(h32[:, slot], pU[:, slot], H_SCALE / (X_SCALE * W_SCALE), sg[:, slot],
                                         ALU.mult, ALU.mult).then_inc(h_ok, 1)

            def update(tile, st, n):
                dve.wait_ge(down_done, n * ST + st + 1 + PRIME)
                dve.wait_ge(gs_ok, 1)
                xt = x[:, tile + st, :]
                dve.scalar_tensor_tensor(xt, pD[:, st], gscale[:, :], xt, ALU.mult, ALU.add).then_inc(x_ok, 1)

            dve.sem_inc(h_ok, PRIME)
            dve.sem_inc(x_ok, PRIME)
            norm.statistics(dve, 0, 0)
            dve.tensor_scalar(gscale[:, :], t["tanh_g"][:, 3:4], 1.0 / (H_SCALE * W_SCALE), None,
                              ALU.mult).then_inc(gs_ok, 1)
            norm.normalise(dve, 0, 0)
            for m in range(MATS):
                dve.wait_ge(whi_ok, m + 1)
                dve.scalar_tensor_tensor(pair_of(m)[:, 1], stage[:, m % 2], W_SCALE, pair_of(m)[:, 0],
                                         ALU.mult, ALU.subtract).then_inc(wlo_ok, 1)
                if m == 0:
                    hid.low(dve, norm.xn[:, :, :], 0)
            with dve.Fori(0, TRIPS) as it:
                for par in range(PAIRS):
                    b = it * PAIRS + par
                    ahead = ((b + 1) * ST) % TILES
                    for u in range(UNITS):
                        gated(u % 2, u, b)
                        if u == 0:
                            norm.statistics(dve, ahead, b + 1)
                            norm.normalise(dve, ahead, b + 1)
                        if u == 2:
                            hid.low(dve, norm.xn[:, :, :], b + 1)
                    for st in range(ST):
                        update(b * ST, st, b)

        @block.tensor
        def _(pe):
            def gate_up(par, slot, u, n):
                k = n * UNITS + u
                pe.wait_ge(silu_done, k - 1 + PRIME)
                pe.wait_ge(h_ok, k - 1 + PRIME)
                for psum, part in ((pG, 0), (pU, FM)):
                    for c in range(2):
                        chunk = 2 * u + c
                        m, at = part + chunk // KC, chunk % KC * P
                        i = 0
                        for kc in range(KC):
                            for a, w in PRODUCTS:
                                ins = pe.matmul(psum[:, slot, c], w_gu[:, m, w, kc, at:at + P],
                                                hid.cols[:, par, a, kc, :], start=(i == 0),
                                                stop=(i == KC * len(PRODUCTS) - 1))
                                i += 1
                ins.then_inc(gu_done, 1)

            def down(st, n):
                pe.wait_ge(x_ok, n * ST + st - 1 + PRIME)
                i, last = 0, FC * len(PRODUCTS) - 1
                for chunk in range(FC):
                    for a, w in PRODUCTS:
                        ins = pe.matmul(pD[:, st], hp[:, a, chunk, st * P:(st + 1) * P],
                                        w_d[:, chunk // KC, w, chunk % KC, :], start=(i == 0), stop=(i == last))
                        i += 1
                ins.then_inc(down_done, 1)

            pe.sem_inc(down_done, PRIME)
            pe.wait_ge(hid.lo_ok, 1)
            for half in range(2):
                hid.turn(pe, half, pT[:, half], ident)
            with pe.Fori(0, TRIPS) as it:
                for par in range(PAIRS):
                    b = it * PAIRS + par
                    pe.wait_ge(hid.cols_ok, 2 * b + 2)
                    pe.wait_ge(wlo_ok, MATS)
                    for u in range(UNITS):
                        gate_up(par, u % 2, u, b)
                        if u == 3:
                            pe.wait_ge(hid.lo_ok, b + 2)
                            for half in range(2):
                                hid.turn(pe, half, pT[:, half], ident)
                    pe.wait_ge(hlo_ok, (b + 1) * UNITS + PRIME)
                    for st in range(ST):
                        down(st, b)


def program(nc, a, out, debug_phase=None):
    with ExitStack() as mem:
        def sb(name, shape, dt):
            return mem.enter_context(nc.sbuf_tensor(name, shape, dt))

        def sem(name):
            return mem.enter_context(nc.semaphore(name))

        t = {}
        t["x"] = x = sb("x", [P, TILES, E], F32)
        t["w_e"] = sb("w_e", [P, NE, 2, KC, E], F16)
        t["stage"] = sb("stage", [P, 2, KC, E], F32)
        t["ident"] = sb("ident", [P, P], F16)
        t["g_raw"] = sb("g_raw", [P, 4], F32)
        t["norm_consts"] = sb("norm_consts", [P, len(NORM_CONSTS)], F32)
        t["tanh_g"] = sb("tanh_g", [P, 4], F32)
        for name in ("ident_in", "gates_in", "gates_ok", "kzero", "kconst"):
            t[name] = sem(name)
        t["ctx_d"] = a["ctx_512"].rearrange("b (c p) l -> p b c l", p=P)
        t["x_d"] = a["x"].rearrange("b (s p) e -> p (b s) e", p=P)
        t["expert_d"] = a["L0_ffn_expert_w"].rearrange("e (k p) d -> p e k d", p=P)
        nc.scalar.dma_start(t["ident"][:, :], a["ident"]).then_inc(t["ident_in"], 16)
        nc.scalar.dma_start(t["g_raw"][:, 0:2], a["g_xattn"].partition_broadcast(P)).then_inc(t["gates_in"], 16)
        nc.scalar.dma_start(t["g_raw"][:, 2:4], a["g_ffn"].partition_broadcast(P)).then_inc(t["gates_in"], 16)
        t["sel_d"], t["router_d"] = a["sel"], a["L0_ffn_router_w"].rearrange("(k p) e -> p k e", p=P)
        t["ramp_d"] = a["ramp"]
        t["expert_b_d"] = a["L0_ffn_expert_b"]
        t["out_b_d"] = a["L0_ffn_out_b"].rearrange("(a n) -> a n", a=1)
        t["router_b_d"] = a["L0_ffn_router_b"].rearrange("(a n) -> a n", a=1)
        t["small_d"] = a["small"].rearrange("m (k p) n -> p m k n", p=P)
        for name in ("big_ident", "mask_row", "mask_key"):
            t[name + "_d"] = a[name]
        t["gu_d"] = a["gate_up"].rearrange("(k p) (m n) -> p m k n", p=P, n=E)
        t["down_d"] = a["down"].rearrange("(m k p) n -> p m k n", k=KC, p=P)
        out_sent = sem("out_sent")
        with ExitStack() as pm:
            phase_attention0(nc, pm, t)
        if debug_phase is None or debug_phase > 1:
            t["w_small"] = sb("w_small", [P, 4, 2, KC, E], F16)
            with ExitStack() as pm:
                phase_experts(nc, pm, t)
        if debug_phase is None or debug_phase > 2:
            with ExitStack() as pm:
                phase_attention1(nc, pm, t)
        if debug_phase is None or debug_phase > 3:
            t["w_d"] = sb("w_d", [P, FM, 2, KC, E], F16)
            with ExitStack() as pm:
                phase_feed_forward(nc, pm, t, out.rearrange("b (s p) e -> p (b s) e", p=P))
            return
        if debug_phase:
            with nc.Block() as block:
                @block.sync
                def _(sp):
                    sp.dma_start(out.rearrange("b (s p) e -> p (b s) e", p=P), x[:, :, :]).then_inc(out_sent, 16)
                    sp.wait_ge(out_sent, 16)
            return


def kernel(_debug=None, **inputs):
    import numpy as np
    import concourse.bacc as bacc
    from concourse.bass_utils import run_bass_kernel_spmd

    nc = bacc.Bacc("TRN2", target_bir_lowering=False, num_devices=1)
    arrays = {k: np.ascontiguousarray(v) for k, v in inputs.items()}
    arrays["ident"] = np.eye(P, dtype=np.float16)
    arrays["ramp"] = np.arange(NE, 0, -1, dtype=np.float32)
    sel = np.zeros((P, BIAS_ROWS, P), np.float16)
    for r in range(BIAS_ROWS):
        sel[[r, BIAS_LOW + r], r, :] = C_SCALE if r == BIAS_OUT else X_SCALE
    arrays["sel"] = sel
    small = np.zeros((4, E, E), np.float32)
    small[0] = arrays.pop("L0_ffn_out_w")
    small[1] = arrays.pop("L1_xattn_Wq").T
    small[2] = arrays.pop("L1_xattn_Wout").T
    small[3].reshape(KC, P, E)[0:2] = arrays.pop("L1_xattn_Wkv_expand").T.reshape(P, 2, E).transpose(1, 0, 2)
    arrays["small"] = small
    arrays["gate_up"] = np.ascontiguousarray(arrays.pop("L1_ffn_w_gate_up").T)
    arrays["down"] = np.ascontiguousarray(arrays.pop("L1_ffn_w_down").T)
    arrays["big_ident"] = (MASK * np.eye(P)).astype(np.float16)
    later = np.triu(np.ones((P, P)), 1)
    arrays["mask_row"] = (-MASK * later).astype(np.float16)
    arrays["mask_key"] = (-MASK * later.T).astype(np.float16)
    aps = {k: nc.dram_tensor("in_" + k, v.shape, mybir.dt.from_np(v.dtype), kind="ExternalInput").ap()
           for k, v in arrays.items()}
    out = nc.dram_tensor("out", (B, S, E), F32, kind="ExternalOutput").ap()
    program(nc, aps, out, _debug)
    r = run_bass_kernel_spmd(nc, [{"in_" + k: v for k, v in arrays.items()}], core_ids=[0])
    return r.results[0]["out"]
```

```python
from contextlib import ExitStack

import concourse.bass as bass
from concourse import mybir

P = 128
F32 = mybir.dt.float32
F16 = mybir.dt.float16
ALU = mybir.AluOpType
ACT = mybir.ActivationFunctionType
AX = mybir.AxisListType

B, S, E, L = 8, 256, 512, 128
TILES = B * S // P
ST = S // P
KC = E // P
EPS = 1e-5

X_SCALE = 512.0
W_SCALE = 256.0
M_SCALE = 4096.0
LIFT0 = 887.0

H0, KV0, D0 = 32, 8, 16
G0 = H0 // KV0
R0 = 64
EXTRA0 = R0 + 3 * D0
V0 = D0 + 1
PAIRS = 2
X_LOAD = 7


class Norm:

    STEPS = 6

    def __init__(self, nc, mem, t):
        def sb(name, shape, dt):
            return mem.enter_context(nc.sbuf_tensor(f"norm_{name}", shape, dt))

        def sem(name):
            return mem.enter_context(nc.semaphore(f"norm_{name}"))

        self.base = 0
        self.x, self.consts = t["x"], t["norm_consts"]
        self.bn = sb("bn", [P, ST, 6], F32)
        self.tmp = sb("tmp", [P, 4, ST], F32)
        self.mean = sb("mean", [P, ST], F32)
        self.rstd = sb("rstd", [P, ST], F32)
        self.xn = sb("xn", [P, ST, E], F32)
        self.bn_ok, self.chain, self.xn_ok = sem("bn_ok"), sem("chain"), sem("xn_ok")

    def const(self, k):
        return self.consts[:, k:k + 1].to_broadcast([P, ST])

    def statistics(self, dve, tile, n):
        for st in range(ST):
            ins = dve.bn_stats(self.bn[:, st, :], self.x[:, tile + st, :])
        ins.then_inc(self.bn_ok, 1)

    def deviation(self, pool, n):
        bn, tmp, chain, at = self.bn, self.tmp, self.chain, self.STEPS * (self.base + n)
        pool.wait_ge(self.bn_ok, self.base + n + 1)
        pool.tensor_tensor(self.mean[:, :], bn[:, :, 1], bn[:, :, 4], ALU.add)
        pool.tensor_tensor(tmp[:, 0], bn[:, :, 1], bn[:, :, 4], ALU.subtract)
        pool.tensor_tensor(tmp[:, 1], bn[:, :, 2], bn[:, :, 5], ALU.add).then_inc(chain, 1)
        pool.wait_ge(chain, at + 1)
        pool.tensor_tensor(self.mean[:, :], self.mean[:, :], self.const(0), ALU.mult)
        pool.tensor_tensor(tmp[:, 2], tmp[:, 0], tmp[:, 0], ALU.mult)
        pool.tensor_tensor(tmp[:, 1], tmp[:, 1], self.const(1), ALU.mult).then_inc(chain, 1)
        pool.wait_ge(chain, at + 2)
        pool.tensor_tensor(tmp[:, 3], tmp[:, 1], tmp[:, 2], ALU.add).then_inc(chain, 1)
        pool.wait_ge(chain, at + 3)
        pool.tensor_tensor(tmp[:, 0], tmp[:, 3], self.const(2), ALU.add).then_inc(chain, 1)
        pool.wait_ge(chain, at + 4)
        pool.tensor_tensor(tmp[:, 1], tmp[:, 0], self.const(3), ALU.pow).then_inc(chain, 1)
        pool.wait_ge(chain, at + 5)
        pool.tensor_tensor(self.rstd[:, :], tmp[:, 1], self.const(4), ALU.mult).then_inc(chain, 1)

    def normalise(self, dve, tile, n):
        dve.wait_ge(self.chain, self.STEPS * (self.base + n + 1))
        for st in range(ST):
            ins = dve.tensor_scalar(self.xn[:, st, :], self.x[:, tile + st, :], self.mean[:, st:st + 1],
                                    self.rstd[:, st:st + 1], ALU.subtract, ALU.mult)
        ins.then_inc(self.xn_ok, 1)

    def made(self, n):
        return self.base + n + 1


class Split:

    def __init__(self, nc, mem, tag, slots):
        def sem(name):
            return mem.enter_context(nc.semaphore(f"{tag}_{name}"))

        self.rows = mem.enter_context(nc.sbuf_tensor(f"{tag}_rows", [P, 2, ST, E], F16))
        self.cols = mem.enter_context(nc.sbuf_tensor(f"{tag}_cols", [P, slots, 2, KC, S], F16))
        self.hi_ok, self.lo_ok = sem("hi_ok"), sem("lo_ok")
        self.turned, self.cols_ok = sem("turned"), sem("cols_ok")

    def high(self, act, src):
        act.activation(self.rows[:, 0], src, ACT.Copy).then_inc(self.hi_ok, 1)

    def low(self, dve, src, n):
        dve.wait_ge(self.hi_ok, n + 1)
        dve.tensor_tensor(self.rows[:, 1], src, self.rows[:, 0], ALU.subtract).then_inc(self.lo_ok, 1)

    def turn(self, pe, half, psum, ident):
        for k in range(KC):
            for st in range(ST):
                ins = pe.transpose(psum[:, k, st * P:(st + 1) * P], self.rows[:, half, st, k * P:(k + 1) * P],
                                   ident[:, :])
        ins.then_inc(self.turned, 1)

    def out(self, act, half, psum, par, n):
        act.wait_ge(self.turned, 2 * n + half + 1)
        act.activation(self.cols[:, par, half], psum, ACT.Copy).then_inc(self.cols_ok, 1)


PRODUCTS = ((0, 0), (1, 0), (0, 1))


def project(pe, psum, cols, par, st, weights, k_chunks=KC, more=False):
    last = len(PRODUCTS) * k_chunks - 1
    i = 0
    for k in range(k_chunks):
        for a, b in PRODUCTS:
            ins = pe.matmul(psum, cols[:, par, a, k, st * P:(st + 1) * P], weights[:, b, k, :],
                            start=(i == 0), stop=(i == last and not more))
            i += 1
    return ins


NORM_CONSTS = (0.5, 4.0 / E, 4.0 * EPS, -0.5, 2.0 * X_SCALE)


def phase_attention0(nc, mem, t):
    x, w_e, stage, ident, gates = t["x"], t["w_e"], t["stage"], t["ident"], t["tanh_g"]
    ctx_d, x_d, expert_d = t["ctx_d"], t["x_d"], t["expert_d"]
    GPB = KV0
    NG = PAIRS * GPB
    TRIPS = B // PAIRS
    SLOTS = 4
    LAG = 2

    def sb(name, shape, dt):
        return mem.enter_context(nc.sbuf_tensor("a0_" + name, shape, dt))

    def sem(name):
        return mem.enter_context(nc.semaphore("a0_" + name))

    wscale = sb("wscale", [P, 1], F32)
    ctx = sb("ctx", [P, PAIRS, ST, L], F32)
    norm = t["norm"]
    xn = norm.xn
    qst = sb("qst", [P, PAIRS, ST, H0, R0], F16)
    kst = sb("kst", [P, ST, KV0, 2, 2 * R0], F16)
    kT = sb("kT", [P, 2, KV0, S], F16)
    extras = qst[:, :, :, :, :].rearrange("p a s (m r) c -> p a s m (r c)", r=2)
    extras = extras[:, :, :, :, EXTRA0:EXTRA0 + 6].rearrange("p a s (g j) (r k) -> p a s g j r k", j=2, r=2)
    vst = sb("vst", [P, PAIRS, ST, KV0, 2, V0], F16)
    qT1 = sb("qT1", [P, 2, 2, S], F16)
    qT2 = sb("qT2", [P, 2, 2, S], F16)
    p32 = sb("p32", [P, ST, 2, 2, S], F32)
    p_hi = sb("p_hi", [P, SLOTS * ST, 2, 2, S], F16)
    p_lo = sb("p_lo", [P, SLOTS * ST, 2, 2, S], F16)
    negm = sb("negm", [P, 2, ST, 2, 2], F32)
    oall = sb("oall", [P, PAIRS, ST, H0, V0], F32)
    rec = sb("rec", [P, ST, H0], F32)

    pS2 = mem.enter_context(nc.psum_tensor("a0_pS2", [P, 2, 2, 2, S], F32))
    pS1 = mem.enter_context(nc.psum_tensor("a0_pS1", [P, 2, 2, S], F32))
    pT = mem.enter_context(nc.psum_tensor("a0_pT", [P, 4, S], F16))
    pO = mem.enter_context(nc.psum_tensor("a0_pO", [P, 512], F32))
    o_ps = pO[:, 0:ST * G0 * V0].rearrange("p (s h d) -> p s h d", s=ST, h=G0)

    x0_in, x_in = sem("x0_in"), sem("x_in")
    ctx_in = [sem(f"ctx{par}_in") for par in range(PAIRS)]
    stage_in = [sem(f"stage{par}_in") for par in range(PAIRS)]
    const_set, qzero = sem("const_set"), sem("qzero")
    v_ok = sem("v_ok")
    qhi_ok, qlo_ok, khi_ok, klo_ok = sem("qhi_ok"), sem("qlo_ok"), sem("khi_ok"), sem("klo_ok")
    t1_done, t2_done, tk_done = sem("t1_done"), sem("t2_done"), sem("tk_done")
    qT1_ok, qT2_ok, kT_ok = sem("qT1_ok"), sem("qT2_ok"), sem("kT_ok")
    s1_done, max_ok, mhi_ok, m_ok = sem("s1_done"), sem("max_ok"), sem("mhi_ok"), sem("m_ok")
    s2_done, exp_done = sem("s2_done"), sem("exp_done")
    plo_ok = [sem(f"plo{c}_ok") for c in range(ST)]
    v256_ok, vhi_ok, zeroed = sem("v256_ok"), sem("vhi_ok"), sem("zeroed")
    bias_zero = sem("bias_zero")
    pv_done, o_ok = sem("pv_done"), sem("o_ok")
    rec0_ok, rec_ok, inc_ok, x_ok = sem("rec0_ok"), sem("rec_ok"), sem("inc_ok"), sem("x_ok")
    lag_set = sem("lag_set")
    whi_ok, wscaled, wlo_ok = sem("whi_ok"), sem("wscaled"), sem("wlo_ok")
    PRIME_EXP, PRIME_PV, PRIME_O, PRIME_INC, PRIME_W, PRIME_LO, PRIME_X = 2, LAG, 1, 1, 2, LAG, 1

    with nc.Block() as block:

        @block.sync
        def _(sp):
            def load_ctx(b, par):
                sp.dma_start(ctx[:, par], ctx_d[:, b]).then_inc(ctx_in[par], 16)

            load_ctx(0, 0)
            sp.dma_start(x[:, 0:ST, :], x_d[:, 0:ST, :]).then_inc(x0_in, 16)
            load_ctx(1, 1)
            for n in range(ST, TILES, X_LOAD):
                sp.dma_start(x[:, n:n + X_LOAD, :], x_d[:, n:n + X_LOAD, :]).then_inc(x_in, 16)
            sp.dma_start(t["rw_raw"][:, :, :], t["router_d"]).then_inc(t["consts_in"], 16)
            sp.dma_start(t["ramp"][:, :], t["ramp_d"].partition_broadcast(P)).then_inc(t["consts_in"], 16)
            sp.wait_ge(bias_zero, 1)
            for row in (0, BIAS_LOW):
                sp.dma_start(t["bias_raw"][row:row + NE, :], t["expert_b_d"]).then_inc(t["consts_in"], 16)
                sp.dma_start(t["bias_raw"][row + BIAS_OUT:row + BIAS_OUT + 1, :], t["out_b_d"]).then_inc(t["consts_in"], 16)
                sp.dma_start(t["bias_raw"][row + BIAS_ROUTER:row + BIAS_ROUTER + 1, 0:NE],
                             t["router_b_d"]).then_inc(t["consts_in"], 16)
            with sp.Fori(0, TRIPS) as it:
                for par in range(PAIRS):
                    sp.wait_ge(wlo_ok, it * PAIRS + par + 1)
                    sp.dma_start(stage[:, par], expert_d[:, it * PAIRS + par]).then_inc(stage_in[par], 16)
                for par in range(PAIRS):
                    sp.wait_ge(klo_ok, it * PAIRS + par + 1)
                    sp.wait_ge(v_ok, it * PAIRS + par + 1)
                    load_ctx((it * PAIRS + PAIRS + par) % B, par)
            for par in range(PAIRS):
                sp.wait_ge(ctx_in[par], 16 * (TRIPS + 1))
            sp.wait_ge(t["consts_in"], 8 * 16)

        @block.gpsimd
        def _(pool):
            def values(par, n, loads):
                pool.wait_ge(ctx_in[par], 16 * loads)
                pool.wait_ge(pv_done, (n - 1) * GPB + LAG + PRIME_PV)
                pool.wait_ge(const_set, 5)
                v_high_low(par, n)

            def v_high_low(par, n):
                src = ctx[:, par].rearrange("p c (g d) -> p (c g) d", d=D0)
                dst = vst[:, par].rearrange("p c g a d -> p (c g) a d")
                scale = wscale[:, :].unsqueeze(2).to_broadcast([P, ST * KV0, D0])
                pool.tensor_tensor(dst[:, :, 0, 0:D0], src, scale, ALU.mult).then_inc(vhi_ok, 1)
                pool.wait_ge(vhi_ok, n + 1)
                pool.wait_ge(klo_ok, n + 1)
                pool.tensor_tensor(src, src, scale, ALU.mult).then_inc(v256_ok, 1)
                pool.wait_ge(v256_ok, n + 1)
                pool.tensor_tensor(dst[:, :, 1, 0:D0], src, dst[:, :, 0, 0:D0],
                                   ALU.subtract).then_inc(v_ok, 1)

            def p_low(slot, n):
                pool.wait_ge(exp_done, n * 2 + 2 + PRIME_EXP)
                pool.tensor_tensor(p_lo[:, 2 * slot + 1], p32[:, 1], p_hi[:, 2 * slot + 1],
                                   ALU.subtract).then_inc(plo_ok[1], 1)

            def divide(par, n):
                pool.wait_ge(rec_ok, n + 1)
                ob = oall[:, par, :, :, 0:D0]
                pool.tensor_tensor(ob, ob, rec[:, :, :].unsqueeze(3).to_broadcast([P, ST, H0, D0]),
                                   ALU.mult).then_inc(inc_ok, 1)

            def add_to_x(par, tile, n):
                pool.wait_ge(inc_ok, n + 1 + PRIME_INC)
                pool.wait_ge(x_in, 16 * (TILES - ST) // X_LOAD)
                xb = x[:, bass.ds(tile, ST), :].rearrange("p s (h d) -> p s h d", d=D0)
                pool.tensor_tensor(xb, xb, oall[:, par, :, :, 0:D0], ALU.add).then_inc(x_ok, 1)

            def split_low(par, e, n, k):
                pool.wait_ge(whi_ok, 2 * n + k // 2 + 1)
                pool.tensor_tensor(stage[:, par, k], stage[:, par, k], wscale[:, :].to_broadcast([P, E]),
                                   ALU.mult).then_inc(wscaled, 1)
                pool.wait_ge(wscaled, KC * n + k + 1)
                ins = pool.tensor_tensor(w_e[:, e, 1, k], stage[:, par, k], w_e[:, e, 0, k], ALU.subtract)
                if k == KC - 1:
                    ins.then_inc(wlo_ok, 1)

            pool.sem_inc(wlo_ok, PRIME_W)
            pool.sem_inc(inc_ok, PRIME_INC)
            pool.sem_inc(x_ok, PRIME_X)
            pool.sem_inc(plo_ok[1], PRIME_LO)
            for k, value in enumerate(NORM_CONSTS):
                ins = pool.memset(norm.consts[:, k:k + 1], value)
            ins.then_inc(const_set, 1)
            pool.memset(wscale[:, :], W_SCALE).then_inc(const_set, 1)
            pool.memset(vst[:, :, :, :, :, :], 0.0).then_inc(zeroed, 1)
            pool.wait_ge(zeroed, 1)
            pool.memset(vst[:, :, :, :, 0, D0:D0 + 1], 1.0).then_inc(const_set, 1)
            pool.memset(qst[:, :, :, :, 3 * D0:], 0.0).then_inc(qzero, 1)
            pool.wait_ge(qzero, 1)
            pool.memset(extras[:, :, :, :, :, :, 2], LIFT0).then_inc(const_set, 2)
            pool.wait_ge(const_set, 5)
            norm.deviation(pool, 0)
            pool.wait_ge(ctx_in[0], 16)
            v_high_low(0, 0)
            pool.memset(t["bias_raw"][:, :], 0.0).then_inc(bias_zero, 1)
            pool.memset(p_hi[:, (SLOTS - LAG) * ST:], 1.0)
            pool.memset(p_lo[:, (SLOTS - LAG) * ST:], 0.0)
            pool.memset(oall[:, :, :, :, 0:D0], 0.0)
            pool.memset(oall[:, :, :, :, D0:D0 + 1], 1.0).then_inc(lag_set, 1)
            with pool.Fori(0, TRIPS) as it:
                for i in range(NG):
                    par, j = divmod(i, GPB)
                    g, b = it * NG + i, it * PAIRS + par
                    if j == 0:
                        norm.deviation(pool, b + 1)
                    p_low(i % SLOTS, g)
                    if j in (1, 3, 6, 7):
                        split_low(par, b, b, (1, 3, 6, 7).index(j))
                    if j == 2:
                        divide(1 - par, b)
                    if j == 4:
                        values(1 - par, b + 1, it + 1 + par)
                    if j == 5:
                        add_to_x(1 - par, ((b - 1) * ST + TILES) % TILES, b)
            divide(1, B)
            add_to_x(1, (B - 1) * ST, B)

        @block.scalar
        def _(act):
            def q_high(par, n):
                act.wait_ge(norm.xn_ok, norm.made(n))
                for st in range(ST):
                    for a in (0, 2):
                        ins = act.activation(qst[:, par, st, :, a * D0:(a + 1) * D0],
                                             xn[:, st, :].rearrange("p (h d) -> p h d", d=D0), ACT.Copy)
                ins.then_inc(qhi_ok, 1)

            def k_high(par, n, loads):
                act.wait_ge(ctx_in[par], 16 * loads)
                src = ctx[:, par].rearrange("p c (g d) -> p c g d", d=D0)
                for r in range(2):
                    for base in (R0 * r, R0 * r + D0):
                        ins = act.activation(kst[:, :, :, r, base:base + D0], src, ACT.Copy, scale=W_SCALE)
                ins.then_inc(khi_ok, 1)

            def k_out(half, r, n):
                act.wait_ge(tk_done, n + 1)
                act.activation(kT[:, r, 4 * half:4 * half + 4, :], pT[:, :, :], ACT.Copy).then_inc(kT_ok, 1)

            def q2_out(slot, n):
                act.wait_ge(t2_done, n + 1)
                act.activation(qT2[:, slot], pT[:, 0:2, :], ACT.Copy).then_inc(qT2_ok, 1)

            def exps(slot, c, n):
                act.wait_ge(s2_done, n * 2 + c + 1)
                if c == 0:
                    act.wait_ge(pv_done, n - SLOTS + 1 + LAG + PRIME_PV)
                scale = D0 ** -0.5 / (X_SCALE * W_SCALE)
                act.activation(p_hi[:, 2 * slot + c], pS2[:, c], ACT.Exp, scale=scale)
                act.wait_ge(plo_ok[c], n + PRIME_LO)
                act.activation(p32[:, c], pS2[:, c], ACT.Exp, scale=scale).then_inc(exp_done, 1)

            def split_high(par, e, it, half):
                act.wait_ge(stage_in[par], it * 16 + 16)
                act.wait_ge(const_set, 5)
                rows = slice(2 * half, 2 * half + 2)
                act.activation(w_e[:, e, 0, rows], stage[:, par, rows], ACT.Copy,
                               scale=W_SCALE).then_inc(whi_ok, 1)

            act.sem_inc(exp_done, PRIME_EXP)
            act.wait_ge(const_set, 5)
            act.wait_ge(t["gates_in"], 32)
            act.activation(gates[:, :], t["g_raw"][:, :], ACT.Tanh).then_inc(t["gates_ok"], 1)
            act.wait_ge(t["kconst"], 1)
            k_high(0, 0, 1)
            q_high(0, 0)
            k_out(0, 0, 0)
            k_out(0, 1, 1)
            q2_out(0, 0)
            act.wait_ge(lag_set, 1)
            with act.Fori(0, TRIPS) as it:
                for i in range(NG):
                    par, j = divmod(i, GPB)
                    g, b = it * NG + i, it * PAIRS + par
                    exps(i % SLOTS, 0, g)
                    q2_out((i + 1) % 2, g + 1)
                    exps(i % SLOTS, 1, g)
                    if j in (0, 1):
                        k_out(1, j, 4 * b + 2 + j)
                    if j == 0:
                        split_high(par, b, it, 0)
                    if j == 1:
                        k_high(1 - par, b + 1, it + 1 + par)
                    if j == 2:
                        q_high(1 - par, b + 1)
                    if j in (4, 5):
                        k_out(0, j - 4, 4 * (b + 1) + j - 4)
                    if j == 5:
                        split_high(par, b, it, 1)

        @block.vector
        def _(dve):
            def q_low(par, n):
                dve.wait_ge(qhi_ok, n + 1)
                for st in range(ST):
                    ins = dve.tensor_tensor(qst[:, par, st, :, D0:2 * D0],
                                            xn[:, st, :].rearrange("p (h d) -> p h d", d=D0),
                                            qst[:, par, st, :, 0:D0], ALU.subtract)
                ins.then_inc(qlo_ok, 1)

            def k_low(par, n):
                dve.wait_ge(khi_ok, n + 1)
                src = ctx[:, par].rearrange("p c (g d) -> p (c g) d", d=D0)
                for r in range(2):
                    flat = kst[:, :, :, r, :].rearrange("p c g n -> p (c g) n")
                    base = R0 * r
                    ins = dve.scalar_tensor_tensor(flat[:, :, base + 2 * D0:base + 3 * D0], src, W_SCALE,
                                                   flat[:, :, base:base + D0], ALU.mult, ALU.subtract)
                ins.then_inc(klo_ok, 1)

            def p_low(slot, n):
                dve.wait_ge(exp_done, n * 2 + 1 + PRIME_EXP)
                dve.tensor_tensor(p_lo[:, 2 * slot], p32[:, 0], p_hi[:, 2 * slot],
                                  ALU.subtract).then_inc(plo_ok[0], 1)

            def q1_out(slot, n):
                dve.wait_ge(t1_done, n + 1)
                dve.tensor_copy(qT1[:, slot], pT[:, 0:2, :]).then_inc(qT1_ok, 1)

            def row_max(st, n, slot):
                for r in range(2):
                    dve.wait_ge(s1_done, n * 4 + 2 * st + r + 1)
                    dve.tensor_reduce(negm[:, slot, st, r], pS1[:, r], AX.X, ALU.max, negate=True).then_inc(max_ok, 1)

            def put_max(par, g, n, slot):
                dve.wait_ge(max_ok, n * 4 + 4)
                for st in range(ST):
                    to = extras[:, par, st, g, :, :, 0].rearrange("p j r -> p r j")
                    ins = dve.tensor_scalar(to, negm[:, slot, st], 1.0 / M_SCALE, None, ALU.mult)
                ins.then_inc(mhi_ok, 1)
                dve.wait_ge(mhi_ok, n + 1)
                for st in range(ST):
                    hi = extras[:, par, st, g, :, :, 0].rearrange("p j r -> p r j")
                    to = extras[:, par, st, g, :, :, 1].rearrange("p j r -> p r j")
                    ins = dve.scalar_tensor_tensor(to, negm[:, slot, st], 1.0 / M_SCALE, hi, ALU.mult, ALU.subtract)
                ins.then_inc(m_ok, 1)

            def o_out(par, g, n):
                dve.wait_ge(pv_done, n + 1 + PRIME_PV)
                dve.tensor_copy(oall[:, par, :, G0 * g:G0 * g + G0, :], o_ps).then_inc(o_ok, 1)

            def row_sums(par, n):
                dve.wait_ge(o_ok, n * GPB + LAG + PRIME_O)
                dve.wait_ge(inc_ok, n + PRIME_INC)
                dve.reciprocal(rec[:, :, :], oall[:, par, :, :, D0]).then_inc(rec0_ok, 1)
                dve.wait_ge(rec0_ok, n + 1)
                dve.tensor_scalar(rec[:, :, :], rec[:, :, :], gates[:, 0:1], 1.0 / W_SCALE, ALU.mult, ALU.mult).then_inc(rec_ok, 1)

            dve.sem_inc(o_ok, PRIME_O)
            dve.sem_inc(plo_ok[0], PRIME_LO)
            dve.memset(kst[:, :, :, :, :], 0.0).then_inc(t["kzero"], 1)
            dve.wait_ge(t["kzero"], 1)
            for r in range(2):
                ins = dve.memset(kst[:, :, :, r, EXTRA0 + 3 * r:EXTRA0 + 3 * r + 3], M_SCALE)
            ins.then_inc(t["kconst"], 1)
            dve.wait_ge(x0_in, 16)
            norm.statistics(dve, 0, 0)
            norm.normalise(dve, 0, 0)
            dve.wait_ge(t["gates_ok"], 1)
            k_low(0, 0)
            q_low(0, 0)
            q1_out(0, 0)
            q1_out(1, 1)
            row_max(0, 0, 0)
            row_max(1, 0, 0)
            put_max(0, 0, 0, 0)
            q1_out(0, 2)
            row_max(0, 1, 1)
            row_max(1, 1, 1)
            put_max(0, 1, 1, 1)
            dve.wait_ge(x_in, 16 * (TILES - ST) // X_LOAD)
            dve.wait_ge(lag_set, 1)
            with dve.Fori(0, TRIPS) as it:
                for i in range(NG):
                    par, j = divmod(i, GPB)
                    g, b = it * NG + i, it * PAIRS + par
                    if j == LAG:
                        dve.wait_ge(x_ok, b + PRIME_X)
                    o_out((i - LAG) // GPB % 2, (i - LAG) % GPB, g)
                    row_max(0, g + 2, i % 2)
                    row_max(1, g + 2, i % 2)
                    q1_out((i + 3) % 2, g + 3)
                    put_max((i + 2) // GPB % 2, (i + 2) % GPB, g + 2, i % 2)
                    p_low(i % SLOTS, g)
                    if j == 0:
                        norm.statistics(dve, ((b + 1) * ST) % TILES, b + 1)
                    if j == 1:
                        norm.normalise(dve, ((b + 1) * ST) % TILES, b + 1)
                        row_sums(1 - par, b)
                    if j == 2:
                        k_low(1 - par, b + 1)
                    if j == 3:
                        q_low(1 - par, b + 1)
            for n in range(LAG):
                o_out(1, GPB - LAG + n, B * GPB + n)
            row_sums(1, B)

        @block.tensor
        def _(pe):
            def keys(half, r):
                for g in range(4):
                    for c in range(ST):
                        ins = pe.transpose(pT[:, g, c * P:(c + 1) * P], kst[:, c, 4 * half + g, r, :], ident[:, :])
                ins.then_inc(tk_done, 1)

            def q_turn(par, g, done):
                for j in range(2):
                    for st in range(ST):
                        src = qst[:, par, st, G0 * g + 2 * j:G0 * g + 2 * j + 2, :].rearrange("p h r -> p (h r)")
                        ins = pe.transpose(pT[:, j, st * P:(st + 1) * P], src, ident[:, :])
                ins.then_inc(done, 1)

            def scores_by_row(slot, g, st, n):
                for r in range(2):
                    if not (isinstance(n, int) and n == 0 and st == 0):
                        pe.wait_ge(max_ok, 4 * n + 2 * st + r - 1)
                    for j in range(2):
                        ins = pe.matmul(pS1[:, r, j, :], qT1[0:EXTRA0, slot, j, st * P:(st + 1) * P],
                                        kT[0:EXTRA0, r, g, :], start=True, stop=True)
                    ins.then_inc(s1_done, 1)

            def scores_by_key(slot, g, c):
                for r in range(2):
                    ins = pe.matmul(pS2[:, c, r].rearrange("p j s -> p (j s)"), kT[:, r, g, c * P:(c + 1) * P],
                                    qT2[:, slot].rearrange("p j s -> p (j s)"), start=True, stop=True)
                ins.then_inc(s2_done, 1)

            def weigh(slot, par, g, n):
                pe.wait_ge(plo_ok[0], n + 1)
                pe.wait_ge(plo_ok[1], n + 1)
                pe.wait_ge(o_ok, n + PRIME_O)
                for st in range(ST):
                    for h in range(G0):
                        i = 0
                        for c in range(ST):
                            for a, v in PRODUCTS:
                                probs = (p_hi, p_lo)[a]
                                ins = pe.matmul(o_ps[:, st, h, :],
                                                probs[:, 2 * slot + c, h % 2, h // 2, st * P:(st + 1) * P],
                                                vst[:, par, c, g, v, :], start=(i == 0),
                                                stop=(i == ST * len(PRODUCTS) - 1))
                                i += 1
                ins.then_inc(pv_done, 1)

            pe.sem_inc(pv_done, PRIME_PV)
            pe.wait_ge(t["ident_in"], 16)
            pe.wait_ge(klo_ok, 1)
            keys(0, 0)
            pe.wait_ge(kT_ok, 1)
            keys(0, 1)
            pe.wait_ge(qlo_ok, 1)
            pe.wait_ge(kT_ok, 2)
            q_turn(0, 0, t1_done)
            pe.wait_ge(qT1_ok, 1)
            q_turn(0, 1, t1_done)
            pe.wait_ge(qT1_ok, 2)
            scores_by_row(0, 0, 0, 0)
            scores_by_row(0, 0, 1, 0)
            q_turn(0, 2, t1_done)
            scores_by_row(1, 1, 0, 1)
            scores_by_row(1, 1, 1, 1)
            pe.wait_ge(qT1_ok, 3)
            pe.wait_ge(m_ok, 1)
            q_turn(0, 0, t2_done)
            pe.wait_ge(lag_set, 1)
            with pe.Fori(0, TRIPS) as it:
                for i in range(NG):
                    par, j = divmod(i, GPB)
                    g, b = it * NG + i, it * PAIRS + par
                    pe.wait_ge(qT2_ok, g + 1)
                    pe.wait_ge(exp_done, 2 * g - 1 + PRIME_EXP)
                    scores_by_key(i % 2, j, 0)
                    if j == LAG:
                        pe.wait_ge(v_ok, b + 1)
                    weigh((i - LAG) % SLOTS, (i - LAG) // GPB % 2, (i - LAG) % GPB, g)
                    p1, g1 = (i + 1) // GPB % 2, (i + 1) % GPB
                    pe.wait_ge(m_ok, g + 2)
                    pe.wait_ge(qT1_ok, g + 3)
                    if j in (1, 2):
                        pe.wait_ge(kT_ok, 4 * b + 2 + j)
                    if j in (5, 6):
                        pe.wait_ge(kT_ok, 4 * (b + 1) + j - 4)
                    q_turn(p1, g1, t2_done)
                    g2 = (i + 2) % GPB
                    scores_by_row((i + 2) % 2, g2, 0, g + 2)
                    pe.wait_ge(exp_done, 2 * g + PRIME_EXP)
                    scores_by_key(i % 2, j, 1)
                    scores_by_row((i + 2) % 2, g2, 1, g + 2)
                    p3, g3 = (i + 3) // GPB % 2, (i + 3) % GPB
                    if g3 == 0:
                        pe.wait_ge(qlo_ok, b + 2)
                    pe.wait_ge(qT2_ok, g + 2)
                    q_turn(p3, g3, t1_done)
                    if j in (0, 1, 4, 5):
                        if j == 4:
                            pe.wait_ge(klo_ok, b + 2)
                        pe.wait_ge(qT1_ok, g + 4)
                        keys(1 - j // 4, j % 4)
            for n in range(LAG):
                weigh(SLOTS - LAG + n, 1, GPB - LAG + n, B * GPB + n)


BIAS_OUT, BIAS_ROUTER, BIAS_ROWS, BIAS_LOW = 8, 9, 10, 32
NE = 8
C_SCALE = 256.0


def phase_experts(nc, mem, t):
    x, w_e, stage, ident, w_small = t["x"], t["w_e"], t["stage"], t["ident"], t["w_small"]
    bias_raw, rw_raw, ramp, consts_in = t["bias_raw"], t["rw_raw"], t["ramp"], t["consts_in"]
    TRIPS = B // PAIRS
    UNITS = NE * ST
    RING = 4

    def sb(name, shape, dt):
        return mem.enter_context(nc.sbuf_tensor("m_" + name, shape, dt))

    def sem(name):
        return mem.enter_context(nc.semaphore("m_" + name))

    norm = t["norm"]
    norm.base = B
    hid = Split(nc, mem, "m_hid", PAIRS)
    com = Split(nc, mem, "m_com", 1)
    y = sb("y", [P, RING, E], F32)
    acc = sb("acc", [P, PAIRS, ST, E], F32)
    sel = sb("sel", [P, BIAS_ROWS, P], F16)
    bias_hi = sb("bias_hi", [P, E], F16)
    bias = sb("bias", [P, E], F16)
    rw = sb("rw", [P, 2, KC, NE], F16)
    wscale = sb("wscale", [P, 1], F32)
    gscale = sb("gscale", [P, 1], F32)
    logit = sb("logit", [P, ST, NE], F32)
    rest = sb("rest", [P, ST, NE], F32)
    first = sb("first", [P, ST, NE], F32)
    second = sb("second", [P, ST, NE], F32)
    best = sb("best", [P, 6, ST], F32)
    tanh_d = sb("tanh_d", [P, ST], F32)
    gate = sb("gate", [P, PAIRS, ST, NE], F32)

    pE = mem.enter_context(nc.psum_tensor("m_pE", [P, RING, E], F32))
    pT = mem.enter_context(nc.psum_tensor("m_pT", [P, 2, KC, S], F16))
    pR = mem.enter_context(nc.psum_tensor("m_pR", [P, 512], F32))
    pO = mem.enter_context(nc.psum_tensor("m_pO", [P, E], F32))
    logits_ps = pR[:, 0:ST * NE].rearrange("p (s e) -> p s e", s=ST)

    consts_ok, bias_ok, sel_in = sem("consts_ok"), sem("bias_ok"), sem("sel_in")
    rw_ok, ramp_ok, wscale_ok = sem("rw_ok"), sem("ramp_ok"), sem("wscale_ok")
    small_in, small_hi, small_32, small_lo = sem("small_in"), sem("small_hi"), sem("small_32"), sem("small_lo")
    routed, tanh_ok, gate_chain = sem("routed"), sem("tanh_ok"), sem("gate_chain")
    expert_done, gelu_done, acc_done = sem("expert_done"), sem("gelu_done"), sem("acc_done")
    out_done, x_ok = sem("out_done"), sem("x_ok")
    GATE_STEPS, GATE_DIFF = 18, 9
    PRIME_X, PRIME_COLS, PRIME_SMALL = 1, 1, 1

    with nc.Block() as block:

        @block.sync
        def _(sp):
            sp.dma_start(sel[:, :, :], t["sel_d"]).then_inc(sel_in, 16)
            with sp.Fori(0, TRIPS) as it:
                sp.wait_ge(small_lo, it + PRIME_SMALL)
                sp.dma_start(stage[:, 0], t["small_d"][:, it]).then_inc(small_in, 16)

        @block.gpsimd
        def _(pool):
            pool.sem_inc(small_lo, PRIME_SMALL)
            pool.memset(wscale[:, :], W_SCALE).then_inc(wscale_ok, 1)
            pool.wait_ge(wscale_ok, 1)
            with pool.Fori(0, TRIPS) as it:
                norm.deviation(pool, it * PAIRS + 1)
                raw = stage[:, 0].rearrange("p k n -> p (k n)")
                hi = w_small[:, it, 0].rearrange("p k n -> p (k n)")
                lo = w_small[:, it, 1].rearrange("p k n -> p (k n)")
                wide = wscale[:, :].to_broadcast([P, KC * E])
                pool.wait_ge(small_in, it * 16 + 16)
                pool.wait_ge(wscale_ok, 1)
                pool.tensor_tensor(hi, raw, wide, ALU.mult).then_inc(small_hi, 1)
                pool.wait_ge(small_hi, it + 1)
                pool.tensor_tensor(raw, raw, wide, ALU.mult).then_inc(small_32, 1)
                pool.wait_ge(small_32, it + 1)
                pool.wait_ge(wscale_ok, 1)
                pool.tensor_tensor(lo, raw, hi, ALU.subtract).then_inc(small_lo, 1)
                norm.deviation(pool, it * PAIRS + 2)

        @block.scalar
        def _(act):
            def gelu(e, st, n):
                u = n * UNITS + e * ST + st
                slot = (e * ST + st) % RING
                act.wait_ge(expert_done, u + 1)
                act.wait_ge(acc_done, u + 1)
                act.activation(y[:, slot], pE[:, slot], ACT.Gelu_apprx_tanh,
                               scale=1.0 / (X_SCALE * W_SCALE)).then_inc(gelu_done, 1)

            def half_difference(n):
                act.wait_ge(gate_chain, n * GATE_STEPS + GATE_DIFF)
                act.activation(tanh_d[:, :], best[:, 4], ACT.Tanh, scale=0.5).then_inc(tanh_ok, 1)

            def hid_high(n):
                act.wait_ge(norm.xn_ok, norm.made(n))
                hid.high(act, norm.xn[:, :, :])

            def com_high(par, n):
                act.wait_ge(acc_done, (n + 1) * UNITS + RING)
                com.high(act, acc[:, par])

            def trip(it, first=False):
                for par in range(PAIRS):
                    b = it * PAIRS + par
                    for e in range(NE):
                        for st in range(ST):
                            gelu(e, st, b)
                        if not (first and par == 0):
                            if e == 0:
                                com_high(1 - par, b - 1)
                            if e == 1:
                                for half in range(2):
                                    com.out(act, half, pT[:, half], 0, b - 1)
                        if e == 2:
                            hid_high(b + 1)
                        if e == 3:
                            for half in range(2):
                                hid.out(act, half, pT[:, half], 1 - par, b + 1)
                        if e == 6:
                            half_difference(b + 1)

            act.sem_inc(gelu_done, RING)
            act.sem_inc(com.cols_ok, PRIME_COLS)
            act.wait_ge(bias_ok, 1)
            act.activation(bias_hi[:, :], bias_raw[:, :], ACT.Copy, scale=W_SCALE).then_inc(consts_ok, 1)
            act.activation(rw[:, 0], rw_raw[:, :, :], ACT.Copy, scale=W_SCALE).then_inc(consts_ok, 1)
            hid_high(0)
            for half in range(2):
                hid.out(act, half, pT[:, half], 0, 0)
            half_difference(0)
            trip(0, first=True)
            with act.Fori(1, TRIPS) as it:
                trip(it)
            com_high(1, B - 1)
            for half in range(2):
                com.out(act, half, pT[:, half], 0, B - 1)

        @block.vector
        def _(dve):
            def spread(ap):
                return ap.unsqueeze(2).to_broadcast([P, ST, NE])

            def link(n, k):
                dve.wait_ge(gate_chain, n * GATE_STEPS + k)

            ramp3 = ramp[:, :].unsqueeze(1).to_broadcast([P, ST, NE])

            def first_best(src, out, m, w, n, k):
                link(n, k)
                dve.tensor_reduce(best[:, m], src, AX.X, ALU.max).then_inc(gate_chain, 1)
                link(n, k + 1)
                dve.tensor_tensor(out, src, spread(best[:, m]), ALU.is_equal).then_inc(gate_chain, 1)
                link(n, k + 2)
                dve.tensor_tensor(out, out, ramp3, ALU.mult).then_inc(gate_chain, 1)
                link(n, k + 3)
                dve.tensor_reduce(best[:, w], out, AX.X, ALU.max).then_inc(gate_chain, 1)
                link(n, k + 4)
                dve.tensor_tensor(out, out, spread(best[:, w]), ALU.is_equal).then_inc(gate_chain, 1)

            def gates_a(n):
                dve.wait_ge(routed, n + 1)
                dve.tensor_scalar(logit[:, :, :], logits_ps, 1.0 / (X_SCALE * W_SCALE), None,
                                  ALU.mult).then_inc(gate_chain, 1)
                first_best(logit[:, :, :], first[:, :, :], 0, 1, n, 1)
                link(n, 6)
                dve.scalar_tensor_tensor(rest[:, :, :], first[:, :, :], -1e30, logit[:, :, :],
                                         ALU.mult, ALU.add).then_inc(gate_chain, 1)
                link(n, 7)
                dve.tensor_reduce(best[:, 2], rest[:, :, :], AX.X, ALU.max).then_inc(gate_chain, 1)
                link(n, 8)
                dve.tensor_tensor(best[:, 4], best[:, 0], best[:, 2], ALU.subtract).then_inc(gate_chain, 1)

            def gates_b(par, n):
                link(n, 9)
                dve.tensor_tensor(second[:, :, :], rest[:, :, :], spread(best[:, 2]),
                                  ALU.is_equal).then_inc(gate_chain, 1)
                link(n, 10)
                dve.tensor_tensor(second[:, :, :], second[:, :, :], ramp3, ALU.mult).then_inc(gate_chain, 1)
                link(n, 11)
                dve.tensor_reduce(best[:, 3], second[:, :, :], AX.X, ALU.max).then_inc(gate_chain, 1)
                link(n, 12)
                dve.tensor_tensor(second[:, :, :], second[:, :, :], spread(best[:, 3]),
                                  ALU.is_equal).then_inc(gate_chain, 1)
                dve.wait_ge(tanh_ok, n + 1)
                dve.tensor_scalar(best[:, 0], tanh_d[:, :], C_SCALE / 2, C_SCALE / 2,
                                  ALU.mult, ALU.add).then_inc(gate_chain, 1)
                dve.tensor_scalar(best[:, 5], tanh_d[:, :], -C_SCALE / 2, C_SCALE / 2,
                                  ALU.mult, ALU.add).then_inc(gate_chain, 1)
                link(n, 15)
                dve.tensor_tensor(first[:, :, :], first[:, :, :], spread(best[:, 0]),
                                  ALU.mult).then_inc(gate_chain, 1)
                dve.tensor_tensor(second[:, :, :], second[:, :, :], spread(best[:, 5]),
                                  ALU.mult).then_inc(gate_chain, 1)
                link(n, 17)
                dve.tensor_tensor(gate[:, par], first[:, :, :], second[:, :, :], ALU.add).then_inc(gate_chain, 1)

            def accumulate(par, e, st, n):
                u = n * UNITS + e * ST + st
                slot = (e * ST + st) % RING
                if e >= 1:
                    dve.wait_ge(acc_done, u - 1 + RING)
                dve.wait_ge(gelu_done, u + 1 + RING)
                scalar = gate[:, par, st, e:e + 1]
                if e == 0:
                    dve.tensor_scalar(acc[:, par, st], y[:, slot], scalar, None, ALU.mult).then_inc(acc_done, 1)
                else:
                    dve.scalar_tensor_tensor(acc[:, par, st], y[:, slot], scalar, acc[:, par, st],
                                             ALU.mult, ALU.add).then_inc(acc_done, 1)

            def update(tile, st, n):
                dve.wait_ge(out_done, n * ST + st + 1)
                dve.wait_ge(rw_ok, 1)
                xt = x[:, tile + st, :]
                dve.scalar_tensor_tensor(xt, pO[:, :], gscale[:, :], xt, ALU.mult, ALU.add).then_inc(x_ok, 1)

            def trip(it, first=False):
                for par in range(PAIRS):
                    b = it * PAIRS + par
                    ahead = ((b + 1) * ST) % TILES
                    before = not (first and par == 0)
                    dve.wait_ge(gate_chain, (b + 1) * GATE_STEPS)
                    for e in range(NE):
                        for st in range(ST):
                            accumulate(par, e, st, b)
                        if e == 0:
                            if before:
                                com.low(dve, acc[:, 1 - par], b - 1)
                            norm.statistics(dve, ahead, b + 1)
                        if e == 1:
                            norm.normalise(dve, ahead, b + 1)
                        if e == 2:
                            hid.low(dve, norm.xn[:, :, :], b + 1)
                        if before and e in (3, 5):
                            update((b - 1) * ST, (e - 3) // 2, b - 1)
                        if e == 5:
                            gates_a(b + 1)
                        if e == 6:
                            gates_b(1 - par, b + 1)

            dve.sem_inc(acc_done, RING)
            dve.sem_inc(x_ok, PRIME_X)
            dve.memset(bias[:, :], 0.0).then_inc(ramp_ok, 1)
            dve.tensor_scalar(gscale[:, :], t["tanh_g"][:, 2:3], 1.0 / (C_SCALE * W_SCALE), None, ALU.mult)
            dve.wait_ge(consts_in, 8 * 16)
            dve.tensor_copy(ramp[:, :], ramp[:, :]).then_inc(bias_ok, 1)
            dve.wait_ge(ramp_ok, 1)
            dve.wait_ge(consts_ok, 2)
            dve.tensor_copy(bias[0:BIAS_ROWS, :], bias_hi[0:BIAS_ROWS, :])
            low = slice(BIAS_LOW, BIAS_LOW + BIAS_ROWS)
            dve.scalar_tensor_tensor(bias[low, :], bias_raw[low, :], W_SCALE, bias_hi[low, :],
                                     ALU.mult, ALU.subtract)
            dve.scalar_tensor_tensor(rw[:, 1], rw_raw[:, :, :], W_SCALE, rw[:, 0],
                                     ALU.mult, ALU.subtract).then_inc(rw_ok, 1)
            hid.low(dve, norm.xn[:, :, :], 0)
            gates_a(0)
            gates_b(0, 0)
            trip(0, first=True)
            with dve.Fori(1, TRIPS) as it:
                trip(it)
            com.low(dve, acc[:, 1], B - 1)
            for st in range(ST):
                update((B - 1) * ST, st, B - 1)

        @block.tensor
        def _(pe):
            def route(par, n):
                pe.wait_ge(gate_chain, (n - 1) * GATE_STEPS + 1)
                route_now(par)

            def route_now(par):
                for st in range(ST):
                    project(pe, logits_ps[:, st], hid.cols, par, st, rw, more=True)
                    ins = pe.matmul(logits_ps[:, st], sel[:, BIAS_ROUTER, :], bias[:, 0:NE], start=False, stop=True)
                ins.then_inc(routed, 1)

            def expert(par, e, st, n):
                u = n * UNITS + e * ST + st
                slot = (e * ST + st) % RING
                pe.wait_ge(gelu_done, u + 1)
                project(pe, pE[:, slot], hid.cols, par, st, w_e[:, e], more=True)
                pe.matmul(pE[:, slot], sel[:, e, :], bias[:, :], start=False, stop=True).then_inc(expert_done, 1)

            def combine(st, n):
                pe.wait_ge(com.cols_ok, 2 * n + 2 + PRIME_COLS)
                pe.wait_ge(x_ok, n * ST + st + PRIME_X)
                project(pe, pO[:, :], com.cols, 0, st, w_small[:, 0], more=True)
                pe.matmul(pO[:, :], sel[:, BIAS_OUT, :], bias[:, :], start=False, stop=True).then_inc(out_done, 1)

            def trip(it, first=False):
                for par in range(PAIRS):
                    b = it * PAIRS + par
                    before = not (first and par == 0)
                    pe.wait_ge(hid.cols_ok, 2 * b + 2)
                    for e in range(NE):
                        for st in range(ST):
                            expert(par, e, st, b)
                        if before and e == 1:
                            pe.wait_ge(com.lo_ok, b)
                            for half in range(2):
                                com.turn(pe, half, pT[:, half], ident)
                        if before and e in (2, 4):
                            pe.wait_ge(small_lo, 1 + PRIME_SMALL)
                            combine((e - 2) // 2, b - 1)
                        if e == 3:
                            pe.wait_ge(hid.lo_ok, b + 2)
                            if before:
                                pe.wait_ge(com.cols_ok, 2 * b + PRIME_COLS)
                            for half in range(2):
                                hid.turn(pe, half, pT[:, half], ident)
                        if e == 4:
                            pe.wait_ge(hid.cols_ok, 2 * b + 4)
                            route(1 - par, b + 1)

            pe.wait_ge(hid.lo_ok, 1)
            for half in range(2):
                hid.turn(pe, half, pT[:, half], ident)
            pe.wait_ge(rw_ok, 1)
            pe.wait_ge(sel_in, 16)
            pe.wait_ge(hid.cols_ok, 2)
            route_now(0)
            trip(0, first=True)
            with pe.Fori(1, TRIPS) as it:
                trip(it)
            pe.wait_ge(com.lo_ok, B)
            for half in range(2):
                com.turn(pe, half, pT[:, half], ident)
            for st in range(ST):
                combine(st, B - 1)


H1, D1 = 16, 32
G1 = 4
R1 = 128
V1 = D1 + 1
Q1_SCALE, K1_SCALE, V1_SCALE = 64.0, 1024.0, 1024.0
LIFT1 = 627.0
MASK = 32768.0


def phase_attention1(nc, mem, t):
    x, ident, w_small = t["x"], t["ident"], t["w_small"]
    GPB = H1 // G1
    NG = PAIRS * GPB
    TRIPS = B // PAIRS
    W = S + P

    def sb(name, shape, dt):
        return mem.enter_context(nc.sbuf_tensor("a1_" + name, shape, dt))

    def sem(name):
        return mem.enter_context(nc.semaphore("a1_" + name))

    arena = t["w_e"][:, :, :, :, :].rearrange("p e a k n -> p (e a k n)")
    used = [0]

    def carve(n):
        used[0] += n
        return arena[:, used[0] - n:used[0]]

    qst = carve(PAIRS * ST * H1 * R1).rearrange("p (a s h r) -> p a s h r", a=PAIRS, s=ST, h=H1)
    kst = carve(ST * H1 * R1).rearrange("p (s h r) -> p s h r", s=ST, h=H1)
    kT = carve(PAIRS * H1 * S).rearrange("p (a h t) -> p a h t", a=PAIRS, h=H1)
    p_hi = carve(2 * G1 * W).rearrange("p (a h w) -> p a h w", a=2, h=G1)
    p_lo = carve(2 * G1 * W).rearrange("p (a h w) -> p a h w", a=2, h=G1)
    vst = carve(PAIRS * ST * H1 * 2 * V1).rearrange("p (a s h v d) -> p a s h v d", a=PAIRS, s=ST, h=H1, v=2)

    norm = t["norm"]
    norm.base = 2 * B
    hid = Split(nc, mem, "a1_hid", 1)
    com = Split(nc, mem, "a1_com", 1)
    ctx = sb("ctx", [P, PAIRS, ST, L], F32)
    cx = sb("cx", [P, 2, ST, L], F16)
    cxT = sb("cxT", [P, 2, S], F16)
    qT1 = sb("qT1", [P, 2, G1, S], F16)
    qT2 = sb("qT2", [P, 2, G1, S], F16)
    p32 = sb("p32", [P, G1, W], F32)
    negm = sb("negm", [P, 2, ST, G1], F32)
    oall = sb("oall", [P, ST, H1, V1], F32)
    o32 = sb("o32", [P, ST, H1, D1], F32)
    rec = sb("rec", [P, ST, H1], F32)
    gscale = sb("gscale", [P, 1], F32)
    big_ident = sb("big_ident", [P, P], F16)
    mask_row = sb("mask_row", [P, P], F16)
    mask_key = sb("mask_key", [P, P], F16)

    pS2 = mem.enter_context(nc.psum_tensor("a1_pS2", [P, 2, 512], F32))
    pS1 = mem.enter_context(nc.psum_tensor("a1_pS1", [P, G1, S], F32))
    pT = mem.enter_context(nc.psum_tensor("a1_pT", [P, 2, G1, S], F16))
    pO = mem.enter_context(nc.psum_tensor("a1_pO", [P, 512], F32))
    pP = mem.enter_context(nc.psum_tensor("a1_pP", [P, E], F32))
    o_ps = pO[:, 0:G1 * V1].rearrange("p (h d) -> p h d", h=G1)
    first_banks = [pP[:, :], pS2[:, 0], pS2[:, 1], pO[:, :]]
    first_banks += [pS1[:, 2 * k:2 * k + 2].rearrange("p h s -> p (h s)") for k in range(2)]
    pT_cx = pT[:, 0].rearrange("p g t -> p (g t)")[:, 0:2 * S].rearrange("p (a t) -> p a t", a=2)

    ctx_in = [sem(f"ctx{par}_in") for par in range(PAIRS)]
    masks_in, zeroed, const_set, k_const = sem("masks_in"), sem("zeroed"), sem("const_set"), sem("k_const")
    cxhi_ok, cxlo_ok, cx_turned, cx_ok = sem("cxhi_ok"), sem("cxlo_ok"), sem("cx_turned"), sem("cx_ok")
    projected, pphi_ok, pp_ok = sem("projected"), sem("pphi_ok"), sem("pp_ok")
    k_turned, kT_ok = sem("k_turned"), sem("kT_ok")
    t1_done, t2_done, qT1_ok, qT2_ok = sem("t1_done"), sem("t2_done"), sem("qT1_ok"), sem("qT2_ok")
    dup_ok = sem("dup_ok")
    s1_done, max_ok, mhi_ok, m_ok = sem("s1_done"), sem("max_ok"), sem("mhi_ok"), sem("m_ok")
    s2_done, exp_done = sem("s2_done"), sem("exp_done")
    plo_ok = [sem("plo_dve"), sem("plo_pool")]
    pv_done, o_ok = sem("pv_done"), sem("o_ok")
    rec_ok, o32_ok = sem("rec_ok"), sem("o32_ok")
    PRIME_EXP, PRIME_PV, PRIME_O = 2, 4, 1
    LOWS = 1, 3

    STEP_USES = (("k", 0), ("k", 1)), (("v", 0), ("q", 0)), (("v", 1), ("q", 1)), (("out", 0), ("out", 1))
    PREP = 6

    def use(g, k):
        return PREP + 2 * g + k

    def high_count(b, j, k):
        return PREP * (b + 1) + 2 * j + k

    with nc.Block() as block:

        @block.sync
        def _(sp):
            def load_ctx(b, par):
                sp.dma_start(ctx[:, par], t["ctx_d"][:, b]).then_inc(ctx_in[par], 16)

            load_ctx(0, 0)
            load_ctx(1, 1)
            sp.dma_start(big_ident[:, :], t["big_ident_d"]).then_inc(masks_in, 16)
            sp.dma_start(mask_row[:, :], t["mask_row_d"]).then_inc(masks_in, 16)
            sp.dma_start(mask_key[:, :], t["mask_key_d"]).then_inc(masks_in, 16)
            for n in range(2):
                sp.dma_start(t["stage"][:, n], ff_source(t, n)).then_inc(t["ff_stage_in"][n], 16)
            with sp.Fori(0, TRIPS) as it:
                for par in range(PAIRS):
                    sp.wait_ge(cxlo_ok, it * PAIRS + par + 1)
                    load_ctx((it * PAIRS + PAIRS + par) % B, par)
            for par in range(PAIRS):
                sp.wait_ge(ctx_in[par], 16 * (TRIPS + 1))
                sp.wait_ge(t["ff_stage_in"][par], 16)

        @block.gpsimd
        def _(pool):
            def p_low(slot, h, n):
                pool.wait_ge(exp_done, G1 * n + h + 1 + PRIME_EXP)
                pool.tensor_tensor(p_lo[:, slot, h], p32[:, h], p_hi[:, slot, h],
                                   ALU.subtract).then_inc(plo_ok[1], 1)

            pool.sem_inc(plo_ok[1], LOWS[1])
            norm.deviation(pool, 1)
            pool.memset(qst[:, :, :, :, 3 * D1:], 0.0)
            pool.memset(vst[:, 0, :, :, 1, D1:], 0.0)
            pool.memset(vst[:, 1], 0.0)
            pool.memset(p_hi[:, 1], 1.0)
            pool.memset(p_lo[:, 1], 0.0)
            pool.memset(oall[:, :, :, :], 0.0).then_inc(zeroed, 1)
            pool.wait_ge(zeroed, 1)
            pool.memset(qst[:, :, :, :, 3 * D1 + 2:3 * D1 + 3], LIFT1)
            pool.memset(oall[:, :, :, D1:D1 + 1], 1.0)
            pool.memset(vst[:, :, :, :, 0, D1:D1 + 1], 1.0).then_inc(const_set, 1)
            with pool.Fori(0, TRIPS) as it:
                for i in range(NG):
                    par, j = divmod(i, GPB)
                    g, b = it * NG + i, it * PAIRS + par
                    if j == 2:
                        norm.deviation(pool, b + 2)
                    for h in range(1, G1):
                        p_low(i % 2, h, g)

        @block.scalar
        def _(act):
            def exps(slot, h, n):
                u = G1 * n + h
                act.wait_ge(s2_done, u + 1)
                if h == 0:
                    act.wait_ge(pv_done, 2 * n + PRIME_PV)
                scale = D1 ** -0.5 / (Q1_SCALE * K1_SCALE)
                act.activation(p_hi[:, slot, h], pS2[:, h % 2, 0:W], ACT.Exp, scale=scale)
                if h == 0:
                    act.wait_ge(plo_ok[0], LOWS[0] * n + 1)
                else:
                    act.wait_ge(plo_ok[1], LOWS[1] * n + h)
                act.activation(p32[:, h], pS2[:, h % 2, 0:W], ACT.Exp, scale=scale).then_inc(exp_done, 1)

            def ctx_high(par, loads):
                act.wait_ge(ctx_in[par], 16 * loads)
                act.activation(cx[:, 0], ctx[:, par], ACT.Copy, scale=W_SCALE).then_inc(cxhi_ok, 1)

            def hid_high(n):
                act.wait_ge(norm.xn_ok, norm.made(n))
                hid.high(act, norm.xn[:, :, :])

            def hid_out(half, n):
                hid.out(act, half, pT[:, 1 - half], 0, n)

            def ctx_out(n):
                act.wait_ge(cx_turned, n + 1)
                act.activation(cxT[:, :, :], pT_cx, ACT.Copy).then_inc(cx_ok, 1)

            def com_out(half, n):
                com.out(act, half, pT[:, 1 - half], 0, n)

            def high(kind, par, st, uses, bank=pP[:, :]):
                heads = bank.rearrange("p (h d) -> p h d", h=H1)
                act.wait_ge(projected, uses + 1)
                if kind == "q":
                    ins = act.activation(qst[:, par, st, :, 0:D1], heads, ACT.Copy,
                                         scale=Q1_SCALE / (X_SCALE * W_SCALE))
                elif kind == "k":
                    ins = act.activation(kst[:, st, :, 0:D1], heads, ACT.Copy,
                                         scale=K1_SCALE / (W_SCALE * W_SCALE))
                else:
                    ins = act.activation(vst[:, par, st, :, 0, 0:D1], heads, ACT.Copy,
                                         scale=V1_SCALE / (W_SCALE * W_SCALE))
                ins.then_inc(pphi_ok, 1)

            def keys_out(par, k, n):
                act.wait_ge(k_turned, 4 * n + k + 1)
                act.activation(kT[:, par, G1 * k:G1 * k + G1, :], pT[:, 1 - k % 2],
                               ACT.Copy).then_inc(kT_ok, 1)

            def com_high(n):
                act.wait_ge(o32_ok, n + 1)
                com.high(act, o32[:, :, :, :].rearrange("p s h d -> p s (h d)"))

            act.sem_inc(exp_done, PRIME_EXP)
            ctx_high(0, 1)
            hid_high(0)
            for half in range(2):
                hid_out(half, 0)
            ctx_out(0)
            act.wait_ge(k_const, 1)
            act.wait_ge(const_set, 1)
            for n, (kind, st) in enumerate(PREPARE):
                high(kind, 0, st, n, first_banks[n])
            for k in range(4):
                keys_out(0, k, 0)
            ctx_high(1, 1)
            hid_high(1)
            ctx_out(1)
            with act.Fori(0, TRIPS) as it:
                for i in range(NG):
                    par, j = divmod(i, GPB)
                    g, b = it * NG + i, it * PAIRS + par
                    exps(i % 2, 0, g)
                    if j == 0:
                        hid_out(0, b + 1)
                    if j == 1 or j == 3:
                        keys_out(1 - par, j - 1, b + 1)
                    if j == 2:
                        com_out(0, b)
                    if j < 3:
                        kind, st = STEP_USES[j][0]
                        high(kind, 1 - par, st, use(g, 0))
                    exps(i % 2, 1, g)
                    if j == 0:
                        hid_out(1, b + 1)
                    if j == 1 or j == 3:
                        keys_out(1 - par, j, b + 1)
                    if j == 2:
                        com_out(1, b)
                    exps(i % 2, 2, g)
                    if j == 1:
                        com_high(b)
                    if j == 3:
                        hid_high(b + 2)
                    if j < 3:
                        kind, st = STEP_USES[j][1]
                        high(kind, 1 - par, st, use(g, 1))
                    exps(i % 2, 3, g)
                    if j == 0:
                        ctx_high(par, it + 2)
                    if j == 3:
                        ctx_out(b + 2)
            com_high(B)
            for half in range(2):
                com_out(half, B)

        @block.vector
        def _(dve):
            def ctx_low(par, n):
                dve.wait_ge(cxhi_ok, n + 1)
                dve.scalar_tensor_tensor(cx[:, 1], ctx[:, par], W_SCALE, cx[:, 0],
                                         ALU.mult, ALU.subtract).then_inc(cxlo_ok, 1)

            def low(kind, par, st, uses, highs, bank=pP[:, :]):
                heads = bank.rearrange("p (h d) -> p h d", h=H1)
                dve.wait_ge(pphi_ok, highs + 1)
                if kind == "q":
                    dst, hi = qst[:, par, st, :, D1:2 * D1], qst[:, par, st, :, 0:D1]
                    scale = Q1_SCALE / (X_SCALE * W_SCALE)
                elif kind == "k":
                    dst, hi = kst[:, st, :, 2 * D1:3 * D1], kst[:, st, :, 0:D1]
                    scale = K1_SCALE / (W_SCALE * W_SCALE)
                else:
                    dst, hi = vst[:, par, st, :, 1, 0:D1], vst[:, par, st, :, 0, 0:D1]
                    scale = V1_SCALE / (W_SCALE * W_SCALE)
                dve.scalar_tensor_tensor(dst, heads, scale, hi, ALU.mult, ALU.subtract).then_inc(pp_ok, 1)
                if kind == "q":
                    dve.tensor_copy(qst[:, par, st, :, 2 * D1:3 * D1], hi).then_inc(dup_ok, 1)
                elif kind == "k":
                    dve.tensor_copy(kst[:, st, :, D1:2 * D1], hi).then_inc(dup_ok, 1)

            def p_low(slot, h, n):
                dve.wait_ge(exp_done, G1 * n + h + 1 + PRIME_EXP)
                dve.tensor_tensor(p_lo[:, slot, h], p32[:, h], p_hi[:, slot, h],
                                  ALU.subtract).then_inc(plo_ok[0], 1)

            def q1_out(slot, n):
                dve.wait_ge(t1_done, n + 1)
                dve.tensor_copy(qT1[:, slot], pT[:, 0]).then_inc(qT1_ok, 1)

            def q2_out(slot, n):
                dve.wait_ge(t2_done, n + 1)
                dve.tensor_copy(qT2[:, slot], pT[:, 1]).then_inc(qT2_ok, 1)

            def row_max(st, slot, n):
                for r in range(2):
                    heads = slice(2 * r, 2 * r + 2)
                    dve.wait_ge(s1_done, 4 * n + 2 * st + r + 1)
                    dve.tensor_reduce(negm[:, slot, st, heads], pS1[:, heads, 0:(st + 1) * P], AX.X, ALU.max,
                                      negate=True).then_inc(max_ok, 1)

            def put_max(par, g, slot, n):
                dve.wait_ge(max_ok, 4 * n + 4)
                heads = qst[:, par, :, G1 * g:G1 * g + G1, :]
                dve.tensor_scalar(heads[:, :, :, 3 * D1], negm[:, slot], 1.0 / M_SCALE, None,
                                  ALU.mult).then_inc(mhi_ok, 1)
                dve.wait_ge(mhi_ok, n + 1)
                dve.scalar_tensor_tensor(heads[:, :, :, 3 * D1 + 1], negm[:, slot], 1.0 / M_SCALE,
                                         heads[:, :, :, 3 * D1], ALU.mult, ALU.subtract).then_inc(m_ok, 1)

            def o_out(st, g, n, batch):
                if g == 0 and st == 0:
                    dve.wait_ge(o32_ok, batch + 1)
                dve.wait_ge(pv_done, 2 * n + st + 1 + PRIME_PV)
                dve.tensor_copy(oall[:, st, G1 * g:G1 * g + G1, :], o_ps).then_inc(o_ok, 1)

            def row_sums(n):
                dve.wait_ge(o_ok, (n * GPB + 1) * ST + PRIME_O)
                dve.reciprocal(rec[:, :, :], oall[:, :, :, D1]).then_inc(rec_ok, 1)

            def divide(n):
                dve.wait_ge(rec_ok, n + 1)
                dve.tensor_tensor(o32[:, :, :, :], oall[:, :, :, 0:D1],
                                  rec[:, :, :].unsqueeze(3).to_broadcast([P, ST, H1, D1]),
                                  ALU.mult).then_inc(o32_ok, 1)

            def com_low(n):
                dve.wait_ge(o32_ok, n + 1)
                com.low(dve, o32[:, :, :, :].rearrange("p s h d -> p s (h d)"), n)

            def update(tile, st, uses):
                dve.wait_ge(projected, uses + 1)
                dve.wait_ge(k_const, 1)
                xt = x[:, tile + st, :]
                dve.scalar_tensor_tensor(xt, pP[:, :], gscale[:, :], xt, ALU.mult, ALU.add).then_inc(pp_ok, 1)

            dve.sem_inc(plo_ok[0], LOWS[0])
            dve.sem_inc(o_ok, PRIME_O)
            dve.tensor_scalar(gscale[:, :], t["tanh_g"][:, 1:2], 1.0 / (V1_SCALE * W_SCALE), None, ALU.mult)
            dve.memset(kst[:, :, :, 3 * D1:], 0.0).then_inc(t["kzero"], 1)
            dve.wait_ge(t["kzero"], 2)
            dve.memset(kst[:, :, :, 3 * D1:3 * D1 + 3], M_SCALE).then_inc(k_const, 1)
            ctx_low(0, 0)
            norm.statistics(dve, ST, 1)
            hid.low(dve, norm.xn[:, :, :], 0)
            for n, (kind, st) in enumerate(PREPARE):
                low(kind, 0, st, n, n, first_banks[n])
            ctx_low(1, 1)
            norm.normalise(dve, ST, 1)
            hid.low(dve, norm.xn[:, :, :], 1)
            q1_out(0, 0)
            row_max(0, 0, 0)
            row_max(1, 0, 0)
            put_max(0, 0, 0, 0)
            q2_out(0, 0)
            dve.wait_ge(const_set, 1)
            with dve.Fori(0, TRIPS) as it:
                for i in range(NG):
                    par, j = divmod(i, GPB)
                    g, b = it * NG + i, it * PAIRS + par
                    p1, g1, s1 = (i + 1) // GPB % 2, (i + 1) % GPB, (i + 1) % 2
                    q1_out(s1, g + 1)
                    for k in range(2):
                        kind, st = STEP_USES[j][k]
                        if k == 1:
                            p_low(i % 2, 0, g)
                            row_max(0, s1, g + 1)
                            o_out(0, (i - 1) % GPB, g, b)
                            row_max(1, s1, g + 1)
                            put_max(p1, g1, s1, g + 1)
                        if kind == "out":
                            update(((b - 1) * ST + TILES) % TILES, st, use(g, k))
                        else:
                            low(kind, 1 - par, st, use(g, k), high_count(b, j, k))
                    q2_out(s1, g + 1)
                    o_out(1, (i - 1) % GPB, g, b)
                    if j == 0:
                        row_sums(b)
                        divide(b)
                        ctx_low(par, b + 2)
                    if j == 1:
                        com_low(b)
                        norm.statistics(dve, ((b + 2) * ST) % TILES, b + 2)
                    if j == 2:
                        norm.normalise(dve, ((b + 2) * ST) % TILES, b + 2)
                    if j == 3:
                        hid.low(dve, norm.xn[:, :, :], b + 2)
            for st in range(ST):
                o_out(st, GPB - 1, B * GPB, B)
            row_sums(B)
            divide(B)
            com_low(B)
            for st in range(ST):
                update((B - 1) * ST, st, use(B * GPB, st))

        @block.tensor
        def _(pe):
            def turn_context():
                for half in range(2):
                    for c in range(ST):
                        ins = pe.transpose(pT_cx[:, half, c * P:(c + 1) * P], cx[:, half, c, :], ident[:, :])
                ins.then_inc(cx_turned, 1)

            def prepare(kind, st, bank=pP[:, :]):
                if kind == "q":
                    ins = project(pe, bank, hid.cols, 0, st, w_small[:, 1])
                else:
                    part = 0 if kind == "k" else 1
                    for k, (a, w) in enumerate(PRODUCTS):
                        ins = pe.matmul(bank, cxT[:, a, st * P:(st + 1) * P], w_small[:, 3, w, part, :],
                                        start=(k == 0), stop=(k == 2))
                ins.then_inc(projected, 1)

            def turn_keys(k):
                for h in range(G1):
                    for c in range(ST):
                        ins = pe.transpose(pT[:, 1 - k % 2, h, c * P:(c + 1) * P], kst[:, c, G1 * k + h, :], ident[:, :])
                ins.then_inc(k_turned, 1)

            def q_turn(bank, par, g, done):
                for h in range(G1):
                    for st in range(ST):
                        ins = pe.transpose(pT[:, bank, h, st * P:(st + 1) * P], qst[:, par, st, G1 * g + h, :],
                                           ident[:, :])
                ins.then_inc(done, 1)

            def scores_by_row(slot, par, g, st, n):
                for h in range(G1):
                    if h % 2 == 0 and not (isinstance(n, int) and n == 0 and st == 0):
                        pe.wait_ge(max_ok, 4 * n + 2 * st + h // 2 - 1)
                    pe.matmul(pS1[:, h, 0:(st + 1) * P], qT1[0:3 * D1, slot, h, st * P:(st + 1) * P],
                              kT[0:3 * D1, par, G1 * g + h, 0:(st + 1) * P], start=True, stop=False)
                    ins = pe.matmul(pS1[:, h, st * P:(st + 1) * P], big_ident[:, :], mask_row[:, :],
                                    start=False, stop=True)
                    if h % 2 == 1:
                        ins.then_inc(s1_done, 1)

            def scores_by_key(slot, par, g, h, n):
                pe.wait_ge(exp_done, G1 * n + h - 1 + PRIME_EXP)
                key = kT[:, par, G1 * g + h, :]
                pe.matmul(pS2[:, h % 2, 0:S], key[:, 0:P], qT2[:, slot, h, :], start=True, stop=False)
                pe.matmul(pS2[:, h % 2, 0:P], big_ident[:, :], mask_key[:, :], start=False, stop=True)
                pe.matmul(pS2[:, h % 2, S:W], key[:, P:S], qT2[:, slot, h, P:S], start=True, stop=False)
                pe.matmul(pS2[:, h % 2, S:W], big_ident[:, :], mask_key[:, :], start=False,
                          stop=True).then_inc(s2_done, 1)

            def weigh(slot, par, g, st, n):
                if st == 0:
                    for k in range(2):
                        pe.wait_ge(plo_ok[k], LOWS[k] * (n + 1))
                pe.wait_ge(o_ok, 2 * n + st + PRIME_O)
                for h in range(G1):
                    for c, at in ((0, 0),) if st == 0 else ((0, P), (1, S)):
                        for a, v in PRODUCTS:
                            probs = (p_hi, p_lo)[a]
                            ins = pe.matmul(o_ps[:, h, :], probs[:, slot, h, at:at + P],
                                            vst[:, par, c, G1 * g + h, v, :], start=(c == 0 and a + v == 0),
                                            stop=(c == st and v == 1))
                ins.then_inc(pv_done, 1)

            def turn_hid(half, n):
                pe.wait_ge(hid.lo_ok, n + 1)
                hid.turn(pe, half, pT[:, 1 - half], ident)

            def turn_com(half, n):
                pe.wait_ge(com.lo_ok, n + 1)
                com.turn(pe, half, pT[:, 1 - half], ident)

            def output(st, n, uses):
                pe.wait_ge(com.cols_ok, 2 * n + 2)
                pe.wait_ge(pp_ok, uses)
                project(pe, pP[:, :], com.cols, 0, st, w_small[:, 2]).then_inc(projected, 1)

            pe.sem_inc(pv_done, PRIME_PV)
            for half in range(2):
                turn_hid(half, 0)
            pe.wait_ge(cxlo_ok, 1)
            pe.wait_ge(hid.cols_ok, 2)
            turn_context()
            pe.wait_ge(cx_ok, 1)
            for n, (kind, st) in enumerate(PREPARE):
                prepare(kind, st, first_banks[n])
            pe.wait_ge(pp_ok, PREP)
            pe.wait_ge(dup_ok, 4)
            for k in range(4):
                if k >= 2:
                    pe.wait_ge(kT_ok, k - 1)
                turn_keys(k)
            pe.wait_ge(kT_ok, 4)
            pe.wait_ge(cxlo_ok, 2)
            turn_context()
            pe.wait_ge(cx_ok, 2)
            q_turn(0, 0, 0, t1_done)
            pe.wait_ge(qT1_ok, 1)
            pe.wait_ge(masks_in, 48)
            scores_by_row(0, 0, 0, 0, 0)
            scores_by_row(0, 0, 0, 1, 0)
            pe.wait_ge(m_ok, 1)
            q_turn(1, 0, 0, t2_done)
            pe.wait_ge(const_set, 1)
            with pe.Fori(0, TRIPS) as it:
                for i in range(NG):
                    par, j = divmod(i, GPB)
                    g, b = it * NG + i, it * PAIRS + par
                    p1, g1, s1 = (i + 1) // GPB % 2, (i + 1) % GPB, (i + 1) % 2

                    def use_bank(k):
                        kind, st = STEP_USES[j][k]
                        if kind == "out":
                            output(st, b, use(g, k))
                        else:
                            pe.wait_ge(pp_ok, use(g, k))
                            prepare(kind, st)

                    def weigh_before(st):
                        weigh((i - 1) % 2, (i - 1) // GPB % 2, (i - 1) % GPB, st, g)

                    def fill(half):
                        if j == 0:
                            turn_hid(half, b + 1)
                        if j == 1:
                            if half == 0:
                                pe.wait_ge(dup_ok, 4 * (b + 1) + 2)
                            turn_keys(half)
                        if j == 2:
                            turn_com(half, b)
                        if j == 3:
                            turn_keys(2 + half)

                    def fill_is_out(j, b, half):
                        if j == 0:
                            pe.wait_ge(hid.cols_ok, 2 * (b + 1) + half + 1)
                        if j == 1:
                            pe.wait_ge(kT_ok, 4 * (b + 1) + half + 1)
                        if j == 2:
                            pe.wait_ge(com.cols_ok, 2 * b + half + 1)
                        if j == 3:
                            pe.wait_ge(kT_ok, 4 * (b + 1) + half + 3)
                            if half == 1:
                                pe.wait_ge(cx_ok, b + 3)

                    pe.wait_ge(qT2_ok, g + 1)
                    scores_by_key(i % 2, par, j, 0, g)
                    fill(0)
                    if j == 3:
                        pe.wait_ge(dup_ok, 4 * (b + 2))
                    fill_is_out((j - 1) % GPB, b if j else b - 1, 1)
                    q_turn(0, p1, g1, t1_done)
                    use_bank(0)
                    scores_by_key(i % 2, par, j, 1, g)
                    pe.wait_ge(qT1_ok, g + 2)
                    scores_by_row(s1, p1, g1, 0, g + 1)
                    fill(1)
                    weigh_before(0)
                    scores_by_key(i % 2, par, j, 2, g)
                    scores_by_row(s1, p1, g1, 1, g + 1)
                    use_bank(1)
                    fill_is_out(j, b, 0)
                    if j == 3:
                        pe.wait_ge(kT_ok, 4 * (b + 1) + 4)
                        pe.wait_ge(cxlo_ok, b + 3)
                        turn_context()
                    scores_by_key(i % 2, par, j, 3, g)
                    pe.wait_ge(m_ok, g + 2)
                    q_turn(1, p1, g1, t2_done)
                    weigh_before(1)
            for st in range(ST):
                weigh(1, 1, GPB - 1, st, B * GPB)
            pe.wait_ge(qT2_ok, B * GPB + 1)
            pe.wait_ge(qT1_ok, B * GPB + 1)
            for half in range(2):
                turn_com(half, B)
            for st in range(ST):
                output(st, B, use(B * GPB, st))


PREPARE = (("k", 0), ("v", 0), ("k", 1), ("v", 1), ("q", 0), ("q", 1))


FF = 2048
FM = FF // E
FC = FF // P
H_SCALE = 256.0


FF_ORDER = [m for k in range(FM) for m in (k, FM + k)] + [2 * FM + k for k in range(FM)]


def ff_source(t, n):
    m = FF_ORDER[n]
    return t["gu_d"][:, m] if m < 2 * FM else t["down_d"][:, m - 2 * FM]


def phase_feed_forward(nc, mem, t, out_d):
    x, stage, ident, w_gu, w_d = t["x"], t["stage"], t["ident"], t["w_e"], t["w_d"]
    TRIPS = B // PAIRS
    UNITS = FC // 2
    MATS = 3 * FM

    def sb(name, shape, dt):
        return mem.enter_context(nc.sbuf_tensor("f_" + name, shape, dt))

    def sem(name):
        return mem.enter_context(nc.semaphore("f_" + name))

    norm = t["norm"]
    norm.base = 3 * B + 1
    hid = Split(nc, mem, "f_hid", PAIRS)
    sg = sb("sg", [P, 2, 2, S], F32)
    h32 = sb("h32", [P, 2, 2, S], F32)
    hp = t["w_small"][:, 0:2].rearrange("p m a k n -> p (m a k n)").rearrange("p (a c s) -> p a c s", a=2, c=FC)
    gscale = sb("gscale", [P, 1], F32)

    pG = mem.enter_context(nc.psum_tensor("f_pG", [P, 2, 2, S], F32))
    pU = mem.enter_context(nc.psum_tensor("f_pU", [P, 2, 2, S], F32))
    pD = mem.enter_context(nc.psum_tensor("f_pD", [P, ST, E], F32))
    pT = mem.enter_context(nc.psum_tensor("f_pT", [P, 2, KC, S], F16))

    stage_in = t["ff_stage_in"]
    whi_ok, wlo_ok, gs_ok = sem("whi_ok"), sem("wlo_ok"), sem("gs_ok")
    gu_done, silu_done, h_ok, hhi_ok, hlo_ok = sem("gu_done"), sem("silu_done"), sem("h_ok"), sem("hhi_ok"), sem("hlo_ok")
    down_done, x_ok, sent = sem("down_done"), sem("x_ok"), sem("sent")
    PRIME = 2

    def pair_of(n):
        m = FF_ORDER[n]
        return w_gu[:, m] if m < 2 * FM else w_d[:, m - 2 * FM]

    SPLITS = ((2,), (3, 4), (5,), (6, 7), (8,), (9, 10), (11,), ())

    with nc.Block() as block:

        @block.sync
        def _(sp):
            for n in range(2, MATS):
                sp.wait_ge(wlo_ok, n - 1)
                sp.dma_start(stage[:, n % 2], ff_source(t, n)).then_inc(stage_in[n % 2], 16)
            with sp.Fori(0, B) as b:
                sp.wait_ge(x_ok, b * ST + ST + PRIME)
                tiles = bass.ds(((b + 1) * ST) % TILES, ST)
                sp.dma_start(out_d[:, tiles, :], x[:, tiles, :]).then_inc(sent, 16)
            sp.wait_ge(sent, 16 * B)

        @block.gpsimd
        def _(pool):
            def h_low(slot, u, n):
                pool.wait_ge(hhi_ok, n * UNITS + u + 1)
                pool.tensor_tensor(hp[:, 1, 2 * u:2 * u + 2, :], h32[:, slot], hp[:, 0, 2 * u:2 * u + 2, :],
                                   ALU.subtract).then_inc(hlo_ok, 1)

            pool.sem_inc(hlo_ok, PRIME)
            with pool.Fori(0, TRIPS) as it:
                for par in range(PAIRS):
                    b = it * PAIRS + par
                    for u in range(UNITS):
                        h_low(u % 2, u, b)
                        if u == 0:
                            norm.deviation(pool, b + 1)

        @block.scalar
        def _(act):
            def silu(slot, u, n):
                k = n * UNITS + u
                act.wait_ge(gu_done, k + 1)
                act.wait_ge(h_ok, k - 1 + PRIME)
                act.activation(sg[:, slot], pG[:, slot], ACT.Silu,
                               scale=1.0 / (X_SCALE * W_SCALE)).then_inc(silu_done, 1)

            def h_high(slot, u, n):
                act.wait_ge(h_ok, n * UNITS + u + 1 + PRIME)
                if u == 0:
                    act.wait_ge(down_done, n * ST + PRIME)
                act.activation(hp[:, 0, 2 * u:2 * u + 2, :], h32[:, slot], ACT.Copy).then_inc(hhi_ok, 1)

            def hid_high(n):
                act.wait_ge(norm.xn_ok, norm.made(n))
                hid.high(act, norm.xn[:, :, :])

            def split_high(n):
                act.wait_ge(stage_in[n % 2], 16 * (n // 2 + 1))
                act.activation(pair_of(n)[:, 0], stage[:, n % 2], ACT.Copy, scale=W_SCALE).then_inc(whi_ok, 1)

            def trip(it):
                for par in range(PAIRS):
                    b = it * PAIRS + par
                    for u in range(UNITS):
                        silu(u % 2, u, b)
                        h_high(u % 2, u, b)
                        if isinstance(b, int) and b == 0:
                            for n in SPLITS[u]:
                                split_high(n)
                        if u == 1:
                            hid_high(b + 1)
                        if u == 4:
                            for half in range(2):
                                hid.out(act, half, pT[:, half], 1 - par, b + 1)

            act.sem_inc(silu_done, PRIME)
            split_high(0)
            hid_high(0)
            split_high(1)
            for half in range(2):
                hid.out(act, half, pT[:, half], 0, 0)
            trip(0)
            with act.Fori(1, TRIPS) as it:
                trip(it)

        @block.vector
        def _(dve):
            def gated(slot, u, n):
                k = n * UNITS + u
                dve.wait_ge(silu_done, k + 1 + PRIME)
                dve.wait_ge(hlo_ok, k - 1 + PRIME)
                dve.scalar_tensor_tensor(h32[:, slot], pU[:, slot], H_SCALE / (X_SCALE * W_SCALE), sg[:, slot],
                                         ALU.mult, ALU.mult).then_inc(h_ok, 1)

            def update(tile, st, n):
                dve.wait_ge(down_done, n * ST + st + 1 + PRIME)
                dve.wait_ge(gs_ok, 1)
                xt = x[:, tile + st, :]
                dve.scalar_tensor_tensor(xt, pD[:, st], gscale[:, :], xt, ALU.mult, ALU.add).then_inc(x_ok, 1)

            def split_low(n):
                dve.wait_ge(whi_ok, n + 1)
                dve.scalar_tensor_tensor(pair_of(n)[:, 1], stage[:, n % 2], W_SCALE, pair_of(n)[:, 0],
                                         ALU.mult, ALU.subtract).then_inc(wlo_ok, 1)

            def trip(it):
                for par in range(PAIRS):
                    b = it * PAIRS + par
                    tile, ahead = ((b + 1) * ST) % TILES, ((b + 2) * ST) % TILES
                    for u in range(UNITS):
                        gated(u % 2, u, b)
                        if isinstance(b, int) and b == 0:
                            for n in SPLITS[u]:
                                split_low(n)
                        if u == 0:
                            norm.statistics(dve, ahead, b + 1)
                            norm.normalise(dve, ahead, b + 1)
                        if u == 2:
                            hid.low(dve, norm.xn[:, :, :], b + 1)
                    for st in range(ST):
                        update(tile, st, b)

            dve.sem_inc(h_ok, PRIME)
            dve.sem_inc(x_ok, PRIME)
            dve.tensor_scalar(gscale[:, :], t["tanh_g"][:, 3:4], 1.0 / (H_SCALE * W_SCALE), None,
                              ALU.mult).then_inc(gs_ok, 1)
            split_low(0)
            hid.low(dve, norm.xn[:, :, :], 0)
            split_low(1)
            trip(0)
            with dve.Fori(1, TRIPS) as it:
                trip(it)

        @block.tensor
        def _(pe):
            def gate_up(par, slot, u, n):
                k = n * UNITS + u
                pe.wait_ge(silu_done, k - 1 + PRIME)
                pe.wait_ge(h_ok, k - 1 + PRIME)
                for psum, part in ((pG, 0), (pU, FM)):
                    for c in range(2):
                        chunk = 2 * u + c
                        m, at = part + chunk // KC, chunk % KC * P
                        i = 0
                        for kc in range(KC):
                            for a, w in PRODUCTS:
                                ins = pe.matmul(psum[:, slot, c], w_gu[:, m, w, kc, at:at + P],
                                                hid.cols[:, par, a, kc, :], start=(i == 0),
                                                stop=(i == KC * len(PRODUCTS) - 1))
                                i += 1
                ins.then_inc(gu_done, 1)

            def down(st, n):
                pe.wait_ge(x_ok, n * ST + st - 1 + PRIME)
                i, last = 0, FC * len(PRODUCTS) - 1
                for chunk in range(FC):
                    if st == 0 and chunk % 2 == 0:
                        pe.wait_ge(hlo_ok, n * UNITS + chunk // 2 + 1 + PRIME)
                        pe.wait_ge(wlo_ok, 2 * FM + chunk // KC + 1)
                    for a, w in PRODUCTS:
                        ins = pe.matmul(pD[:, st], hp[:, a, chunk, st * P:(st + 1) * P],
                                        w_d[:, chunk // KC, w, chunk % KC, :], start=(i == 0), stop=(i == last))
                        i += 1
                ins.then_inc(down_done, 1)

            pe.sem_inc(down_done, PRIME)
            pe.wait_ge(hid.lo_ok, 1)
            for half in range(2):
                hid.turn(pe, half, pT[:, half], ident)
            with pe.Fori(0, TRIPS) as it:
                for par in range(PAIRS):
                    b = it * PAIRS + par
                    pe.wait_ge(hid.cols_ok, 2 * b + 2)
                    for u in range(UNITS):
                        pe.wait_ge(wlo_ok, 2 * (2 * u // KC) + 2)
                        gate_up(par, u % 2, u, b)
                        if u == 3:
                            pe.wait_ge(hid.lo_ok, b + 2)
                            for half in range(2):
                                hid.turn(pe, half, pT[:, half], ident)
                    for st in range(ST):
                        down(st, b)


def program(nc, a, out, debug_phase=None):
    with ExitStack() as mem:
        def sb(name, shape, dt):
            return mem.enter_context(nc.sbuf_tensor(name, shape, dt))

        def sem(name):
            return mem.enter_context(nc.semaphore(name))

        t = {}
        t["x"] = x = sb("x", [P, TILES, E], F32)
        t["w_e"] = sb("w_e", [P, NE, 2, KC, E], F16)
        t["stage"] = sb("stage", [P, 2, KC, E], F32)
        t["ident"] = sb("ident", [P, P], F16)
        t["g_raw"] = sb("g_raw", [P, 4], F32)
        t["norm_consts"] = sb("norm_consts", [P, len(NORM_CONSTS)], F32)
        t["tanh_g"] = sb("tanh_g", [P, 4], F32)
        t["norm"] = Norm(nc, mem, t)
        t["bias_raw"] = sb("bias_raw", [P, E], F32)
        t["rw_raw"] = sb("rw_raw", [P, KC, NE], F32)
        t["ramp"] = sb("ramp", [P, NE], F32)
        t["consts_in"] = sem("consts_in")
        for name in ("ident_in", "gates_in", "gates_ok", "kzero", "kconst"):
            t[name] = sem(name)
        t["ff_stage_in"] = [sem(f"ff_stage{k}_in") for k in range(2)]
        t["ctx_d"] = a["ctx_512"].rearrange("b (c p) l -> p b c l", p=P)
        t["x_d"] = a["x"].rearrange("b (s p) e -> p (b s) e", p=P)
        t["expert_d"] = a["L0_ffn_expert_w"].rearrange("e (k p) d -> p e k d", p=P)
        nc.scalar.dma_start(t["ident"][:, :], a["ident"]).then_inc(t["ident_in"], 16)
        nc.scalar.dma_start(t["g_raw"][:, 0:2], a["g_xattn"].partition_broadcast(P)).then_inc(t["gates_in"], 16)
        nc.scalar.dma_start(t["g_raw"][:, 2:4], a["g_ffn"].partition_broadcast(P)).then_inc(t["gates_in"], 16)
        t["sel_d"], t["router_d"] = a["sel"], a["L0_ffn_router_w"].rearrange("(k p) e -> p k e", p=P)
        t["ramp_d"] = a["ramp"]
        t["expert_b_d"] = a["L0_ffn_expert_b"]
        t["out_b_d"] = a["L0_ffn_out_b"].rearrange("(a n) -> a n", a=1)
        t["router_b_d"] = a["L0_ffn_router_b"].rearrange("(a n) -> a n", a=1)
        t["small_d"] = a["small"].rearrange("m (k p) n -> p m k n", p=P)
        for name in ("big_ident", "mask_row", "mask_key"):
            t[name + "_d"] = a[name]
        t["gu_d"] = a["gate_up"].rearrange("(k p) (m n) -> p m k n", p=P, n=E)
        t["down_d"] = a["down"].rearrange("(m k p) n -> p m k n", k=KC, p=P)
        out_sent = sem("out_sent")
        with ExitStack() as pm:
            phase_attention0(nc, pm, t)
        if debug_phase is None or debug_phase > 1:
            t["w_small"] = sb("w_small", [P, 4, 2, KC, E], F16)
            with ExitStack() as pm:
                phase_experts(nc, pm, t)
        if debug_phase is None or debug_phase > 2:
            with ExitStack() as pm:
                phase_attention1(nc, pm, t)
        if debug_phase is None or debug_phase > 3:
            t["w_d"] = sb("w_d", [P, FM, 2, KC, E], F16)
            with ExitStack() as pm:
                phase_feed_forward(nc, pm, t, out.rearrange("b (s p) e -> p (b s) e", p=P))
            return
        if debug_phase:
            with nc.Block() as block:
                @block.sync
                def _(sp):
                    sp.dma_start(out.rearrange("b (s p) e -> p (b s) e", p=P), x[:, :, :]).then_inc(out_sent, 16)
                    sp.wait_ge(out_sent, 16)
            return


def kernel(_debug=None, **inputs):
    import numpy as np
    import concourse.bacc as bacc
    from concourse.bass_utils import run_bass_kernel_spmd

    nc = bacc.Bacc("TRN2", target_bir_lowering=False, num_devices=1)
    arrays = {k: np.ascontiguousarray(v) for k, v in inputs.items()}
    arrays["ident"] = np.eye(P, dtype=np.float16)
    arrays["ramp"] = np.arange(NE, 0, -1, dtype=np.float32)
    sel = np.zeros((P, BIAS_ROWS, P), np.float16)
    for r in range(BIAS_ROWS):
        sel[[r, BIAS_LOW + r], r, :] = C_SCALE if r == BIAS_OUT else X_SCALE
    arrays["sel"] = sel
    small = np.zeros((4, E, E), np.float32)
    small[0] = arrays.pop("L0_ffn_out_w")
    small[1] = arrays.pop("L1_xattn_Wq").T
    small[2] = arrays.pop("L1_xattn_Wout").T
    small[3].reshape(KC, P, E)[0:2] = arrays.pop("L1_xattn_Wkv_expand").T.reshape(P, 2, E).transpose(1, 0, 2)
    arrays["small"] = small
    arrays["gate_up"] = np.ascontiguousarray(arrays.pop("L1_ffn_w_gate_up").T)
    arrays["down"] = np.ascontiguousarray(arrays.pop("L1_ffn_w_down").T)
    arrays["big_ident"] = (MASK * np.eye(P)).astype(np.float16)
    later = np.triu(np.ones((P, P)), 1)
    arrays["mask_row"] = (-MASK * later).astype(np.float16)
    arrays["mask_key"] = (-MASK * later.T).astype(np.float16)
    aps = {k: nc.dram_tensor("in_" + k, v.shape, mybir.dt.from_np(v.dtype), kind="ExternalInput").ap()
           for k, v in arrays.items()}
    out = nc.dram_tensor("out", (B, S, E), F32, kind="ExternalOutput").ap()
    program(nc, aps, out, _debug)
    r = run_bass_kernel_spmd(nc, [{"in_" + k: v for k, v in arrays.items()}], core_ids=[0])
    return r.results[0]["out"]
```
